# Optimizing a Trainium2 kernel written in Bass

```python
import numpy as np
import jax
import jax.numpy as jnp

def _softmax(x, axis=-1):
    return jax.nn.softmax(x, axis=axis)

def _gelu(x):
    return jax.nn.gelu(x, approximate=True)

def _silu(x):
    return jax.nn.silu(x)

def _sigmoid(x):
    return jax.nn.sigmoid(x)

def _layernorm(x, axis=-1, eps=1e-05):
    m = jnp.mean(x, axis=axis, keepdims=True)
    v = jnp.var(x, axis=axis, keepdims=True)
    return (x - m) / jnp.sqrt(v + eps)

def _scatter_add(tgt, idx, src, axis=0):
    return tgt.at[idx].add(src)

def _segment_sum(src, seg, n):
    return jax.ops.segment_sum(src, seg, n)
kernel_name = 'mk_early_fusion_d1_tok_img1024_r4_414790'

def setup_inputs(seed: int=0):
    np.random.seed(seed)
    _w = jnp.asarray

    def _rec_inputs():
        import jax
        import jax.numpy as jnp
        _rk = jax.random.key(seed)
        x = -0.000125008 + 0.999885 * jax.random.normal(jax.random.fold_in(_rk, 1), (16, 512, 256, 4), jnp.float32)
        txt = -8.03667e-05 + 0.656214 * jax.random.normal(jax.random.fold_in(_rk, 2), (16, 32, 256), jnp.float32)
        return (x, txt)
    x, txt = _rec_inputs()

    def _L0_tok_setup():
        import jax, jax.numpy as jnp
        import numpy as np
        key = jax.random.key(seed)
        k1, k2, k3 = jax.random.split(key, 3)
        B, H, I, O, Dp1 = (4, 512, 256, 256, 4)
        x = jax.random.normal(k1, (B, H, I, Dp1), dtype=jnp.float32)
        weight = 0.1 * jax.random.normal(k2, (O, Dp1), dtype=jnp.float32)
        weighted_sum = 0.1 * jax.random.normal(k3, (O, I), dtype=jnp.float32)
        return {'x': x, 'weight': weight, 'weighted_sum': weighted_sum}
    _L0_tok_all = _L0_tok_setup()
    _L0_tok_in = {k: v for k, v in _L0_tok_all.items() if k in ('weight', 'weighted_sum')}
    del _L0_tok_all

    def _L0_attn_setup():
        import jax, jax.numpy as jnp
        import numpy as np
        from jax.scipy.linalg import solve_triangular
        B, L, HID, H = (2, 512, 256, 4)
        DK, DV = (HID // H, HID // H)
        CHUNK = 32
        CONV_K, FIR_SK, FIR_LK, FIR_WK = (4, 3, 31, 64)
        GIN = HID + 15 * H
        GH = 2 * HID
        FLOOR_INIT = float(np.log(0.05 / 0.95))

        def _l2norm(x):
            return x / jnp.sqrt(jnp.sum(x * x, -1, keepdims=True) + 1e-06)

        def _dwconv_causal(x_blc, w_ck):
            K = w_ck.shape[-1]
            x = jnp.moveaxis(x_blc, 1, 2)
            x = jnp.pad(x, ((0, 0), (0, 0), (K - 1, 0)))
            y = jax.lax.conv_general_dilated(x, w_ck[:, None, :], (1,), 'VALID', feature_group_count=w_ck.shape[0], dimension_numbers=('NCH', 'OIH', 'NCH'))
            return jnp.moveaxis(y, 2, 1)

        def _delta_rule(q, k, v, beta):
            b, h, Ll, dk = q.shape
            dv = v.shape[-1]
            n = Ll // CHUNK
            q = _l2norm(q)
            k = _l2norm(k)
            v = v * beta[..., None]
            kb = k * beta[..., None]
            rs = lambda t: t.reshape(b, h, n, CHUNK, t.shape[-1])
            q, k, v, kb = (rs(q), rs(k), rs(v), rs(kb))
            tril_strict = jnp.tril(jnp.ones((CHUNK, CHUNK), bool), -1)
            tril = jnp.tril(jnp.ones((CHUNK, CHUNK), bool), 0)
            A = jnp.where(tril_strict, kb @ jnp.swapaxes(k, -1, -2), 0.0)
            eye = jnp.eye(CHUNK, dtype=q.dtype)
            inv = solve_triangular(eye + A, jnp.broadcast_to(eye, A.shape), lower=True)
            u = inv @ v
            w = inv @ kb
            qs, ks, us, ws = (jnp.moveaxis(t, 2, 0) for t in (q, k, u, w))
            S0 = jnp.zeros((b, h, dk, dv), q.dtype)

            def step(S, xs):
                q_i, k_i, u_i, w_i = xs
                attn = jnp.where(tril, q_i @ jnp.swapaxes(k_i, -1, -2), 0.0)
                u_adj = u_i - w_i @ S
                o_i = q_i @ S + attn @ u_adj
                S = S + jnp.swapaxes(k_i, -1, -2) @ u_adj
                return (S, o_i)
            S, o = jax.lax.scan(step, S0, (qs, ks, us, ws))
            o = jnp.moveaxis(o, 0, 2).reshape(b, h, Ll, dv)
            return (o, S)

        def _stats(x):
            mean = x.mean(-1)
            rms = jnp.sqrt(jnp.clip(jnp.mean(x * x, -1), 1e-08))
            mx = jnp.abs(x).max(-1)
            return jnp.concatenate([mean, rms, mx], -1)

        def _forward(hidden_states, q_w, k_w, v_w, b_w, convq_w, convk_w, convv_w, fir_s, fir_l, fir_wd, g1_w, g1_b, g2_w, g2_b, value_bias, log_temp, floor_logit, onorm_w, o_w):
            b, Ll, _ = hidden_states.shape
            q = jax.nn.silu(_dwconv_causal(hidden_states @ q_w.T, convq_w))
            k = jax.nn.silu(_dwconv_causal(hidden_states @ k_w.T, convk_w))
            v = jax.nn.silu(_dwconv_causal(hidden_states @ v_w.T, convv_w))
            tohd = lambda t: t.reshape(b, Ll, H, -1)
            q, k, v = (tohd(q), tohd(k), tohd(v))
            beta = jax.nn.sigmoid(hidden_states @ b_w.T)
            tr = lambda t: jnp.moveaxis(t, 1, 2)
            delta_out, _S = _delta_rule(tr(q), tr(k), tr(v), jnp.moveaxis(beta, 1, 2))
            delta_out = jnp.moveaxis(delta_out, 1, 2)

            def fir(x, filt):
                y = _dwconv_causal(x.reshape(b, Ll, H * DV), filt.reshape(H * DV, -1))
                return y.reshape(b, Ll, H, DV)
            short, long_, wide = (fir(v, fir_s), fir(v, fir_l), fir(v, fir_wd))
            gate_in = jnp.concatenate([hidden_states, _stats(short), _stats(long_), _stats(wide), _stats(delta_out), _stats(v)], -1)
            hdn = jax.nn.gelu(gate_in @ g1_w.T + g1_b, approximate=False)
            logits = (hdn @ g2_w.T + g2_b).reshape(b, Ll, H, 5)
            logits = logits.at[..., 4].add(value_bias)
            logits = logits / jnp.exp(log_temp)[None, None, :, None]
            p = jax.nn.softmax(logits, -1)
            f = jax.nn.sigmoid(floor_logit)[None, None, :, None]
            scale = 1.0 - 4.0 * f
            w_ctx = f + scale * p[..., :4]
            w_val = scale * p[..., 4:5]
            o = w_ctx[..., 0:1] * short + w_ctx[..., 1:2] * long_ + w_ctx[..., 2:3] * wide + w_ctx[..., 3:4] * delta_out + w_val * v
            o = o * jax.lax.rsqrt(jnp.mean(o * o, -1, keepdims=True) + 1e-05) * onorm_w
            return o.reshape(b, Ll, HID) @ o_w.T
        key = jax.random.key(seed)
        ks = jax.random.split(key, 16)
        rn = lambda i, shp, s: jax.random.normal(ks[i], shp, jnp.float32) * s
        fir_init = lambda i, K: jnp.zeros((H, DV, K), jnp.float32).at[..., -1].set(1.0) + rn(i, (H, DV, K), 0.02)
        g2_b = jnp.zeros((5 * H,), jnp.float32).at[4::5].set(4.0)
        return {'hidden_states': jax.random.normal(ks[0], (B, L, HID), jnp.float32), 'q_w': rn(1, (HID, HID), 0.02), 'k_w': rn(2, (HID, HID), 0.02), 'v_w': rn(3, (HID, HID), 0.02), 'b_w': rn(4, (H, HID), 0.02), 'convq_w': rn(5, (HID, CONV_K), 0.2), 'convk_w': rn(6, (HID, CONV_K), 0.2), 'convv_w': rn(7, (HID, CONV_K), 0.2), 'fir_s': fir_init(8, FIR_SK), 'fir_l': fir_init(9, FIR_LK), 'fir_wd': fir_init(10, FIR_WK), 'g1_w': rn(11, (GH, GIN), 0.02), 'g1_b': jnp.zeros((GH,), jnp.float32), 'g2_w': rn(12, (5 * H, GH), 0.02), 'g2_b': g2_b, 'value_bias': jnp.full((H,), 4.0, jnp.float32), 'log_temp': jnp.zeros((H,), jnp.float32), 'floor_logit': jnp.full((H,), FLOOR_INIT, jnp.float32), 'onorm_w': jnp.ones((DV,), jnp.float32), 'o_w': rn(13, (HID, HID), 0.02)}
    _L0_attn_all = _L0_attn_setup()
    _L0_attn_in = {k: v for k, v in _L0_attn_all.items() if k in ('q_w', 'k_w', 'v_w', 'b_w', 'convq_w', 'convk_w', 'convv_w', 'fir_s', 'fir_l', 'fir_wd', 'g1_w', 'g1_b', 'g2_w', 'g2_b', 'value_bias', 'log_temp', 'floor_logit', 'onorm_w', 'o_w')}
    del _L0_attn_all

    def _L0_ffn_setup():
        import jax, jax.numpy as jnp
        import numpy as np
        B, T, C = (2, 512, 256)
        H, D = (16, 64)
        CR = 8
        R = C // CR
        ROPE = D // 2
        NOPE = D - ROPE
        E, K, I, S = (8, 2, 128, 1)
        THETA = 100000.0
        EPS = 1e-05

        def _rmsnorm(x, w):
            rms = jnp.sqrt(jnp.mean(x * x, axis=-1, keepdims=True) + EPS)
            return w * (x / rms)

        def _rope(xh):
            d = xh.shape[-1]
            t = jnp.arange(xh.shape[2], dtype=jnp.float32)
            freqs = 1.0 / THETA ** (jnp.arange(0, d, 2, dtype=jnp.float32) / d)
            ang = jnp.outer(t, freqs)
            cos, sin = (jnp.cos(ang), jnp.sin(ang))
            xr = xh.reshape(xh.shape[:-1] + (d // 2, 2))
            x0, x1 = (xr[..., 0], xr[..., 1])
            rot = jnp.stack([x0 * cos - x1 * sin, x0 * sin + x1 * cos], axis=-1)
            return rot.reshape(xh.shape)

        def _attention(x, Wq, Wkva, Wkvb, Wo):
            b, t, _ = x.shape
            q = (x @ Wq).reshape(b, t, H, D).transpose(0, 2, 1, 3)
            ckv = x @ Wkva
            kv_latent, k_rope = (ckv[:, :, :R], ckv[:, :, R:])
            kv = (kv_latent @ Wkvb).reshape(b, t, H, NOPE).transpose(0, 2, 1, 3)
            k_rope = jnp.broadcast_to(k_rope[:, None, :, :], (b, H, t, ROPE))
            q_nope, q_rope = (q[..., :NOPE], q[..., NOPE:])
            q = jnp.concatenate([q_nope, _rope(q_rope)], axis=-1)
            k = jnp.concatenate([kv, _rope(k_rope)], axis=-1)
            v = jnp.concatenate([kv, jnp.zeros_like(k_rope)], axis=-1)
            att = jnp.einsum('bhqd,bhkd->bhqk', q, k) / jnp.sqrt(jnp.float32(D))
            mask = jnp.tril(jnp.ones((t, t), dtype=bool))
            att = jnp.where(mask, att, jnp.float32(-jnp.inf))
            att = jax.nn.softmax(att, axis=-1)
            y = jnp.einsum('bhqk,bhkd->bhqd', att, v)
            y = y.transpose(0, 2, 1, 3).reshape(b, t, H * D)
            return y @ Wo

        def _experts(x_flat, Wg, Wu, Wd):
            g = jax.nn.silu(jnp.einsum('nc,eci->nei', x_flat, Wg))
            u = jnp.einsum('nc,eci->nei', x_flat, Wu)
            return jnp.einsum('nei,eic->nec', g * u, Wd)

        def _moe(x, Wgate, expert_bias, Wg, Wu, Wd, sWg, sWu, sWd):
            b, t, c = x.shape
            xf = x.reshape(-1, c)
            shared = jnp.mean(_experts(xf, sWg, sWu, sWd), axis=1)
            logits = xf @ Wgate + expert_bias
            probs = jax.nn.softmax(logits, axis=-1)
            topk_p, topk_i = jax.lax.top_k(probs, K)
            topk_p = topk_p / jnp.sum(topk_p, axis=-1, keepdims=True)
            comb = jnp.sum(jax.nn.one_hot(topk_i, E, dtype=xf.dtype) * topk_p[..., None], axis=1)
            routed = jnp.einsum('ne,nec->nc', comb, _experts(xf, Wg, Wu, Wd))
            return (shared + routed).reshape(b, t, c)
        key = jax.random.key(seed)
        ks = jax.random.split(key, 16)
        w = lambda k, shp: jax.random.normal(k, shp, dtype=jnp.float32) * 0.02
        return {'x': jax.random.normal(ks[0], (B, T, C), dtype=jnp.float32), 'w_ln1': jnp.ones((C,), jnp.float32), 'Wq': w(ks[1], (C, H * D)), 'Wkva': w(ks[2], (C, R + ROPE)), 'Wkvb': w(ks[3], (R, H * NOPE)), 'Wo': w(ks[4], (H * D, C)), 'w_ln2': jnp.ones((C,), jnp.float32), 'Wgate': w(ks[5], (C, E)), 'expert_bias': jnp.zeros((E,), jnp.float32), 'Wg': w(ks[6], (E, C, I)), 'Wu': w(ks[7], (E, C, I)), 'Wd': w(ks[8], (E, I, C)), 'sWg': w(ks[9], (S, C, I)), 'sWu': w(ks[10], (S, C, I)), 'sWd': w(ks[11], (S, I, C))}
    _L0_ffn_all = _L0_ffn_setup()
    _L0_ffn_in = {k: v for k, v in _L0_ffn_all.items() if k in ('w_ln1', 'Wq', 'Wkva', 'Wkvb', 'Wo', 'w_ln2', 'Wgate', 'expert_bias', 'Wg', 'Wu', 'Wd', 'sWg', 'sWu', 'sWd')}
    del _L0_ffn_all
    return {'x': x, 'txt': txt, 'L0_tok_weight': _L0_tok_in['weight'], 'L0_tok_weighted_sum': _L0_tok_in['weighted_sum'], 'L0_attn_q_w': _L0_attn_in['q_w'], 'L0_attn_k_w': _L0_attn_in['k_w'], 'L0_attn_v_w': _L0_attn_in['v_w'], 'L0_attn_b_w': _L0_attn_in['b_w'], 'L0_attn_convq_w': _L0_attn_in['convq_w'], 'L0_attn_convk_w': _L0_attn_in['convk_w'], 'L0_attn_convv_w': _L0_attn_in['convv_w'], 'L0_attn_fir_s': _L0_attn_in['fir_s'], 'L0_attn_fir_l': _L0_attn_in['fir_l'], 'L0_attn_fir_wd': _L0_attn_in['fir_wd'], 'L0_attn_g1_w': _L0_attn_in['g1_w'], 'L0_attn_g1_b': _L0_attn_in['g1_b'], 'L0_attn_g2_w': _L0_attn_in['g2_w'], 'L0_attn_g2_b': _L0_attn_in['g2_b'], 'L0_attn_value_bias': _L0_attn_in['value_bias'], 'L0_attn_log_temp': _L0_attn_in['log_temp'], 'L0_attn_floor_logit': _L0_attn_in['floor_logit'], 'L0_attn_onorm_w': _L0_attn_in['onorm_w'], 'L0_attn_o_w': _L0_attn_in['o_w'], 'L0_ffn_w_ln1': _L0_ffn_in['w_ln1'], 'L0_ffn_Wq': _L0_ffn_in['Wq'], 'L0_ffn_Wkva': _L0_ffn_in['Wkva'], 'L0_ffn_Wkvb': _L0_ffn_in['Wkvb'], 'L0_ffn_Wo': _L0_ffn_in['Wo'], 'L0_ffn_w_ln2': _L0_ffn_in['w_ln2'], 'L0_ffn_Wgate': _L0_ffn_in['Wgate'], 'L0_ffn_expert_bias': _L0_ffn_in['expert_bias'], 'L0_ffn_Wg': _L0_ffn_in['Wg'], 'L0_ffn_Wu': _L0_ffn_in['Wu'], 'L0_ffn_Wd': _L0_ffn_in['Wd'], 'L0_ffn_sWg': _L0_ffn_in['sWg'], 'L0_ffn_sWu': _L0_ffn_in['sWu'], 'L0_ffn_sWd': _L0_ffn_in['sWd']}

def reference(x, txt, L0_tok_weight, L0_tok_weighted_sum, L0_attn_q_w, L0_attn_k_w, L0_attn_v_w, L0_attn_b_w, L0_attn_convq_w, L0_attn_convk_w, L0_attn_convv_w, L0_attn_fir_s, L0_attn_fir_l, L0_attn_fir_wd, L0_attn_g1_w, L0_attn_g1_b, L0_attn_g2_w, L0_attn_g2_b, L0_attn_value_bias, L0_attn_log_temp, L0_attn_floor_logit, L0_attn_onorm_w, L0_attn_o_w, L0_ffn_w_ln1, L0_ffn_Wq, L0_ffn_Wkva, L0_ffn_Wkvb, L0_ffn_Wo, L0_ffn_w_ln2, L0_ffn_Wgate, L0_ffn_expert_bias, L0_ffn_Wg, L0_ffn_Wu, L0_ffn_Wd, L0_ffn_sWg, L0_ffn_sWu, L0_ffn_sWd):
    import jax
    import jax.numpy as jnp

    def _L0_tok_ref(x, weight, weighted_sum):
        import jax, jax.numpy as jnp
        import numpy as np
        return jnp.einsum('bhid,oi,od->bho', x, weighted_sum, weight)

    def _L0_attn_ref(hidden_states, q_w, k_w, v_w, b_w, convq_w, convk_w, convv_w, fir_s, fir_l, fir_wd, g1_w, g1_b, g2_w, g2_b, value_bias, log_temp, floor_logit, onorm_w, o_w):
        import jax, jax.numpy as jnp
        import numpy as np
        from jax.scipy.linalg import solve_triangular
        B, L, HID, H = (2, 512, 256, 4)
        DK, DV = (HID // H, HID // H)
        CHUNK = 32
        CONV_K, FIR_SK, FIR_LK, FIR_WK = (4, 3, 31, 64)
        GIN = HID + 15 * H
        GH = 2 * HID
        FLOOR_INIT = float(np.log(0.05 / 0.95))

        def _l2norm(x):
            return x / jnp.sqrt(jnp.sum(x * x, -1, keepdims=True) + 1e-06)

        def _dwconv_causal(x_blc, w_ck):
            K = w_ck.shape[-1]
            x = jnp.moveaxis(x_blc, 1, 2)
            x = jnp.pad(x, ((0, 0), (0, 0), (K - 1, 0)))
            y = jax.lax.conv_general_dilated(x, w_ck[:, None, :], (1,), 'VALID', feature_group_count=w_ck.shape[0], dimension_numbers=('NCH', 'OIH', 'NCH'))
            return jnp.moveaxis(y, 2, 1)

        def _delta_rule(q, k, v, beta):
            b, h, Ll, dk = q.shape
            dv = v.shape[-1]
            n = Ll // CHUNK
            q = _l2norm(q)
            k = _l2norm(k)
            v = v * beta[..., None]
            kb = k * beta[..., None]
            rs = lambda t: t.reshape(b, h, n, CHUNK, t.shape[-1])
            q, k, v, kb = (rs(q), rs(k), rs(v), rs(kb))
            tril_strict = jnp.tril(jnp.ones((CHUNK, CHUNK), bool), -1)
            tril = jnp.tril(jnp.ones((CHUNK, CHUNK), bool), 0)
            A = jnp.where(tril_strict, kb @ jnp.swapaxes(k, -1, -2), 0.0)
            eye = jnp.eye(CHUNK, dtype=q.dtype)
            inv = solve_triangular(eye + A, jnp.broadcast_to(eye, A.shape), lower=True)
            u = inv @ v
            w = inv @ kb
            qs, ks, us, ws = (jnp.moveaxis(t, 2, 0) for t in (q, k, u, w))
            S0 = jnp.zeros((b, h, dk, dv), q.dtype)

            def step(S, xs):
                q_i, k_i, u_i, w_i = xs
                attn = jnp.where(tril, q_i @ jnp.swapaxes(k_i, -1, -2), 0.0)
                u_adj = u_i - w_i @ S
                o_i = q_i @ S + attn @ u_adj
                S = S + jnp.swapaxes(k_i, -1, -2) @ u_adj
                return (S, o_i)
            S, o = jax.lax.scan(step, S0, (qs, ks, us, ws))
            o = jnp.moveaxis(o, 0, 2).reshape(b, h, Ll, dv)
            return (o, S)

        def _stats(x):
            mean = x.mean(-1)
            rms = jnp.sqrt(jnp.clip(jnp.mean(x * x, -1), 1e-08))
            mx = jnp.abs(x).max(-1)
            return jnp.concatenate([mean, rms, mx], -1)

        def _forward(hidden_states, q_w, k_w, v_w, b_w, convq_w, convk_w, convv_w, fir_s, fir_l, fir_wd, g1_w, g1_b, g2_w, g2_b, value_bias, log_temp, floor_logit, onorm_w, o_w):
            b, Ll, _ = hidden_states.shape
            q = jax.nn.silu(_dwconv_causal(hidden_states @ q_w.T, convq_w))
            k = jax.nn.silu(_dwconv_causal(hidden_states @ k_w.T, convk_w))
            v = jax.nn.silu(_dwconv_causal(hidden_states @ v_w.T, convv_w))
            tohd = lambda t: t.reshape(b, Ll, H, -1)
            q, k, v = (tohd(q), tohd(k), tohd(v))
            beta = jax.nn.sigmoid(hidden_states @ b_w.T)
            tr = lambda t: jnp.moveaxis(t, 1, 2)
            delta_out, _S = _delta_rule(tr(q), tr(k), tr(v), jnp.moveaxis(beta, 1, 2))
            delta_out = jnp.moveaxis(delta_out, 1, 2)

            def fir(x, filt):
                y = _dwconv_causal(x.reshape(b, Ll, H * DV), filt.reshape(H * DV, -1))
                return y.reshape(b, Ll, H, DV)
            short, long_, wide = (fir(v, fir_s), fir(v, fir_l), fir(v, fir_wd))
            gate_in = jnp.concatenate([hidden_states, _stats(short), _stats(long_), _stats(wide), _stats(delta_out), _stats(v)], -1)
            hdn = jax.nn.gelu(gate_in @ g1_w.T + g1_b, approximate=False)
            logits = (hdn @ g2_w.T + g2_b).reshape(b, Ll, H, 5)
            logits = logits.at[..., 4].add(value_bias)
            logits = logits / jnp.exp(log_temp)[None, None, :, None]
            p = jax.nn.softmax(logits, -1)
            f = jax.nn.sigmoid(floor_logit)[None, None, :, None]
            scale = 1.0 - 4.0 * f
            w_ctx = f + scale * p[..., :4]
            w_val = scale * p[..., 4:5]
            o = w_ctx[..., 0:1] * short + w_ctx[..., 1:2] * long_ + w_ctx[..., 2:3] * wide + w_ctx[..., 3:4] * delta_out + w_val * v
            o = o * jax.lax.rsqrt(jnp.mean(o * o, -1, keepdims=True) + 1e-05) * onorm_w
            return o.reshape(b, Ll, HID) @ o_w.T
        return _forward(hidden_states, q_w, k_w, v_w, b_w, convq_w, convk_w, convv_w, fir_s, fir_l, fir_wd, g1_w, g1_b, g2_w, g2_b, value_bias, log_temp, floor_logit, onorm_w, o_w)

    def _L0_ffn_ref(x, w_ln1, Wq, Wkva, Wkvb, Wo, w_ln2, Wgate, expert_bias, Wg, Wu, Wd, sWg, sWu, sWd):
        import jax, jax.numpy as jnp
        import numpy as np
        B, T, C = (2, 512, 256)
        H, D = (16, 64)
        CR = 8
        R = C // CR
        ROPE = D // 2
        NOPE = D - ROPE
        E, K, I, S = (8, 2, 128, 1)
        THETA = 100000.0
        EPS = 1e-05

        def _rmsnorm(x, w):
            rms = jnp.sqrt(jnp.mean(x * x, axis=-1, keepdims=True) + EPS)
            return w * (x / rms)

        def _rope(xh):
            d = xh.shape[-1]
            t = jnp.arange(xh.shape[2], dtype=jnp.float32)
            freqs = 1.0 / THETA ** (jnp.arange(0, d, 2, dtype=jnp.float32) / d)
            ang = jnp.outer(t, freqs)
            cos, sin = (jnp.cos(ang), jnp.sin(ang))
            xr = xh.reshape(xh.shape[:-1] + (d // 2, 2))
            x0, x1 = (xr[..., 0], xr[..., 1])
            rot = jnp.stack([x0 * cos - x1 * sin, x0 * sin + x1 * cos], axis=-1)
            return rot.reshape(xh.shape)

        def _attention(x, Wq, Wkva, Wkvb, Wo):
            b, t, _ = x.shape
            q = (x @ Wq).reshape(b, t, H, D).transpose(0, 2, 1, 3)
            ckv = x @ Wkva
            kv_latent, k_rope = (ckv[:, :, :R], ckv[:, :, R:])
            kv = (kv_latent @ Wkvb).reshape(b, t, H, NOPE).transpose(0, 2, 1, 3)
            k_rope = jnp.broadcast_to(k_rope[:, None, :, :], (b, H, t, ROPE))
            q_nope, q_rope = (q[..., :NOPE], q[..., NOPE:])
            q = jnp.concatenate([q_nope, _rope(q_rope)], axis=-1)
            k = jnp.concatenate([kv, _rope(k_rope)], axis=-1)
            v = jnp.concatenate([kv, jnp.zeros_like(k_rope)], axis=-1)
            att = jnp.einsum('bhqd,bhkd->bhqk', q, k) / jnp.sqrt(jnp.float32(D))
            mask = jnp.tril(jnp.ones((t, t), dtype=bool))
            att = jnp.where(mask, att, jnp.float32(-jnp.inf))
            att = jax.nn.softmax(att, axis=-1)
            y = jnp.einsum('bhqk,bhkd->bhqd', att, v)
            y = y.transpose(0, 2, 1, 3).reshape(b, t, H * D)
            return y @ Wo

        def _experts(x_flat, Wg, Wu, Wd):
            g = jax.nn.silu(jnp.einsum('nc,eci->nei', x_flat, Wg))
            u = jnp.einsum('nc,eci->nei', x_flat, Wu)
            return jnp.einsum('nei,eic->nec', g * u, Wd)

        def _moe(x, Wgate, expert_bias, Wg, Wu, Wd, sWg, sWu, sWd):
            b, t, c = x.shape
            xf = x.reshape(-1, c)
            shared = jnp.mean(_experts(xf, sWg, sWu, sWd), axis=1)
            logits = xf @ Wgate + expert_bias
            probs = jax.nn.softmax(logits, axis=-1)
            topk_p, topk_i = jax.lax.top_k(probs, K)
            topk_p = topk_p / jnp.sum(topk_p, axis=-1, keepdims=True)
            comb = jnp.sum(jax.nn.one_hot(topk_i, E, dtype=xf.dtype) * topk_p[..., None], axis=1)
            routed = jnp.einsum('ne,nec->nc', comb, _experts(xf, Wg, Wu, Wd))
            return (shared + routed).reshape(b, t, c)
        x = x + _attention(_rmsnorm(x, w_ln1), Wq, Wkva, Wkvb, Wo)
        residual = x
        xn = _rmsnorm(x, w_ln2)
        x_out = _moe(xn, Wgate, expert_bias, Wg, Wu, Wd, sWg, sWu, sWd)
        return residual + x_out
    h = _L0_tok_ref(x, L0_tok_weight, L0_tok_weighted_sum)
    h = jnp.concatenate([h, txt], axis=1)
    h = h + _L0_attn_ref(_layernorm(h, axis=-1), L0_attn_q_w, L0_attn_k_w, L0_attn_v_w, L0_attn_b_w, L0_attn_convq_w, L0_attn_convk_w, L0_attn_convv_w, L0_attn_fir_s, L0_attn_fir_l, L0_attn_fir_wd, L0_attn_g1_w, L0_attn_g1_b, L0_attn_g2_w, L0_attn_g2_b, L0_attn_value_bias, L0_attn_log_temp, L0_attn_floor_logit, L0_attn_onorm_w, L0_attn_o_w)
    h = h + _L0_ffn_ref(_layernorm(h, axis=-1), L0_ffn_w_ln1, L0_ffn_Wq, L0_ffn_Wkva, L0_ffn_Wkvb, L0_ffn_Wo, L0_ffn_w_ln2, L0_ffn_Wgate, L0_ffn_expert_bias, L0_ffn_Wg, L0_ffn_Wu, L0_ffn_Wd, L0_ffn_sWg, L0_ffn_sWu, L0_ffn_sWd)
    return h

_drawn_inputs = setup_inputs


def setup_inputs(seed=0):
    import zlib

    import numpy as np

    out = dict(_drawn_inputs(seed))
    spreads = {'L0_attn_g1_b': (0.0, 0.8),
     'L0_attn_value_bias': (4.0, 0.6),
     'L0_attn_log_temp': (0.0, 0.8),
     'L0_attn_floor_logit': (-2.944438934326172, 0.6),
     'L0_attn_onorm_w': (1.0, 0.2),
     'L0_ffn_w_ln1': (1.0, 0.6),
     'L0_ffn_w_ln2': (1.0, 0.6),
     'L0_ffn_expert_bias': (0.0, 0.8)}
    factors = {'L0_attn_b_w': 8.0,
     'L0_attn_g1_w': 8.0,
     'L0_attn_g2_w': 8.0,
     'L0_ffn_Wq': 8.0,
     'L0_ffn_Wkva': 8.0,
     'L0_ffn_Wkvb': 8.0,
     'L0_ffn_Wo': 8.0,
     'L0_ffn_Wgate': 8.0,
     'L0_ffn_Wg': 8.0,
     'L0_ffn_Wu': 8.0,
     'L0_ffn_Wd': 8.0,
     'L0_ffn_sWg': 6.408,
     'L0_ffn_sWu': 6.265,
     'L0_ffn_sWd': 6.228}
    for name, (base, spread) in spreads.items():
        noise = np.random.default_rng([zlib.crc32(name.encode()), seed]).standard_normal(out[name].shape)
        drawn = base * np.exp(spread * noise) if base else spread * noise
        out[name] = jnp.asarray(drawn.astype(out[name].dtype))
    for name, factor in factors.items():
        out[name] = (out[name] * factor).astype(out[name].dtype)
    return out
```

```python
from contextlib import ExitStack

import numpy as np

import concourse.bass as bass
from concourse import mybir

F32 = mybir.dt.float32
ALU = mybir.AluOpType
ACT = mybir.ActivationFunctionType
AX = mybir.AxisListType

P = 128
B = 16
LI = 512
LT = 32
L = LI + LT
C = 256
KB = C // P
HALF = L // 2
D1 = 4
T = 5
NT = [128, 128, 128, 128, 32]
GH, GD = 4, 64
CH = 32
NCHUNK = L // CH
CONV = 4
FIRS = (3, 31, 64)
PAD = FIRS[2] - 1
NFIR = KB * sum(FIRS)
AH, AD, NOPE = 16, 64, 32
QB = AH // 2
E, EI = 8, 128
NE = E + 1
BIG = 3.0e38


ARENA = 26100
VSTEPS, ASTEPS = 178, 0


class Signal:

    def __init__(self, sem, per, start=0):
        self.sem, self.per, self.start = sem, per, start

    def __call__(self, i, k):
        return self.sem, i * self.per + k + self.start


CONSTS = dict(ident=P, mean=P, heads=P, swap=P, causal=P, strict=P, upper=P, cos=L, sin=L, pick=E * P, before=64,
              eps5=1, eps6=1)


def constants():
    out = {}
    r = np.arange(P)
    out["ident"] = np.eye(P)
    out["mean"] = np.full((P, P), 1.0 / C)
    out["heads"] = (r[:, None] // GD == r[None, :] // GD) * 1.0
    swap = np.zeros((P, P))
    for m in range(P):
        if m % AD >= NOPE:
            if m % 2 == 0:
                swap[m + 1, m] = -1.0
            else:
                swap[m - 1, m] = 1.0
    out["swap"] = swap
    out["causal"] = np.where(r[None, :] <= r[:, None], BIG, -BIG)
    same = r[:, None] // CH == r[None, :] // CH
    out["strict"] = np.where(same & (r[None, :] < r[:, None]), -1.0, 0.0)
    out["upper"] = np.where(same & (r[None, :] >= r[:, None]), 1.0, 0.0)
    width = AD - NOPE
    freqs = (1.0 / np.float32(100000.0) ** (np.arange(0, width, 2, dtype=np.float32) / np.float32(width))).astype(np.float32)
    ang = np.outer(np.arange(L, dtype=np.float32), freqs).astype(np.float32)
    cos, sin = np.ones((P, L)), np.zeros((P, L))
    for m in range(P):
        if m % AD >= NOPE:
            pair = (m % AD - NOPE) // 2
            cos[m], sin[m] = np.cos(ang[:, pair]), np.sin(ang[:, pair])
    out["cos"], out["sin"] = cos, sin
    pick = np.zeros((P, E, P))
    for e in range(E):
        pick[e, e] = 1.0
    out["pick"] = pick.reshape(P, E * P)
    e = np.arange(E)
    out["before"] = np.broadcast_to((e[None, :] < e[:, None]).reshape(1, 64), (P, 64)) * 1.0
    out["eps5"] = np.full((P, 1), 1e-5)
    out["eps6"] = np.full((P, 1), 1e-6)
    return np.ascontiguousarray(np.concatenate([out[k] for k in CONSTS], axis=1).astype(np.float32))


WEIGHTS = dict(wqkv=(P, KB * 3 * C), bw=(P, KB * GH), convw=(P, 6 * CONV), firw=(P, KB * sum(FIRS)),
               g1=(P, 3 * 512), g1b=(P, 4), g2=(P, 4 * 20), g2b=(P, 20), vbias=(P, GH), ltemp=(P, GH),
               floor=(P, GH), onorm=(P, GD), ow=(P, KB * C), ln1=(P, KB), ln2=(P, KB), wq=(P, KB * AH * AD),
               wkva=(P, KB * AD), wkvb=(32, AH * NOPE), kpad=(64, AH * AD), wo=(P, 4 * C), wgate=(P, KB * E),
               ebias=(P, E), wg=(P, NE * KB * EI), wu=(P, NE * KB * EI), wd=(P, NE * C))


def build(nc, x, txt, consts, tokw, tokws, weights, out, nseq=B):
    ctx = ExitStack()
    with ctx:
        def sb(name, words, parts=P):
            return ctx.enter_context(nc.sbuf_tensor(name, [parts, words], F32))

        def signal(name, per, start=0):
            return Signal(ctx.enter_context(nc.semaphore(name)), per, start)

        PS = ctx.enter_context(nc.psum_tensor("PS", [P, 8, 512], F32))
        K = {}
        cst = sb("cst", sum(CONSTS.values()))
        at = 0
        for name, n in CONSTS.items():
            K[name] = cst[:, at:at + n]
            at += n
        Wt = {name: sb("w_" + name, n, parts) for name, (parts, n) in WEIGHTS.items()}
        tokwT = sb("tokwT", 8 * C)[:, :].rearrange("p (k o) -> p k o", k=8)
        h = sb("h", KB * L)[:, :].rearrange("p (b l) -> p b l", b=KB)
        hn = sb("hn", KB * L)[:, :].rearrange("p (b l) -> p b l", b=KB)
        hcsq = sb("hcsq", 2 * KB * L)
        hc = hcsq[:, 0:KB * L].rearrange("p (b l) -> p b l", b=KB)
        sq = hcsq[:, KB * L:2 * KB * L].rearrange("p (b l) -> p b l", b=KB)
        yT = hcsq[:, :].rearrange("p (b l) -> p b l", b=4)
        sd = sb("sd", L)[:, :]
        gk = sb("gk", 3 * 20)
        gfloor = sb("gfloor", 20)

        arena = sb("arena", ARENA)
        used = [0]

        def take(words, again=None):
            start = used[0] if again is None else again
            if again is None:
                used[0] += words
            assert start + words <= ARENA, (start, words)
            return start

        def view(start, words, pattern=None, parts=P, **kw):
            v = arena[0:parts, start:start + words]
            return v.rearrange(pattern, **kw) if pattern else v

        aF = take(T * 5 * C)
        xs = view(aF, 4 * 1024, "p (t i d) -> p t i d", t=4, d=D1)
        xt = view(aF + 4096, C, parts=LT)
        F = view(aF, T * 5 * C, "p (t k c) -> p t k c", t=T, k=5)
        a0 = take(4096)
        xT = view(a0, 8 * LI, "p (k l) -> p k l", k=8)
        z = view(a0, 6 * (L + 3), "p (b l) -> p b l", b=6)
        fir = view(a0, 3 * KB * L, "p (f b l) -> p f b l", f=3, b=KB)
        acv = take(KB * L)
        cv = view(acv, KB * L, "p (b l) -> p b l", b=KB)
        oT = cv
        aqk = take(4 * L)
        qk = view(aqk, 4 * L, "p (b l) -> p b l", b=4)
        asq4 = take(4 * L)
        sq4 = view(asq4, 4 * L, "p (b l) -> p b l", b=4)
        fsq = view(asq4, 5 * C)
        hd = sq4
        avp = take(KB * (L + PAD))
        vp = view(avp, KB * (L + PAD), "p (b l) -> p b l", b=KB)
        ktok = view(take(T * C), T * C, "p (t c) -> p t c", t=T)
        ot = ktok
        au = take(T * C)
        u = view(au, T * C, "p (t c) -> p t c", t=T)
        o = u
        kbt = view(take(C), C)
        vbt = view(take(C), C)
        X = view(take(512), 512, "p (h n) -> p h n", h=GH)
        XT = view(take(512), 512, "p (h n) -> p h n", h=GH)
        R = view(take(512), 512, "p (h n) -> p h n", h=GH)
        atT = view(take(512), 512, "p (h n) -> p h n", h=GH)
        wT = view(take(2 * L), 2 * L, "p (b l) -> p b l", b=2)
        Sb = view(take(256), 256, "p (b n) -> p b n", b=2)
        st = view(take(T * 60), T * 60)
        ast = take(L)
        sT = view(ast, L, parts=60)
        beta = view(take(20), 20, "p (t h) -> p t h", t=T)
        ms = view(take(100), 100)
        lg = view(take(100), 100)
        gw = view(take(100), 100)
        m20 = view(take(20), 20)
        s20 = view(take(20), 20)
        ngdn = used[0]
        used[0] = a0
        qT = view(take(QB * L), QB * L, "p (b l) -> p b l", b=QB)
        cb = qT
        akT = take(QB * L)
        kT = view(akT, QB * L, "p (b l) -> p b l", b=QB)
        vt = view(take(T * 512), T * 512, "p (t c) -> p t c", t=T)
        x1 = view(take(KB * L), KB * L, "p (b l) -> p b l", b=KB)
        xn = x1
        x2 = view(take(KB * L), KB * L, "p (b l) -> p b l", b=KB)
        qraw = view(take(2 * L), 2 * L, "p (b l) -> p b l", b=2)
        qrot = view(take(L), L)
        ck = qraw[:, 0, :]
        ckr = view(take(L), L)
        pr = view(take(2 * L), 2 * L, "p (b l) -> p b l", b=2)
        prT = view(take(2 * 640), 1280, "p (b l) -> p b l", b=2)
        yn = view(take(512), 512, "p (h d) -> p h d", h=AH)
        rsum = view(take(2 * AH), 2 * AH, "p (b h) -> p b h", b=2)
        rinv = view(take(AH), AH)
        nmax = view(take(2 * AH), 2 * AH, "p (b h) -> p b h", b=2)
        gl = view(take(T * E), T * E, "p (t e) -> p t e", t=T)
        rank = view(take(T * E), T * E, "p (t e) -> p t e", t=T)
        m5 = view(take(T), T)
        s5 = view(take(T), T)
        cmpA = view(take(64), 64, "p (e j) -> p e j", e=E)
        cmpB = view(take(64), 64, "p (e j) -> p e j", e=E)
        cT = view(take(L), L, parts=E)
        gs = view(akT, L, "p (b l) -> p b l", b=2)
        gu = view(akT + L, L, "p (b l) -> p b l", b=2)
        used[0] = max(used[0], ngdn)

        tokws_sb = view(a0, KB * C, "p (b o) -> p b o", b=KB)
        tokw_sb = view(a0 + KB * C, D1 * C, "p (d o) -> p d o", d=D1)

        ident, causal = K["ident"], K["causal"]
        wqkv = Wt["wqkv"][:, :].rearrange("p (b m) -> p b m", b=KB)
        bw = Wt["bw"][:, :].rearrange("p (b m) -> p b m", b=KB)
        convw = Wt["convw"][:, :].rearrange("p (b j) -> p b j", b=6)
        firw = Wt["firw"][:, :].rearrange("p (b j) -> p b j", b=KB)
        g1 = Wt["g1"][:, :].rearrange("p (b m) -> p b m", b=3)
        g2 = Wt["g2"][:, :].rearrange("p (b m) -> p b m", b=4)
        ow = Wt["ow"][:, :].rearrange("p (b m) -> p b m", b=KB)
        wq = Wt["wq"][:, :].rearrange("p (b m) -> p b m", b=KB)
        wkva = Wt["wkva"][:, :].rearrange("p (b m) -> p b m", b=KB)
        wkvb, kpad = Wt["wkvb"], Wt["kpad"]
        wo = Wt["wo"][:, :].rearrange("p (b m) -> p b m", b=4)
        wgate = Wt["wgate"][:, :].rearrange("p (b m) -> p b m", b=KB)
        wg = Wt["wg"][:, :].rearrange("p (e b m) -> p e b m", e=NE, b=KB)
        wu = Wt["wu"][:, :].rearrange("p (e b m) -> p e b m", e=NE, b=KB)
        wd = Wt["wd"][:, :].rearrange("p (e m) -> p e m", e=NE)
        pick = K["pick"].rearrange("p (e m) -> p e m", e=E)

        def pair(bank, parts=P):
            return PS[0:parts, bank:bank + 2, 0:HALF]

        def halves(v):
            return v.rearrange("p (a c) -> p a c", a=2)

        def cols(a):
            return slice(a * HALF, (a + 1) * HALF)

        def tok(t):
            return slice(P * t, P * t + NT[t])

        loaded = signal("loaded", 0)
        setup = signal("setup", 0)
        setup_act = signal("setup_act", 0)
        setup_dve = signal("setup_dve", 0)
        x_in = signal("x_in", 32)
        y_out = signal("y_out", 32, start=16)
        v_step = signal("v_step", VSTEPS)
        a_step = signal("a_step", ASTEPS)
        fir_step = signal("fir_step", NFIR)
        xT_ps = signal("xT_ps", 9)
        xT_a = signal("xT_a", 4)
        xT_v = signal("xT_v", 4)
        tok_ps = signal("tok_ps", 1)
        mean_src = signal("mean_src", 2)
        mean_ps = signal("mean_ps", 2)
        norm_src = signal("norm_src", 4)
        norm_sq = signal("norm_sq", 4)
        norm_ps = signal("norm_ps", 4)
        norm_sd = signal("norm_sd", 4)
        norm_out = signal("norm_out", 4)
        qkv_ps = signal("qkv_ps", 6)
        z_done = signal("z_done", 6)
        conv_done = signal("conv_done", 6)
        silu_done = signal("silu_done", 6)
        beta_ps = signal("beta_ps", 1)
        beta_done = signal("beta_done", 1)
        l2_sq = signal("l2_sq", 1)
        l2_ps = signal("l2_ps", 1)
        l2_sd = signal("l2_sd", 1)
        qk_done = signal("qk_done", 1)
        kv_ps = signal("kv_ps", T)
        kv_tok = signal("kv_tok", T)
        kvb_done = signal("kvb_done", T)
        G_ps = signal("G_ps", T)
        M_done = signal("M_done", T)
        MT_ps = signal("MT_ps", T)
        MT_done = signal("MT_done", T)
        R_done = signal("R_done", 5 * T)
        sq_ps = signal("sq_ps", 4 * T)
        X_done = signal("X_done", 4 * T)
        XT_done = signal("XT_done", 3 * T)
        R_ps = signal("R_ps", 4 * T)
        uw_ps = signal("uw_ps", T)
        uw_done = signal("uw_done", T)
        at_ps = signal("at_ps", T)
        at_done = signal("at_done", T)
        w_ps = signal("w_ps", NCHUNK)
        ua_done = signal("ua_done", NCHUNK)
        S_ps = signal("S_ps", NCHUNK)
        S_done = signal("S_done", NCHUNK + 1)
        o_ps = signal("o_ps", T)
        o_done = signal("o_done", T)
        f_ps = signal("f_ps", T)
        f_tok = signal("f_tok", T)
        f_sq = signal("f_sq", T)
        f_used = signal("f_used", T)
        rms_in = signal("rms_in", 1)
        st_done = signal("st_done", 1)
        st_ps = signal("st_ps", 1)
        sT_done = signal("sT_done", 1)
        g1_ps = signal("g1_ps", 4)
        hd_done = signal("hd_done", 4)
        g2_ps = signal("g2_ps", 1)
        lg_in = signal("lg_in", 1)
        lg_exp = signal("lg_exp", 1)
        oss = signal("oss", 1)
        oss_sd = signal("oss_sd", 1)
        on_done = signal("on_done", 1)
        oT_ps = signal("oT_ps", 1)
        oT_done = signal("oT_done", 1)
        ow_ps = signal("ow_ps", 1)
        ck_ps = signal("ck_ps", 1)
        ck_done = signal("ck_done", 1)
        cks_ps = signal("cks_ps", 1)
        ckr_done = signal("ckr_done", 1)
        kT_ps = signal("kT_ps", QB)
        kT_done = signal("kT_done", QB)
        vt_ps = signal("vt_ps", T)
        vt_done = signal("vt_done", T)
        q_ps = signal("q_ps", QB)
        q_done = signal("q_done", QB)
        qs_ps = signal("qs_ps", QB)
        qT_done = signal("qT_done", QB)
        s_ps = signal("s_ps", T * AH)
        max_done = signal("max_done", T * AH)
        exp_done = signal("exp_done", T * AH)
        pT_ps = signal("pT_ps", T * AH)
        pT_done = signal("pT_done", T * AH)
        y_ps = signal("y_ps", T)
        yn_done = signal("yn_done", T)
        yT_ps = signal("yT_ps", T)
        yT_done = signal("yT_done", T)
        wo_ps = signal("wo_ps", 1)
        gl_ps = signal("gl_ps", 1)
        gl_in = signal("gl_in", 1)
        gl_exp = signal("gl_exp", 1)
        comb_done = signal("comb_done", 1)
        cT_ps = signal("cT_ps", 1)
        cT_done = signal("cT_done", 1)
        cb_ps = signal("cb_ps", E)
        cb_done = signal("cb_done", E)
        gu_ps = signal("gu_ps", 2 * NE)
        gs_done = signal("gs_done", 2 * NE)
        gu_done = signal("gu_done", 2 * NE)
        dn_ps = signal("dn_ps", 2 * NE)
        res_done = signal("res_done", 2)
        rT_ps = signal("rT_ps", T)
        rT_done = signal("rT_done", T, start=1)

        block = ctx.enter_context(nc.Block())
        nloads = len(WEIGHTS) + 3

        @block.sync
        def _(sp):
            for name in WEIGHTS:
                sp.dma_start(Wt[name][:, :], weights[name]).then_inc(loaded.sem, 16)
            sp.dma_start(cst[:, :], consts).then_inc(loaded.sem, 16)
            sp.dma_start(tokws_sb, tokws.rearrange("(b p) o -> p b o", p=P)).then_inc(loaded.sem, 16)
            sp.dma_start(tokw_sb, tokw.rearrange("p (d o) -> p d o", d=D1)).then_inc(loaded.sem, 16)
            sp.wait_ge(setup.sem, 2)

            def load(i):
                sp.dma_start(xs.rearrange("p t i d -> p t (i d)"),
                             x[bass.ds(i, 1)].rearrange("a (t p) i d -> p (a t) (i d)", p=P)).then_inc(x_in.sem, 16)
                sp.dma_start(xt, txt[bass.ds(i, 1)].rearrange("a t c -> (a t) c")).then_inc(x_in.sem, 16)

            def store(i):
                sp.wait_ge(*rT_done(i, T))
                sp.dma_start(out[bass.ds(i, 1), 0:LI].rearrange("a (t p) c -> p (a t) c", p=P),
                             ot[:, 0:4, :]).then_inc(y_out.sem, 16)
                sp.dma_start(out[bass.ds(i, 1), LI:L].rearrange("a t c -> (a t) c"),
                             ot[0:LT, 4, :]).then_inc(y_out.sem, 16)

            sp.sem_inc(y_out.sem, y_out.start)
            load(0)
            with sp.Fori(0, nseq - 1) as i:
                sp.wait_ge(*on_done(i, 1))
                load(i + 1)
                store(i)
            store(nseq - 1)
            sp.wait_ge(*y_out(nseq, 0))

        @block.tensor
        def _(pe):
            mm, tr = pe.matmul, pe.transpose
            pe.wait_ge(loaded.sem, 16 * nloads)
            pe.wait_ge(setup.sem, 3)

            carrier = pe.alloc_register("carrier")
            pe.reg_mov(carrier, 0)

            def small(yes=True):
                if yes:
                    pe.nop(nofuse=True)

            def norm(i, n, src, bank):
                pe.wait_ge(*norm_sq(i, n + 1))
                for a in range(2):
                    for b in range(KB):
                        last = mm(PS[:, bank + a, 0:HALF], K["mean"], sq[:, b, cols(a)], start=b == 0, stop=b == KB - 1)
                last.then_inc(norm_ps.sem, 1)

            def mean(i, n):
                pe.wait_ge(*mean_src(i, n + 1))
                for a in range(2):
                    for b in range(KB):
                        last = mm(PS[:, a, 0:HALF], K["mean"], h[:, b, cols(a)], start=b == 0, stop=b == KB - 1)
                last.then_inc(mean_ps.sem, 1)

            with pe.Fori(0, nseq) as i:
                pe.wait_ge(*x_in(i, 32))
                pe.wait_ge(*rT_done(i, 0))
                for k in range(8):
                    d, b = k // KB, k % KB
                    if k >= 2:
                        pe.wait_ge(*(xT_v if k % 2 else xT_a)(i, k // 2))
                    for t in range(4):
                        last = tr(PS[:, k % 2, P * t:P * t + P], xs[:, t, P * b:P * b + P, d], ident)
                    last.then_inc(xT_ps.sem, 1)
                for b in range(KB):
                    last = tr(PS[:, 4, LT * b:LT * b + LT], xt[:, P * b:P * b + P], ident[0:LT, 0:LT])
                last.then_inc(xT_ps.sem, 1)
                pe.wait_ge(*xT_a(i, 4))
                pe.wait_ge(*xT_v(i, 4))
                for m in range(KB):
                    for k in range(8):
                        last = mm(PS[:, 2 + m, :], tokwT[:, k, P * m:P * m + P], xT[:, k, :], start=k == 0, stop=k == 7)
                last.then_inc(tok_ps.sem, 1)
                mean(i, 0)
                norm(i, 0, None, 2)
                pe.wait_ge(*norm_out(i, 1))
                for m in range(6):
                    if m >= 2:
                        pe.wait_ge(*z_done(i, m - 1))
                    for a in range(2):
                        for b in range(KB):
                            last = mm(PS[:, 2 * (m % 2) + a, 0:HALF], wqkv[:, b, P * m:P * m + P], hn[:, b, cols(a)],
                                      start=b == 0, stop=b == KB - 1)
                    last.then_inc(qkv_ps.sem, 1)
                for t in range(T):
                    for b in range(KB):
                        last = mm(PS[0:NT[t], 4, GH * t:GH * t + GH], hn[:, b, tok(t)], bw[:, b, :],
                                  start=b == 0, stop=b == KB - 1)
                last.then_inc(beta_ps.sem, 1)
                pe.wait_ge(*l2_sq(i, 1))
                for m in range(4):
                    for a in range(2):
                        last = mm(PS[:, 2 * m + a, 0:HALF], K["heads"], sq4[:, m, cols(a)], start=True, stop=True)
                last.then_inc(l2_ps.sem, 1)
                pe.wait_ge(*qk_done(i, 1))
                for t in range(T):
                    if t >= 2:
                        pe.wait_ge(*kv_tok(i, t - 1))
                    for b in range(KB):
                        tr(PS[0:NT[t], t % 2, P * b:P * b + P], qk[:, 2 + b, tok(t)], ident)
                        last = tr(PS[0:NT[t], t % 2, C + P * b:C + P * b + P],
                                  vp[:, b, PAD + P * t:PAD + P * t + NT[t]], ident)
                    last.then_inc(kv_ps.sem, 1)
                pe.wait_ge(*S_done(i, 1))
                for t in range(T):
                    n = NT[t]
                    small(t == 4)
                    for hh in range(GH):
                        kh = qk[GD * (hh % 2):GD * (hh % 2) + GD, 2 + hh // 2, tok(t)]
                        last = mm(PS[0:n, 2 + hh % 2, P * (hh // 2):P * (hh // 2) + n], kh, kh, start=True, stop=True)
                    last.then_inc(G_ps.sem, 1)
                    if t:
                        pe.wait_ge(*at_done(i, t))
                        pe.wait_ge(*o_done(i, t))
                        small(t == 4)
                    for hh in range(GH):
                        kh = qk[GD * (hh % 2):GD * (hh % 2) + GD, 2 + hh // 2, tok(t)]
                        qh = qk[GD * (hh % 2):GD * (hh % 2) + GD, hh // 2, tok(t)]
                        last = mm(PS[0:n, 5 + hh % 2, P * (hh // 2):P * (hh // 2) + n], kh, qh, start=True, stop=True)
                    last.then_inc(at_ps.sem, 1)
                    pe.wait_ge(*M_done(i, t + 1))
                    small(t == 4)
                    for hh in range(GH):
                        last = tr(PS[0:n, 3, P * hh:P * hh + n], X[0:n, hh, 0:n], ident[0:n, 0:n])
                    last.then_inc(MT_ps.sem, 1)
                    pe.wait_ge(*MT_done(i, t + 1))
                    pe.wait_ge(*at_done(i, t + 1))
                    for lv in range(4):
                        if lv:
                            pe.wait_ge(*XT_done(i, 3 * t + lv))
                        small(t == 4)
                        for hh in range(GH):
                            last = mm(PS[0:n, 4, P * hh:P * hh + n], XT[0:n, hh, 0:n], X[0:n, hh, 0:n],
                                      start=True, stop=True)
                            if lv < 3:
                                last = mm(PS[0:n, 5, P * hh:P * hh + n], X[0:n, hh, 0:n], XT[0:n, hh, 0:n],
                                          start=True, stop=True)
                        last.then_inc(sq_ps.sem, 1)
                        pe.wait_ge(*X_done(i, 4 * t + lv + 1))
                        pe.wait_ge(*R_done(i, 5 * t + lv + 1))
                        small(t == 4)
                        for hh in range(GH):
                            last = mm(PS[0:n, 6, P * hh:P * hh + n], X[0:n, hh, 0:n], R[0:n, hh, 0:n],
                                      start=True, stop=True)
                        last.then_inc(R_ps.sem, 1)
                    pe.wait_ge(*R_done(i, 5 * t + 5))
                    pe.wait_ge(*kvb_done(i, t + 1))
                    small(t == 4)
                    for hh in range(GH):
                        mm(PS[0:n, 2, GD * hh:GD * hh + GD], R[0:n, hh, 0:n], vbt[0:n, GD * hh:GD * hh + GD],
                           start=True, stop=True)
                        r0 = GD * (hh % 2)
                        last = mm(PS[r0:r0 + GD, 3, P * (hh // 2):P * (hh // 2) + n], kbt[0:n, GD * hh:GD * hh + GD],
                                  R[0:n, hh, 0:n], start=True, stop=True)
                    last.then_inc(uw_ps.sem, 1)
                    pe.wait_ge(*uw_done(i, t + 1))
                    for j in range(n // CH):
                        c = 4 * t + j
                        rows = slice(CH * j, CH * j + CH)
                        pe.wait_ge(*S_done(i, c + 1))
                        for p in range(2):
                            mm(PS[rows, 4, P * p:P * p + P], wT[:, p, CH * c:CH * c + CH], Sb[:, p, :],
                               start=p == 0, stop=True, skip_group_check=True, tile_position=(0, CH * j))
                            last = mm(PS[rows, 5, P * p:P * p + P], qk[:, p, CH * c:CH * c + CH], Sb[:, p, :],
                                      start=p == 0, stop=False, skip_group_check=True, tile_position=(0, CH * j))
                        last.then_inc(w_ps.sem, 1)
                        pe.wait_ge(*ua_done(i, c + 1))
                        for p in range(2):
                            last = mm(PS[:, 7, P * p:P * p + P], ktok[rows, t, P * p:P * p + P],
                                      u[rows, t, P * p:P * p + P], start=c == 0 and p == 0, stop=True,
                                      skip_group_check=True, tile_position=(CH * j, 0))
                        last.then_inc(S_ps.sem, 1)
                    for hh in range(GH):
                        last = mm(PS[0:n, 5, GD * hh:GD * hh + GD], atT[0:n, hh, 0:n], u[0:n, t, GD * hh:GD * hh + GD],
                                  start=False, stop=True, skip_group_check=True)
                    last.then_inc(o_ps.sem, 1)
                pe.wait_ge(*fir_step(i, NFIR))
                pe.wait_ge(*uw_done(i, T))
                for t in range(T):
                    if t >= 2:
                        pe.wait_ge(*f_tok(i, t - 1))
                    for f in range(3):
                        for b in range(KB):
                            dst = C * f + P * b
                            last = tr(PS[0:NT[t], 2 * (t % 2) + dst // 512, dst % 512:dst % 512 + P],
                                      fir[:, f, b, tok(t)], ident)
                    last.then_inc(f_ps.sem, 1)
                pe.wait_ge(*st_done(i, 1))
                pe.wait_ge(*o_done(i, T))
                small()
                for t in range(T):
                    last = tr(PS[0:60, 4 + t // 4, P * (t % 4):P * (t % 4) + NT[t]], st[0:NT[t], 60 * t:60 * t + 60],
                              ident[0:NT[t], 0:NT[t]])
                last.then_inc(st_ps.sem, 1)
                pe.wait_ge(*sT_done(i, 1))
                for m in range(4):
                    if m >= 2:
                        pe.wait_ge(*hd_done(i, m - 1))
                    for a in range(2):
                        dst = PS[:, 2 * (m % 2) + a, 0:HALF]
                        mm(dst, g1[:, 0, P * m:P * m + P], hn[:, 0, cols(a)], start=True, stop=False)
                        mm(dst, g1[:, 1, P * m:P * m + P], hn[:, 1, cols(a)], start=False, stop=False)
                        last = mm(dst, g1[0:60, 2, P * m:P * m + P], sT[:, cols(a)], start=False, stop=True)
                    last.then_inc(g1_ps.sem, 1)
                pe.wait_ge(*hd_done(i, 4))
                for t in range(T):
                    for b in range(4):
                        last = mm(PS[0:NT[t], 6, 20 * t:20 * t + 20], hd[:, b, tok(t)], g2[:, b, :],
                                  start=b == 0, stop=b == 3)
                last.then_inc(g2_ps.sem, 1)
                pe.wait_ge(*on_done(i, 1))
                for t in range(T):
                    for b in range(KB):
                        dst = PS[:, 4 + b, P * t:P * t + P] if t < 4 else PS[:, 6, LT * b:LT * b + LT]
                        last = tr(dst, o[0:NT[t], t, P * b:P * b + P], ident[0:NT[t], 0:NT[t]])
                last.then_inc(oT_ps.sem, 1)
                pe.wait_ge(*oT_done(i, 1))
                for m in range(KB):
                    for a in range(2):
                        for b in range(KB):
                            last = mm(PS[:, 2 * m + a, 0:HALF], ow[:, b, P * m:P * m + P], oT[:, b, cols(a)],
                                      start=b == 0, stop=b == KB - 1)
                last.then_inc(ow_ps.sem, 1)
                mean(i, 1)
                norm(i, 1, None, 2)
                norm(i, 2, None, 0)
                pe.wait_ge(*norm_out(i, 3))
                for a in range(2):
                    for b in range(KB):
                        last = mm(PS[0:AD, 2 + a, 0:HALF], wkva[:, b, :], x1[:, b, cols(a)], start=b == 0, stop=b == KB - 1)
                last.then_inc(ck_ps.sem, 1)
                pe.wait_ge(*ck_done(i, 1))
                small()
                for a in range(2):
                    last = mm(PS[0:AD, 4 + a, 0:HALF], K["swap"][0:AD, 0:AD], ck[0:AD, cols(a)], start=True, stop=True)
                last.then_inc(cks_ps.sem, 1)
                pe.wait_ge(*ckr_done(i, 1))
                for m in range(QB):
                    if m >= 2:
                        pe.wait_ge(*kT_done(i, m - 1))
                    for a in range(2):
                        last = mm(PS[:, 2 * (m % 2) + a, 0:HALF], kpad[:, P * m:P * m + P], ckr[0:AD, cols(a)],
                                  start=True, stop=True)
                    last.then_inc(kT_ps.sem, 1)
                for t in range(T):
                    if t >= 2:
                        pe.wait_ge(*vt_done(i, t - 1))
                    small(t == 4)
                    mm(PS[0:NT[t], 4 + t % 2, :], ckr[0:32, tok(t)], wkvb[:, :], start=True, stop=True
                       ).then_inc(vt_ps.sem, 1)
                pe.wait_ge(*kT_done(i, QB))
                pe.wait_ge(*vt_done(i, T))
                for m in range(QB + 1):
                    if m < QB:
                        if m >= 2:
                            pe.wait_ge(*q_done(i, m - 1))
                        for a in range(2):
                            for b in range(KB):
                                last = mm(PS[:, 2 * (m % 2) + a, 0:HALF], wq[:, b, P * m:P * m + P], x1[:, b, cols(a)],
                                          start=b == 0, stop=b == KB - 1)
                        last.then_inc(q_ps.sem, 1)
                    if m:
                        r = m - 1
                        pe.wait_ge(*q_done(i, r + 1))
                        if r >= 2:
                            pe.wait_ge(*qT_done(i, r - 1))
                        for a in range(2):
                            last = mm(PS[:, 4 + 2 * (r % 2) + a, 0:HALF], K["swap"], qraw[:, r % 2, cols(a)],
                                      start=True, stop=True)
                        last.then_inc(qs_ps.sem, 1)
                pe.wait_ge(*qT_done(i, QB))
                steps = [(t, hh) for t in range(T) for hh in range(AH)]

                def scores(n):
                    t, hh = steps[n]
                    if n >= 2:
                        pe.wait_ge(*exp_done(i, n - 1))
                        small(t == 4)
                    r0 = AD * (hh % 2)
                    q = qT[r0:r0 + AD, hh // 2, tok(t)]
                    for c0 in range(0, P * t + NT[t], 512):
                        c1 = min(c0 + 512, P * t + NT[t])
                        last = mm(PS[0:NT[t], 2 * (n % 2) + c0 // 512, 0:c1 - c0], q, kT[r0:r0 + AD, hh // 2, c0:c1],
                                  start=True, stop=True)
                    last.then_inc(s_ps.sem, 1)

                def turn(n):
                    t, hh = steps[n]
                    pe.wait_ge(*exp_done(i, n + 1))
                    if n >= 1:
                        pe.wait_ge(*pT_done(i, n))
                        small(t == 4)
                    for k in range(t + 1):
                        last = tr(PS[0:NT[k], 4 + k // 4, P * (k % 4):P * (k % 4) + NT[t]],
                                  pr[0:NT[t], n % 2, tok(k)], ident[0:NT[t], 0:NT[t]])
                    last.then_inc(pT_ps.sem, 1)

                def times_v(n):
                    t, hh = steps[n]
                    pe.wait_ge(*pT_done(i, n + 1))
                    if hh == 0 and t:
                        pe.wait_ge(*yn_done(i, t))
                    small(t == 4)
                    for k in range(t + 1):
                        last = mm(PS[0:NT[t], 6, NOPE * hh:NOPE * hh + NOPE], prT[0:NT[k], n % 2, P * k:P * k + NT[t]],
                                  vt[0:NT[k], k, NOPE * hh:NOPE * hh + NOPE], start=k == 0, stop=k == t)
                    if hh == AH - 1:
                        last.then_inc(y_ps.sem, 1)

                def y_turn(t):
                    pe.wait_ge(*yn_done(i, t + 1))
                    if t:
                        pe.wait_ge(*yT_done(i, t))
                    small(t == 4)
                    for b in range(4):
                        last = tr(PS[:, 7, P * b:P * b + NT[t]], yn[0:NT[t], 4 * b:4 * b + 4, :].rearrange(
                            "p h d -> p (h d)"), ident[0:NT[t], 0:NT[t]])
                    last.then_inc(yT_ps.sem, 1)

                N = len(steps)
                scores(0)
                for n in range(N + 1):
                    if n + 1 < N:
                        scores(n + 1)
                    if n < N:
                        turn(n)
                    if n >= 1:
                        times_v(n - 1)
                        if (n - 1) % AH == AH - 1:
                            y_turn((n - 1) // AH)
                pe.wait_ge(*yT_done(i, T))
                for m in range(KB):
                    for a in range(2):
                        for b in range(4):
                            last = mm(PS[:, 2 * m + a, 0:HALF], wo[:, b, P * m:P * m + P], yT[:, b, cols(a)],
                                      start=b == 0, stop=b == 3)
                last.then_inc(wo_ps.sem, 1)
                norm(i, 3, None, 4)
                pe.wait_ge(*norm_out(i, 4))
                for t in range(T):
                    for b in range(KB):
                        last = mm(PS[0:NT[t], 6, E * t:E * t + E], xn[:, b, tok(t)], wgate[:, b, :],
                                  start=b == 0, stop=b == KB - 1)
                last.then_inc(gl_ps.sem, 1)
                pe.wait_ge(*comb_done(i, 1))
                small()
                for t in range(T):
                    last = tr(PS[0:E, 4 + t // 4, P * (t % 4):P * (t % 4) + NT[t]], gl[0:NT[t], t, :],
                              ident[0:NT[t], 0:NT[t]])
                last.then_inc(cT_ps.sem, 1)
                pe.wait_ge(*cT_done(i, 1))
                small()
                for e in range(E):
                    if e >= 2:
                        pe.wait_ge(*cb_done(i, e - 1))
                    for a in range(2):
                        last = mm(PS[:, 2 * (e % 2) + a, 0:HALF], pick[0:E, e, :], cT[:, cols(a)], start=True, stop=True)
                    last.then_inc(cb_ps.sem, 1)
                pe.wait_ge(*cb_done(i, E))
                units = [(a, e) for a in range(2) for e in range(NE)]
                for n in range(len(units) + 1):
                    if n < len(units):
                        a, e = units[n]
                        if n >= 2:
                            pe.wait_ge(*gu_done(i, n - 1))
                        for w, bank in ((wg, 2 * (n % 2)), (wu, 2 * (n % 2) + 1)):
                            for b in range(KB):
                                last = mm(PS[:, bank, 0:HALF], w[:, e, b, :], xn[:, b, cols(a)],
                                          start=b == 0, stop=b == KB - 1)
                        last.then_inc(gu_ps.sem, 1)
                    if n:
                        a, e = units[n - 1]
                        pe.wait_ge(*gu_done(i, n))
                        for m in range(KB):
                            last = mm(PS[:, 4 + 2 * a + m, 0:HALF], wd[:, e, P * m:P * m + P], gu[:, (n - 1) % 2, :],
                                      start=e == 0, stop=e == NE - 1)
                        last.then_inc(dn_ps.sem, 1)
                pe.wait_ge(*res_done(i, 2))
                for t in range(T):
                    if t >= 2:
                        pe.wait_ge(*rT_done(i, t - 1))
                    for b in range(KB):
                        last = tr(PS[0:NT[t], t % 2, P * b:P * b + P], h[:, b, tok(t)], ident)
                    last.then_inc(rT_ps.sem, 1)

        @block.scalar
        def _(act):
            A = act.activation
            steps = [0]

            def link(i, ins):
                ins.then_inc(a_step.sem, 1)
                steps[0] += 1
                act.wait_ge(*a_step(i, steps[0]))

            act.wait_ge(loaded.sem, 16 * nloads)
            act.wait_ge(setup.sem, 2)
            for hh in range(GH):
                A(gk[:, 20 + 5 * hh:25 + 5 * hh], Wt["ltemp"][:, hh:hh + 1].to_broadcast([P, 5]), ACT.Exp, scale=-1.0)
                last = A(gk[:, 40 + 5 * hh:45 + 5 * hh], Wt["floor"][:, hh:hh + 1].to_broadcast([P, 5]), ACT.Sigmoid)
            last.then_inc(setup_act.sem, 1)

            act.sem_inc(rT_done.sem, rT_done.start)

            def norm(i, n, src):
                act.wait_ge(*norm_src(i, n + 1))
                A(sq, src, ACT.Square).then_inc(norm_sq.sem, 1)
                act.wait_ge(*norm_ps(i, n + 1))
                bank = (2, 2, 0, 4)[n]
                A(halves(sd), pair(bank), ACT.Sqrt, bias=K["eps5"]).then_inc(norm_sd.sem, 1)

            with act.Fori(0, nseq) as i:
                for k in range(0, 8, 2):
                    act.wait_ge(*xT_ps(i, k + 1))
                    A(xT[:, k, :], PS[:, 0, :], ACT.Copy).then_inc(xT_a.sem, 1)
                norm(i, 0, hc)
                for m in range(6):
                    act.wait_ge(*qkv_ps(i, m + 1))
                    A(halves(z[:, m, 3:3 + L]), pair(2 * (m % 2)), ACT.Copy).then_inc(z_done.sem, 1)
                for m in range(6):
                    act.wait_ge(*conv_done(i, m + 1))
                    dst = qk[:, m, :] if m < 4 else vp[:, m - 4, PAD:PAD + L]
                    A(dst, cv[:, m % 2, :], ACT.Silu).then_inc(silu_done.sem, 1)
                act.wait_ge(*beta_ps(i, 1))
                A(beta[:, 0:4, :], PS[:, 4, 0:16].rearrange("p (t h) -> p t h", t=4), ACT.Sigmoid)
                A(beta[0:LT, 4, :], PS[0:LT, 4, 16:20], ACT.Sigmoid).then_inc(beta_done.sem, 1)
                act.wait_ge(*silu_done(i, 4))
                A(sq4, qk, ACT.Square).then_inc(l2_sq.sem, 1)
                act.wait_ge(*l2_ps(i, 1))
                A(sq4.rearrange("p b (a c) -> p (b a) c", a=2), PS[:, :, 0:HALF], ACT.Sqrt,
                  bias=K["eps6"]).then_inc(l2_sd.sem, 1)
                act.wait_ge(*y_out(i, 0))
                A(Sb, Sb, ACT.Copy, scale=0.0).then_inc(S_done.sem, 1)
                for t in range(T):
                    n = NT[t]
                    act.wait_ge(*kv_ps(i, t + 1))
                    A(ktok[0:n, t, :], PS[0:n, t % 2, 0:C], ACT.Copy)
                    A(F[0:n, t, 4, :], PS[0:n, t % 2, C:2 * C], ACT.Copy).then_inc(kv_tok.sem, 1)
                for t in range(T):
                    n = NT[t]
                    act.wait_ge(*MT_ps(i, t + 1))
                    A(XT[0:n, :, 0:n], PS[0:n, 3, :].rearrange("p (h n) -> p h n", h=GH)[:, :, 0:n],
                      ACT.Copy).then_inc(MT_done.sem, 1)
                    act.wait_ge(*R_done(i, 5 * t + 1))
                    for lv in range(3):
                        act.wait_ge(*sq_ps(i, 4 * t + lv + 1))
                        A(XT[0:n, :, 0:n], PS[0:n, 5, :].rearrange("p (h n) -> p h n", h=GH)[:, :, 0:n],
                          ACT.Copy).then_inc(XT_done.sem, 1)
                    act.wait_ge(*uw_ps(i, t + 1))
                    A(u[0:n, t, :], PS[0:n, 2, 0:C], ACT.Copy)
                    A(wT[:, :, tok(t)], PS[:, 3, 0:C].rearrange("p (b n) -> p b n", b=2)[:, :, 0:n],
                      ACT.Copy).then_inc(uw_done.sem, 1)
                    for j in range(n // CH):
                        c = 4 * t + j
                        act.wait_ge(*S_ps(i, c + 1))
                        for q in range(2):
                            r = slice(GD * q, GD * q + GD)
                            last = A(Sb[r, :, r], PS[r, 7, 0:C].rearrange("p (b n) -> p b n", b=2)[:, :, r], ACT.Copy)
                        last.then_inc(S_done.sem, 1)
                    act.wait_ge(*o_ps(i, t + 1))
                    A(F[0:n, t, 3, :], PS[0:n, 5, 0:C], ACT.Copy).then_inc(o_done.sem, 1)
                for t in range(T):
                    n = NT[t]
                    act.wait_ge(*f_ps(i, t + 1))
                    A(F[0:n, t, 0:2, :], PS[0:n, 2 * (t % 2), :].rearrange("p (k c) -> p k c", k=2), ACT.Copy)
                    A(F[0:n, t, 2, :], PS[0:n, 2 * (t % 2) + 1, 0:C], ACT.Copy).then_inc(f_tok.sem, 1)
                    act.wait_ge(*f_tok(i, t + 1))
                    if t:
                        act.wait_ge(*f_used(i, t))
                    A(fsq[0:n, :], F[0:n, t, :, :].rearrange("p k c -> p (k c)"), ACT.Square).then_inc(f_sq.sem, 1)
                act.wait_ge(*rms_in(i, 1))
                A(st.rearrange("p (g s h) -> p g s h", s=3, h=4)[:, :, 1, :], ms.rearrange("p (g h) -> p g h", h=4),
                  ACT.Sqrt).then_inc(st_done.sem, 1)
                act.wait_ge(*st_ps(i, 1))
                A(sT[:, 0:512], PS[0:60, 4, :], ACT.Copy)
                A(sT[:, 512:L], PS[0:60, 5, 0:LT], ACT.Copy).then_inc(sT_done.sem, 1)
                for m in range(4):
                    act.wait_ge(*g1_ps(i, m + 1))
                    A(halves(hd[:, m, :]), pair(2 * (m % 2)), ACT.Gelu, bias=Wt["g1b"][:, m:m + 1]).then_inc(hd_done.sem, 1)
                act.wait_ge(*lg_in(i, 1))
                A(lg, lg, ACT.Exp).then_inc(lg_exp.sem, 1)
                act.wait_ge(*oss(i, 1))
                A(s20, m20, ACT.Sqrt, bias=K["eps5"]).then_inc(oss_sd.sem, 1)
                act.wait_ge(*oT_ps(i, 1))
                for b in range(KB):
                    A(oT[:, b, 0:512], PS[:, 4 + b, :], ACT.Copy)
                A(oT[:, :, 512:L], PS[:, 6, 0:2 * LT].rearrange("p (b l) -> p b l", b=2), ACT.Copy).then_inc(oT_done.sem, 1)
                norm(i, 1, hc)
                norm(i, 2, hn)
                act.wait_ge(*ck_ps(i, 1))
                A(halves(ck[0:AD, :]), pair(2, AD), ACT.Copy).then_inc(ck_done.sem, 1)
                for m in range(QB):
                    act.wait_ge(*kT_ps(i, m + 1))
                    A(halves(kT[:, m, :]), pair(2 * (m % 2)), ACT.Copy).then_inc(kT_done.sem, 1)
                for t in range(T):
                    n = NT[t]
                    act.wait_ge(*vt_ps(i, t + 1))
                    A(vt[0:n, t, :], PS[0:n, 4 + t % 2, :], ACT.Copy).then_inc(vt_done.sem, 1)
                for m in range(QB):
                    act.wait_ge(*q_ps(i, m + 1))
                    if m >= 2:
                        act.wait_ge(*qT_done(i, m - 1))
                    A(halves(qraw[:, m % 2, :]), pair(2 * (m % 2)), ACT.Copy, scale=AD ** -0.5).then_inc(q_done.sem, 1)
                for n in range(T * AH):
                    t, hh = n // AH, n % AH
                    rows, kk = NT[t], P * t + NT[t]
                    act.wait_ge(*max_done(i, n + 1))
                    if n >= 2:
                        act.wait_ge(*pT_ps(i, n - 1))
                    if hh == 0 and t >= 2:
                        act.wait_ge(*yn_done(i, t - 1))
                    bank = 2 * (n % 2)
                    src = PS[0:rows, bank:bank + 2, :].rearrange("p a c -> p (a c)")[:, 0:kk]
                    A(pr[0:rows, n % 2, 0:kk], src, ACT.Exp, bias=nmax[0:rows, t % 2, hh:hh + 1],
                      accum_out=rsum[0:rows, t % 2, hh:hh + 1]).then_inc(exp_done.sem, 1)
                    if hh == 2 and t:
                        act.wait_ge(*yT_ps(i, t))
                        A(yT[:, :, tok(t - 1)], PS[:, 7, :].rearrange("p (b n) -> p b n", b=4)[:, :, 0:P],
                          ACT.Copy).then_inc(yT_done.sem, 1)
                act.wait_ge(*yT_ps(i, T))
                A(yT[:, :, tok(T - 1)], PS[:, 7, :].rearrange("p (b n) -> p b n", b=4)[:, :, 0:LT],
                  ACT.Copy).then_inc(yT_done.sem, 1)
                norm(i, 3, x2)
                act.wait_ge(*gl_in(i, 1))
                A(gl, gl, ACT.Exp).then_inc(gl_exp.sem, 1)
                act.wait_ge(*cT_ps(i, 1))
                A(cT[:, 0:512], PS[0:E, 4, :], ACT.Copy)
                A(cT[:, 512:L], PS[0:E, 5, 0:LT], ACT.Copy).then_inc(cT_done.sem, 1)
                for e in range(E):
                    act.wait_ge(*cb_ps(i, e + 1))
                    A(halves(cb[:, e, :]), pair(2 * (e % 2)), ACT.Copy).then_inc(cb_done.sem, 1)
                for n in range(2 * NE):
                    act.wait_ge(*gu_ps(i, n + 1))
                    if n >= 2:
                        act.wait_ge(*gu_done(i, n - 1))
                    A(gs[:, n % 2, :], PS[:, 2 * (n % 2), 0:HALF], ACT.Silu).then_inc(gs_done.sem, 1)
                for t in range(T):
                    n = NT[t]
                    act.wait_ge(*rT_ps(i, t + 1))
                    A(ot[0:n, t, :], PS[0:n, t % 2, 0:C], ACT.Copy).then_inc(rT_done.sem, 1)
                assert steps[0] == ASTEPS, ("ASTEPS", steps[0])

        @block.vector
        def _(dve):
            steps = [0]

            def link(i, ins):
                ins.then_inc(v_step.sem, 1)
                steps[0] += 1
                dve.wait_ge(*v_step(i, steps[0]))

            TT, TS, STT, RED, CP = (dve.tensor_tensor, dve.tensor_scalar, dve.scalar_tensor_tensor,
                                    dve.tensor_reduce, dve.tensor_copy)

            dve.wait_ge(loaded.sem, 16 * nloads)
            dve.memset(hc, 0.0).then_inc(setup.sem, 1)
            for k in range(8):
                d, b = k // KB, k % KB
                TT(tokwT[:, k, :], tokws_sb[:, b, :], tokw_sb[:, d, :], ALU.mult)
            dve.memset(gfloor[:, :], 0.0)
            last = CP(gk[:, 0:20], Wt["g2b"][:, :])
            last.then_inc(setup_dve.sem, 1)
            dve.wait_ge(setup_dve.sem, 1)
            dve.memset(arena[:, :], 0.0).then_inc(setup.sem, 1)
            g3 = gk[:, 0:20].rearrange("p (h k) -> p h k", k=5)
            TT(g3[:, :, 4], g3[:, :, 4], Wt["vbias"][:, :], ALU.add)
            dve.wait_ge(setup_act.sem, 1)
            f3 = gfloor[:, :].rearrange("p (h k) -> p h k", k=5)
            s3 = gk[:, 40:60].rearrange("p (h k) -> p h k", k=5)
            CP(f3[:, :, 0:4], s3[:, :, 0:4]).then_inc(setup_dve.sem, 1)
            dve.wait_ge(setup_dve.sem, 2)
            TS(gk[:, 40:60], gk[:, 40:60], -4.0, 1.0, ALU.mult, ALU.add).then_inc(setup.sem, 1)

            def centre(i, n):
                dve.wait_ge(*mean_ps(i, n + 1))
                for b in range(KB):
                    last = TT(halves(hc[:, b, :]), halves(h[:, b, :]), pair(0), ALU.subtract)
                last.then_inc(norm_src.sem, 1)

            def norm(i, n, src, dst, weight=None):
                dve.wait_ge(*norm_sd(i, n + 1))
                link(i, dve.reciprocal(sd, sd))
                for b in range(KB):
                    if weight is None:
                        last = TT(dst[:, b, :], src[:, b, :], sd, ALU.mult)
                    else:
                        last = STT(dst[:, b, :], src[:, b, :], weight[:, b:b + 1], sd, ALU.mult, ALU.mult)
                last.then_inc(norm_out.sem, 1)

            with dve.Fori(0, nseq) as i:
                for k in range(1, 8, 2):
                    dve.wait_ge(*xT_ps(i, k + 1))
                    CP(xT[:, k, :], PS[:, 1, :]).then_inc(xT_v.sem, 1)
                dve.wait_ge(*xT_ps(i, 9))
                CP(h[:, :, 512:L], PS[:, 4, 0:2 * LT].rearrange("p (b l) -> p b l", b=2))
                dve.wait_ge(*tok_ps(i, 1))
                CP(h[:, :, 0:512], PS[:, 2:4, :]).then_inc(mean_src.sem, 1)
                dve.wait_ge(*mean_src(i, 1))
                centre(i, 0)
                dve.wait_ge(*norm_src(i, 1))
                norm(i, 0, hc, hn)
                dve.memset(z[:, :, 0:3], 0.0)
                link(i, dve.memset(vp[:, :, 0:PAD], 0.0))
                for m in range(6):
                    dve.wait_ge(*z_done(i, m + 1))
                    if m >= 2:
                        dve.wait_ge(*silu_done(i, m - 1))
                    link(i, TS(cv[:, m % 2, :], z[:, m, 0:L], convw[:, m, 0:1], None, ALU.mult))
                    for j in range(1, CONV):
                        last = STT(cv[:, m % 2, :], z[:, m, j:j + L], convw[:, m, j:j + 1], cv[:, m % 2, :],
                                   ALU.mult, ALU.add)
                        if j < CONV - 1:
                            link(i, last)
                    last.then_inc(conv_done.sem, 1)
                dve.wait_ge(*l2_sd(i, 1))
                link(i, dve.reciprocal(sq4, sq4))
                TT(qk, qk, sq4, ALU.mult).then_inc(qk_done.sem, 1)
                dve.wait_ge(*conv_done(i, 6))

                taps = [(f, j, b) for j in range(FIRS[2]) for f in range(3) if j < FIRS[f] for b in range(KB)]
                at_tap = {}
                done = [0]

                def filters(n):
                    for f, j, b in taps[done[0]:done[0] + n]:
                        src = vp[:, b, PAD - j:PAD - j + L]
                        w = firw[:, b, sum(FIRS[:f]) + FIRS[f] - 1 - j:sum(FIRS[:f]) + FIRS[f] - j]
                        if j == 0:
                            ins = TS(fir[:, f, b, :], src, w, None, ALU.mult)
                        else:
                            dve.wait_ge(*fir_step(i, at_tap[f, b]))
                            ins = STT(fir[:, f, b, :], src, w, fir[:, f, b, :], ALU.mult, ALU.add)
                        ins.then_inc(fir_step.sem, 1)
                        done[0] += 1
                        at_tap[f, b] = done[0]

                dve.wait_ge(*silu_done(i, 6))
                dve.wait_ge(*beta_done(i, 1))
                for t in range(T):
                    n = NT[t]
                    bt = beta[0:n, t, :]
                    bb = bt.rearrange("p (h a) -> p h a", a=1).to_broadcast([n, GH, GD])
                    dve.wait_ge(*G_ps(i, t + 1))
                    for hh in range(GH):
                        last = STT(X[0:n, hh, 0:n], PS[0:n, 2 + hh % 2, P * (hh // 2):P * (hh // 2) + n], bt[:, hh:hh + 1],
                                   K["strict"][0:n, 0:n], ALU.mult, ALU.mult)
                    last.then_inc(M_done.sem, 1)
                    dve.wait_ge(*at_ps(i, t + 1))
                    for q in range(2):
                        last = TT(atT[0:n, q::2, 0:n], PS[0:n, 5 + q, 0:C].rearrange("p (h n) -> p h n", h=2)[:, :, 0:n],
                                  K["upper"][0:n, 0:n].rearrange("p (a n) -> p a n", a=1).to_broadcast([n, 2, n]),
                                  ALU.mult)
                    last.then_inc(at_done.sem, 1)
                    dve.wait_ge(*kv_tok(i, t + 1))
                    TT(kbt[0:n, :].rearrange("p (h d) -> p h d", h=GH),
                       ktok[0:n, t, :].rearrange("p (h d) -> p h d", h=GH), bb, ALU.mult)
                    TT(vbt[0:n, :].rearrange("p (h d) -> p h d", h=GH),
                       F[0:n, t, 4, :].rearrange("p (h d) -> p h d", h=GH), bb, ALU.mult).then_inc(kvb_done.sem, 1)
                    dve.wait_ge(*MT_done(i, t + 1))
                    TT(R[0:n, :, 0:n], XT[0:n, :, 0:n],
                       ident[0:n, 0:n].rearrange("p (a n) -> p a n", a=1).to_broadcast([n, GH, n]),
                       ALU.add).then_inc(R_done.sem, 1)
                    for lv in range(4):
                        dve.wait_ge(*sq_ps(i, 4 * t + lv + 1))
                        CP(X[0:n, :, 0:n], PS[0:n, 4, :].rearrange("p (h n) -> p h n", h=GH)[:, :, 0:n]
                           ).then_inc(X_done.sem, 1)
                        filters(2)
                        dve.wait_ge(*R_ps(i, 4 * t + lv + 1))
                        dve.wait_ge(*R_done(i, 5 * t + lv + 1))
                        TT(R[0:n, :, 0:n], R[0:n, :, 0:n],
                           PS[0:n, 6, :].rearrange("p (h n) -> p h n", h=GH)[:, :, 0:n],
                           ALU.add).then_inc(R_done.sem, 1)
                    filters(4)
                    for j in range(n // CH):
                        c = 4 * t + j
                        rows = slice(CH * j, CH * j + CH)
                        dve.wait_ge(*w_ps(i, c + 1))
                        TT(u[rows, t, :], u[rows, t, :], PS[rows, 4, 0:C], ALU.subtract).then_inc(ua_done.sem, 1)
                        filters(3)
                filters(NFIR)
                assert done[0] == NFIR
                st4 = st.rearrange("p (g s h) -> p g s h", s=3, h=4)
                for t in range(T):
                    n = NT[t]
                    dve.wait_ge(*f_tok(i, t + 1))
                    f3 = F[0:n, t, :, :].rearrange("p k (h d) -> p (k h) d", h=GH)
                    s4 = st[0:n, 60 * t:60 * t + 60].rearrange("p (k s h) -> p k s h", s=3, h=4)
                    f4 = F[0:n, t, :, :].rearrange("p k (h d) -> p k h d", h=GH)
                    dve.wait_ge(*o_done(i, t + 1))
                    RED(s4[:, :, 0, :], f4, AX.X, ALU.add)
                    RED(s4[:, :, 2, :], f4, AX.X, ALU.max, apply_absolute_value=True)
                    dve.wait_ge(*f_sq(i, t + 1))
                    RED(ms[0:n, 20 * t:20 * t + 20], fsq[0:n, :].rearrange("p (g d) -> p g d", d=GD), AX.X,
                        ALU.add).then_inc(f_used.sem, 1)
                dve.wait_ge(*f_used(i, T))
                TS(st4[:, :, 0, :], st4[:, :, 0, :], 1.0 / GD, None, ALU.mult)
                TS(ms, ms, 1.0 / GD, 1e-8, ALU.mult, ALU.max).then_inc(rms_in.sem, 1)
                dve.wait_ge(*g2_ps(i, 1))
                for n, s in ((P, slice(0, 80)), (LT, slice(80, 100))):
                    g = (s.stop - s.start) // 20
                    last = TT(lg[0:n, s].rearrange("p (t k) -> p t k", t=g),
                              PS[0:n, 6, s].rearrange("p (t k) -> p t k", t=g),
                              gk[0:n, 0:20].rearrange("p (a k) -> p a k", a=1).to_broadcast([n, g, 20]), ALU.add)
                link(i, last)
                lg3 = lg.rearrange("p (t k) -> p t k", t=T)
                lg5 = lg.rearrange("p (g k) -> p g k", k=5)
                gw3 = gw.rearrange("p (t k) -> p t k", t=T)
                gw5 = gw.rearrange("p (g k) -> p g k", k=5)

                def over_tiles(v):
                    return v.rearrange("p (a k) -> p a k", a=1).to_broadcast([P, T, 20])

                def over_five(v):
                    return v.rearrange("p (g a) -> p g a", a=1).to_broadcast([P, 20, 5])

                link(i, TT(lg3, lg3, over_tiles(gk[:, 20:40]), ALU.mult))
                link(i, RED(m20, lg5, AX.X, ALU.max))
                TT(lg5, lg5, over_five(m20), ALU.subtract).then_inc(lg_in.sem, 1)
                dve.wait_ge(*lg_exp(i, 1))
                link(i, RED(s20, lg5, AX.X, ALU.add))
                link(i, dve.reciprocal(s20, s20))
                link(i, TT(gw5, lg5, over_five(s20), ALU.mult))
                link(i, TT(gw3, gw3, over_tiles(gk[:, 40:60]), ALU.mult))
                link(i, TT(gw3, gw3, over_tiles(gfloor[:, :]), ALU.add))
                gw4 = gw.rearrange("p (t h k) -> p t k h", t=T, h=GH)
                for t in range(T):
                    n = NT[t]
                    for k in range(5):
                        f3 = F[0:n, t, k, :].rearrange("p (h d) -> p h d", h=GH)
                        wb = gw[0:n, 20 * t:20 * t + 20].rearrange("p (h k a) -> p h k a", h=GH, a=1)[:, :, k, :]
                        last = TT(f3, f3, wb.to_broadcast([n, GH, GD]), ALU.mult)
                    link(i, last)
                    last = RED(o[0:n, t, :], F[0:n, t, :, :].rearrange("p k c -> p c k"), AX.X, ALU.add)
                link(i, last)
                o3 = o.rearrange("p t (h d) -> p (t h) d", h=GH)
                osq = view(asq4, T * C, "p (g d) -> p g d", d=GD)
                link(i, TT(osq, o3, o3, ALU.mult))
                link(i, RED(m20, osq, AX.X, ALU.add))
                TS(m20, m20, 1.0 / GD, None, ALU.mult).then_inc(oss.sem, 1)
                dve.wait_ge(*oss_sd(i, 1))
                link(i, dve.reciprocal(s20, s20))
                link(i, TT(o3, o3, s20.rearrange("p (g a) -> p g a", a=1).to_broadcast([P, 20, GD]), ALU.mult))
                TT(o3, o3, Wt["onorm"][:, :].rearrange("p (a d) -> p a d", a=1).to_broadcast([P, 20, GD]),
                   ALU.mult).then_inc(on_done.sem, 1)
                dve.wait_ge(*ow_ps(i, 1))
                for m in range(KB):
                    last = TT(halves(h[:, m, :]), halves(h[:, m, :]), pair(2 * m), ALU.add)
                last.then_inc(mean_src.sem, 1)
                dve.wait_ge(*mean_src(i, 2))
                centre(i, 1)
                dve.wait_ge(*norm_src(i, 2))
                norm(i, 1, hc, hn)
                dve.wait_ge(*norm_out(i, 2))
                dve.nop().then_inc(norm_src.sem, 1)
                norm(i, 2, hn, x1, Wt["ln1"])
                dve.wait_ge(*cks_ps(i, 1))
                dve.wait_ge(*ck_done(i, 1))
                TT(ckr[0:AD, :], ck[0:AD, :], K["cos"][0:AD, :], ALU.mult)
                link(i, TT(halves(qrot[0:AD, :]), pair(4, AD), halves(K["sin"][0:AD, :]), ALU.mult))
                TT(ckr[0:AD, :], ckr[0:AD, :], qrot[0:AD, :], ALU.add).then_inc(ckr_done.sem, 1)
                for m in range(QB):
                    dve.wait_ge(*qs_ps(i, m + 1))
                    TT(qT[:, m, :], qraw[:, m % 2, :], K["cos"], ALU.mult)
                    if m:
                        dve.wait_ge(*qT_done(i, m))
                    link(i, TT(halves(qrot), pair(4 + 2 * (m % 2)), halves(K["sin"]), ALU.mult))
                    TT(qT[:, m, :], qT[:, m, :], qrot, ALU.add).then_inc(qT_done.sem, 1)
                N = T * AH

                def top(n):
                    t, hh = n // AH, n % AH
                    rows, kk, bank = NT[t], P * t + NT[t], 2 * (n % 2)
                    flat = PS[0:rows, bank:bank + 2, :].rearrange("p a c -> p (a c)")
                    dve.wait_ge(*s_ps(i, n + 1))
                    if hh == 0 and t >= 2:
                        dve.wait_ge(*exp_done(i, n - AH))
                    link(i, TT(flat[:, P * t:kk], flat[:, P * t:kk], causal[0:rows, 0:rows], ALU.min))
                    RED(nmax[0:rows, t % 2, hh:hh + 1], flat[:, 0:kk], AX.X, ALU.max, negate=True).then_inc(max_done.sem, 1)

                def copy_probs(n):
                    t, hh = n // AH, n % AH
                    dve.wait_ge(*pT_ps(i, n + 1))
                    flat = PS[:, 4:6, :].rearrange("p a c -> p (a c)")
                    if t < 4:
                        CP(prT[:, n % 2, 0:P * (t + 1)], flat[:, 0:P * (t + 1)]).then_inc(pT_done.sem, 1)
                    else:
                        CP(prT[:, n % 2, 0:512].rearrange("p (k q) -> p k q", k=4)[:, :, 0:LT],
                           flat[:, 0:512].rearrange("p (k q) -> p k q", k=4)[:, :, 0:LT])
                        CP(prT[0:LT, n % 2, 512:512 + LT], flat[0:LT, 512:512 + LT]).then_inc(pT_done.sem, 1)

                def over_sums(t):
                    n = NT[t]
                    dve.wait_ge(*y_ps(i, t + 1))
                    if t:
                        dve.wait_ge(*yT_ps(i, t))
                    link(i, dve.reciprocal(rinv[0:n, :], rsum[0:n, t % 2, :]))
                    TT(yn[0:n], PS[0:n, 6, :].rearrange("p (h d) -> p h d", h=AH),
                       rinv[0:n, :].rearrange("p (h a) -> p h a", a=1).to_broadcast([n, AH, NOPE]),
                       ALU.mult).then_inc(yn_done.sem, 1)

                top(0)
                for n in range(N):
                    if n + 1 < N:
                        top(n + 1)
                    copy_probs(n)
                    if n % AH == 0 and n:
                        over_sums(n // AH - 1)
                over_sums(T - 1)
                dve.wait_ge(*wo_ps(i, 1))
                for m in range(KB):
                    last = TT(halves(x2[:, m, :]), halves(hn[:, m, :]), pair(2 * m), ALU.add)
                last.then_inc(norm_src.sem, 1)
                dve.wait_ge(*norm_src(i, 4))
                TT(h, h, x2, ALU.add)
                norm(i, 3, x2, xn, Wt["ln2"])
                dve.wait_ge(*gl_ps(i, 1))
                TT(gl[:, 0:4, :], PS[:, 6, 0:4 * E].rearrange("p (t e) -> p t e", t=4),
                   Wt["ebias"][:, :].rearrange("p (a e) -> p a e", a=1).to_broadcast([P, 4, E]), ALU.add)
                link(i, TT(gl[0:LT, 4, :], PS[0:LT, 6, 4 * E:5 * E], Wt["ebias"][0:LT, :], ALU.add))
                link(i, RED(m5, gl, AX.X, ALU.max))
                TT(gl, gl, m5.rearrange("p (t a) -> p t a", a=1).to_broadcast([P, T, E]),
                   ALU.subtract).then_inc(gl_in.sem, 1)
                dve.wait_ge(*gl_exp(i, 1))
                for t in range(T):
                    mine = gl[:, t, :].rearrange("p (e a) -> p e a", a=1).to_broadcast([P, E, E])
                    other = gl[:, t, :].rearrange("p (a e) -> p a e", a=1).to_broadcast([P, E, E])
                    TT(cmpA, other, mine, ALU.is_gt)
                    link(i, TT(cmpB, other, mine, ALU.is_equal))
                    link(i, TT(cmpB, cmpB, K["before"].rearrange("p (e j) -> p e j", e=E), ALU.mult))
                    link(i, TT(cmpA, cmpA, cmpB, ALU.add))
                    link(i, RED(rank[:, t, :], cmpA, AX.X, ALU.add))
                link(i, TS(rank, rank, 1.5, None, ALU.is_lt))
                link(i, TT(gl, gl, rank, ALU.mult))
                link(i, RED(s5, gl, AX.X, ALU.add))
                link(i, dve.reciprocal(s5, s5))
                TT(gl, gl, s5.rearrange("p (t a) -> p t a", a=1).to_broadcast([P, T, E]),
                   ALU.mult).then_inc(comb_done.sem, 1)
                for n in range(2 * NE):
                    a, e = n // NE, n % NE
                    dve.wait_ge(*gs_done(i, n + 1))
                    if n >= 2:
                        dve.wait_ge(*dn_ps(i, n - 1))
                    if e < E:
                        dve.wait_ge(*cb_done(i, E))
                        link(i, TT(gu[:, n % 2, :], gs[:, n % 2, :], PS[:, 2 * (n % 2) + 1, 0:HALF], ALU.mult))
                        TT(gu[:, n % 2, :], gu[:, n % 2, :], cb[:, e, cols(a)], ALU.mult).then_inc(gu_done.sem, 1)
                    else:
                        TT(gu[:, n % 2, :], gs[:, n % 2, :], PS[:, 2 * (n % 2) + 1, 0:HALF],
                           ALU.mult).then_inc(gu_done.sem, 1)
                for a in range(2):
                    dve.wait_ge(*dn_ps(i, NE * (a + 1)))
                    TT(h[:, :, cols(a)], h[:, :, cols(a)], PS[:, 4 + 2 * a:6 + 2 * a, 0:HALF],
                       ALU.add).then_inc(res_done.sem, 1)
                assert steps[0] == VSTEPS, ("VSTEPS", steps[0])


def kernel(**inputs):
    import numpy as _np
    import concourse.bacc as _bacc
    from concourse import mybir as _mybir
    from concourse.bass_utils import run_bass_kernel_spmd as _run

    a = {k: _np.asarray(v) for k, v in inputs.items()}

    def blocks(w, p=P):
        return _np.ascontiguousarray(w.reshape(-1, p, w.shape[1]).transpose(1, 0, 2).reshape(p, -1))

    def everywhere(v):
        return _np.ascontiguousarray(_np.broadcast_to(v.reshape(1, -1), (P, v.size)))

    w = {}
    w["wqkv"] = blocks(_np.concatenate([a[f"L0_attn_{n}_w"].T for n in "qkv"], axis=1))
    w["bw"] = blocks(a["L0_attn_b_w"].T)
    w["convw"] = blocks(_np.concatenate([a[f"L0_attn_conv{n}_w"] for n in "qkv"], axis=0))
    w["firw"] = blocks(_np.concatenate([a["L0_attn_" + n].reshape(C, -1) for n in ("fir_s", "fir_l", "fir_wd")], axis=1))
    g1 = _np.zeros((3 * P, 512), _np.float32)
    g1[:316] = a["L0_attn_g1_w"].T
    w["g1"] = blocks(g1)
    w["g1b"] = _np.ascontiguousarray(a["L0_attn_g1_b"].reshape(4, P).T)
    w["g2"] = blocks(a["L0_attn_g2_w"].T)
    w["g2b"] = everywhere(a["L0_attn_g2_b"])
    w["vbias"] = everywhere(a["L0_attn_value_bias"])
    w["ltemp"] = everywhere(a["L0_attn_log_temp"])
    w["floor"] = everywhere(a["L0_attn_floor_logit"])
    w["onorm"] = everywhere(a["L0_attn_onorm_w"])
    w["ow"] = blocks(a["L0_attn_o_w"].T)
    w["ln1"] = _np.ascontiguousarray(a["L0_ffn_w_ln1"].reshape(KB, P).T)
    w["ln2"] = _np.ascontiguousarray(a["L0_ffn_w_ln2"].reshape(KB, P).T)
    w["wq"] = blocks(a["L0_ffn_Wq"])
    w["wkva"] = blocks(a["L0_ffn_Wkva"])
    w["wkvb"] = _np.ascontiguousarray(a["L0_ffn_Wkvb"])
    kpad = _np.zeros((AD, AH, AD), _np.float32)
    kpad[:32, :, :NOPE] = a["L0_ffn_Wkvb"].reshape(32, AH, NOPE)
    kpad[32:, :, NOPE:] = _np.broadcast_to(_np.eye(32, dtype=_np.float32)[:, None, :], (32, AH, 32))
    w["kpad"] = kpad.reshape(AD, AH * AD)
    w["wo"] = blocks(_np.ascontiguousarray(a["L0_ffn_Wo"].reshape(AH, AD, C)[:, :NOPE]).reshape(AH * NOPE, C))
    w["wgate"] = blocks(a["L0_ffn_Wgate"])
    w["ebias"] = everywhere(a["L0_ffn_expert_bias"])
    for n, m in (("wg", "Wg"), ("wu", "Wu")):
        both = _np.concatenate([a["L0_ffn_" + m], a["L0_ffn_s" + m]], axis=0)
        w[n] = _np.ascontiguousarray(both.reshape(NE, KB, P, EI).transpose(2, 0, 1, 3).reshape(P, -1))
    both = _np.concatenate([a["L0_ffn_Wd"], a["L0_ffn_sWd"]], axis=0)
    w["wd"] = _np.ascontiguousarray(both.transpose(1, 0, 2).reshape(P, -1))

    nc = _bacc.Bacc("TRN2", target_bir_lowering=False, num_devices=1)
    arrays = {}

    def put(name, v):
        arrays[name] = v
        return nc.dram_tensor(name, v.shape, _mybir.dt.from_np(v.dtype), kind="ExternalInput").ap()

    x = put("x", _np.ascontiguousarray(a["x"]))
    txt = put("txt", _np.ascontiguousarray(a["txt"]))
    consts = put("consts", constants())
    tokw = put("tokw", everywhere(_np.ascontiguousarray(a["L0_tok_weight"].T)))
    tokws = put("tokws", _np.ascontiguousarray(a["L0_tok_weighted_sum"].T))
    weights = {n: put("w_" + n + "_dram", v) for n, v in w.items()}
    out = nc.dram_tensor("out", (B, L, C), F32, kind="ExternalOutput").ap()
    build(nc, x, txt, consts, tokw, tokws, weights, out)
    r = _run(nc, [arrays], core_ids=[0])
    return r.results[0]["out"]
```

```python
from contextlib import ExitStack

import numpy as np

import concourse.bass as bass
from concourse import mybir

F32 = mybir.dt.float32
ALU = mybir.AluOpType
ACT = mybir.ActivationFunctionType
AX = mybir.AxisListType

P = 128
B = 16
LI = 512
LT = 32
L = LI + LT
C = 256
KB = C // P
HALF = L // 2
D1 = 4
T = 5
NT = [128, 128, 128, 128, 32]
GH, GD = 4, 64
CH = 32
NCHUNK = L // CH
CONV = 4
FIRS = (3, 31, 64)
PAD = FIRS[2] - 1
WP = 38
NWIDE = KB * WP
VTAPS = [(f, j, b) for r in range(FIRS[2]) for f in range(3) for b in range(KB)
         for j in [r + (WP if f == 2 else 0)] if j < FIRS[f]]
NFIR = len(VTAPS) + KB
AH, AD, NOPE = 16, 64, 32
QB = AH // 2
E, EI = 8, 128
NE = E + 1
BIG = 3.0e38
STEPS = [(t, h) for t in range(T - 1) for h in range(AH)] + [(T - 1, s) for s in range(4)]
NSTEP = len(STEPS)


def place(h):
    return (h % 8) // 2, 2 * (h // 8) + h % 2


def head_at(b, s):
    return 8 * (s // 2) + 2 * b + s % 2


QKV = (4, 5, 0, 1, 2, 3)
WIDE_AT = (20, 24, 28)


def wide_after(part):
    return WIDE_AT[2] + (part + 1) * (NWIDE - WIDE_AT[2]) // len(DELTA)


def delta_parts():
    parts = [("inverse", 0, k) for k in range(8)]
    for t in range(T):
        for k in range(max(2 * (NT[t] // CH), 8 if t + 1 < T else 0)):
            if t + 1 < T and k < 8:
                parts.append(("inverse", t + 1, k))
            if k < 2 * (NT[t] // CH):
                parts.append(("chunk", t, k))
    return parts


DELTA = delta_parts()


ARENA = 26100
VSTEPS = 146


class Signal:

    def __init__(self, sem, per, start=0, stage=0):
        self.sem, self.per, self.start, self.stage = sem, per, start, stage

    def __call__(self, i, k):
        return self.sem, (i + self.stage) * self.per + (k + self.start - self.stage * self.per)


CONSTS = dict(ident=P, mean=P, heads=P, swap=P, causal=P, strict=P, upper=P, cos=L, sin=L, causal4=LT, before=64,
              eps5=1, eps6=1)


def constants():
    out = {}
    r = np.arange(P)
    out["ident"] = np.eye(P)
    out["mean"] = np.full((P, P), 1.0 / C)
    out["heads"] = (r[:, None] // GD == r[None, :] // GD) * 1.0
    swap = np.zeros((P, P))
    for m in range(P):
        if m % AD >= NOPE:
            if m % 2 == 0:
                swap[m + 1, m] = -1.0
            else:
                swap[m - 1, m] = 1.0
    out["swap"] = swap
    out["causal"] = np.where(r[None, :] <= r[:, None], BIG, -BIG)
    same = r[:, None] // CH == r[None, :] // CH
    out["strict"] = np.where(same & (r[None, :] < r[:, None]), -1.0, 0.0)
    out["upper"] = np.where(same & (r[None, :] >= r[:, None]), 1.0, 0.0)
    width = AD - NOPE
    freqs = (1.0 / np.float32(100000.0) ** (np.arange(0, width, 2, dtype=np.float32) / np.float32(width))).astype(np.float32)
    ang = np.outer(np.arange(L, dtype=np.float32), freqs).astype(np.float32)
    cos, sin = np.ones((P, L)), np.zeros((P, L))
    for m in range(P):
        if m % AD >= NOPE:
            pair = (m % AD - NOPE) // 2
            cos[m], sin[m] = np.cos(ang[:, pair]), np.sin(ang[:, pair])
    out["cos"], out["sin"] = cos, sin
    out["causal4"] = np.where(r[None, :LT] <= r[:, None] % LT, BIG, -BIG)
    e = np.arange(E)
    out["before"] = np.broadcast_to((e[None, :] < e[:, None]).reshape(1, 64), (P, 64)) * 1.0
    out["eps5"] = np.full((P, 1), 1e-5)
    out["eps6"] = np.full((P, 1), 1e-6)
    return np.ascontiguousarray(np.concatenate([out[k] for k in CONSTS], axis=1).astype(np.float32))


WEIGHTS = dict(wqkv=(P, KB * 3 * C), bw=(P, KB * GH), convw=(P, 6 * CONV), firw=(P, KB * sum(FIRS)),
               g1=(P, 3 * 512), g1b=(P, 4), g2=(P, 4 * 20), g2b=(P, 20), vbias=(P, GH), ltemp=(P, GH),
               floor=(P, GH), onorm=(P, GD), ow=(P, KB * C), ln1=(P, KB), ln2=(P, KB), wq=(P, KB * AH * AD),
               wkva=(P, KB * P), wo=(P, 4 * C), wgate=(P, KB * E),
               ebias=(P, E), wg=(P, NE * KB * EI), wu=(P, NE * KB * EI), wd=(P, NE * C))


def build(nc, x, txt, consts, tokw, tokws, wqn, wlat, weights, out, nseq=B):
    ctx = ExitStack()
    with ctx:
        def sb(name, words, parts=P):
            return ctx.enter_context(nc.sbuf_tensor(name, [parts, words], F32))

        stage = [0]

        def signal(name, per, start=0):
            return Signal(ctx.enter_context(nc.semaphore(name)), per, start, stage[0])

        PS = ctx.enter_context(nc.psum_tensor("PS", [P, 8, 512], F32))
        K = {}
        cst = sb("cst", sum(CONSTS.values()))
        at = 0
        for name, n in CONSTS.items():
            K[name] = cst[:, at:at + n]
            at += n
        Wt = {name: sb("w_" + name, n, parts) for name, (parts, n) in WEIGHTS.items()}
        tokwT = sb("tokwT", 8 * C)[:, :].rearrange("p (k o) -> p k o", k=8)
        h = sb("h", KB * L)[:, :].rearrange("p (b l) -> p b l", b=KB)
        hn = sb("hn", KB * L)[:, :].rearrange("p (b l) -> p b l", b=KB)
        hcsq = sb("hcsq", 2 * KB * L)
        hc = hcsq[:, 0:KB * L].rearrange("p (b l) -> p b l", b=KB)
        sq = hcsq[:, KB * L:2 * KB * L].rearrange("p (b l) -> p b l", b=KB)
        yT = hcsq[:, :].rearrange("p (b l) -> p b l", b=4)
        rt = sb("rt", T)[:, :]
        gk = sb("gk", 3 * 20)
        gfloor = sb("gfloor", 20)
        kz = sb("kz", 2 * L)[:, :].rearrange("p (b l) -> p b l", b=2)
        diag = sb("diag", 8 * P)[:, :].rearrange("p (b n) -> p b n", b=8)
        scrap = sb("scrap", 16)[:, :]

        arena = sb("arena", ARENA)
        used = [0]

        def take(words, again=None):
            start = used[0] if again is None else again
            if again is None:
                used[0] += words
            assert start + words <= ARENA, (start, words)
            return start

        def view(start, words, pattern=None, parts=P, **kw):
            v = arena[0:parts, start:start + words]
            return v.rearrange(pattern, **kw) if pattern else v

        aF = take(T * 5 * C)
        xs = view(aF, 4 * 1024, "p (t i d) -> p t i d", t=4, d=D1)
        xt = view(aF + 4096, C, parts=LT)
        F = view(aF, T * 5 * C, "p (t k c) -> p t k c", t=T, k=5)
        a0 = take(4096)
        xT = view(a0, 8 * LI, "p (k l) -> p k l", k=8)
        z = view(a0, 6 * (L + 3), "p (b l) -> p b l", b=6)
        fir = view(a0, 3 * KB * L, "p (f b l) -> p f b l", f=3, b=KB)
        acv = take(KB * L)
        cv = view(acv, KB * L, "p (b l) -> p b l", b=KB)
        oT = cv
        aqk = take(4 * L)
        qk = view(aqk, 4 * L, "p (b l) -> p b l", b=4)
        asq4 = take(4 * L)
        sq4 = view(asq4, 4 * L, "p (b l) -> p b l", b=4)
        rlx = view(asq4, 4 * 512, "p (t c) -> p t c", t=4)
        fsq = view(asq4, 5 * C)
        hd = sq4
        avp = take(KB * (L + PAD))
        vp = view(avp, KB * (L + PAD), "p (b l) -> p b l", b=KB)
        ktok = view(take(T * C), T * C, "p (t c) -> p t c", t=T)
        ot = ktok
        au = take(T * C)
        u = view(au, T * C, "p (t c) -> p t c", t=T)
        o = u
        akbt = take(2 * C)
        kbt = view(akbt, C)
        vbt = view(akbt + C, C)
        rly = view(akbt, 512)
        X = view(take(512), 512, "p (h n) -> p h n", h=GH)
        XT = view(take(512), 512, "p (h n) -> p h n", h=GH)
        R = view(take(512), 512, "p (h n) -> p h n", h=GH)
        atT = view(take(1024), 1024, "p (b h n) -> p b h n", b=2, h=GH)
        wT = view(take(2 * L), 2 * L, "p (b l) -> p b l", b=2)
        Sb = view(take(256), 256, "p (b n) -> p b n", b=2)
        st = view(take(T * 60), T * 60)
        ast = take(L)
        sT = view(ast, L, parts=60)
        beta = view(take(20), 20, "p (t h) -> p t h", t=T)
        ms = view(take(100), 100)
        lg = view(take(100), 100)
        gw = view(take(100), 100)
        m20 = view(take(20), 20)
        s20 = view(take(20), 20)
        rl = view(take(T * 8), T * 8)
        ngdn = used[0]
        used[0] = a0
        qT = view(take(QB * L), QB * L, "p (b l) -> p b l", b=QB)
        qlast = view(take(QB * LT), QB * LT)
        cb = qT
        vt = view(take(T * NOPE), T * NOPE, "p (t c) -> p t c", t=T)
        x1 = view(take(KB * L), KB * L, "p (b l) -> p b l", b=KB)
        xn = x1
        x2 = view(take(KB * L), KB * L, "p (b l) -> p b l", b=KB)
        qraw = view(take(2 * L), 2 * L, "p (b l) -> p b l", b=2)
        qrot = view(take(L), L)
        ck = qraw[:, 0, :]
        ckr = view(take(L), L)
        pr = view(take(3 * L), 3 * L, "p (b l) -> p b l", b=3)
        prT = view(take(2 * 640), 1280, "p (b l) -> p b l", b=2)
        yn = view(take(512), 512, "p (h d) -> p h d", h=AH)
        rsum = view(take(2 * AH), 2 * AH, "p (b h) -> p b h", b=2)
        rinv = view(take(AH), AH)
        nmax = view(take(2 * AH), 2 * AH, "p (b h) -> p b h", b=2)
        gl = view(take(T * E), T * E, "p (t e) -> p t e", t=T)
        rank = view(take(T * E), T * E, "p (t e) -> p t e", t=T)
        m5 = view(take(T), T)
        s5 = view(take(T), T)
        cmpA = view(take(T * 64), T * 64, "p (t e j) -> p t e j", t=T, e=E)
        cmpB = view(take(T * 64), T * 64, "p (t e j) -> p t e j", t=T, e=E)
        gs = view(take(L), L, "p (b l) -> p b l", b=2)
        gu = view(take(L), L, "p (b l) -> p b l", b=2)
        used[0] = max(used[0], ngdn)

        tokws_sb = view(a0, KB * C, "p (b o) -> p b o", b=KB)
        tokw_sb = view(a0 + KB * C, D1 * C, "p (d o) -> p d o", d=D1)
        wqn_sb = view(aF, 4 * C, "p (b c) -> p b c", b=4)
        wlat_sb = view(aF + 4 * C, 4 * P, "p (b l) -> p b l", b=4)

        ident, causal = K["ident"], K["causal"]
        wqkv = Wt["wqkv"][:, :].rearrange("p (b m) -> p b m", b=KB)
        bw = Wt["bw"][:, :].rearrange("p (b m) -> p b m", b=KB)
        convw = Wt["convw"][:, :].rearrange("p (b j) -> p b j", b=6)
        firw = Wt["firw"][:, :].rearrange("p (b j) -> p b j", b=KB)
        g1 = Wt["g1"][:, :].rearrange("p (b m) -> p b m", b=3)
        g2 = Wt["g2"][:, :].rearrange("p (b m) -> p b m", b=4)
        ow = Wt["ow"][:, :].rearrange("p (b m) -> p b m", b=KB)
        wq = Wt["wq"][:, :].rearrange("p (b m) -> p b m", b=KB)
        wkva = Wt["wkva"][:, :].rearrange("p (b m) -> p b m", b=KB)
        wo = Wt["wo"][:, :].rearrange("p (b m) -> p b m", b=4)
        wgate = Wt["wgate"][:, :].rearrange("p (b m) -> p b m", b=KB)
        wg = Wt["wg"][:, :].rearrange("p (e b m) -> p e b m", e=NE, b=KB)
        wu = Wt["wu"][:, :].rearrange("p (e b m) -> p e b m", e=NE, b=KB)
        wd = Wt["wd"][:, :].rearrange("p (e m) -> p e m", e=NE)

        def pair(bank, parts=P):
            return PS[0:parts, bank:bank + 2, 0:HALF]

        def halves(v):
            return v.rearrange("p (a c) -> p a c", a=2)

        def cols(a):
            return slice(a * HALF, (a + 1) * HALF)

        def tok(t):
            return slice(P * t, P * t + NT[t])

        loaded = signal("loaded", 0)
        setup = signal("setup", 0)
        setup_pe = signal("setup_pe", 0)
        setup_act = signal("setup_act", 0)
        setup_dve = signal("setup_dve", 0)
        x_in = signal("x_in", 32)
        y_out = signal("y_out", 32, start=16)
        v_step = signal("v_step", VSTEPS)
        fir_step = signal("fir_step", NFIR)
        diag_done = signal("diag_done", NWIDE)
        wide_ps = signal("wide_ps", NWIDE)
        wide_out = signal("wide_out", KB)
        xT_ps = signal("xT_ps", 9)
        xT_a = signal("xT_a", 4)
        xT_v = signal("xT_v", 4)
        tok_ps = signal("tok_ps", 1)
        mean_src = signal("mean_src", 2)
        mean_ps = signal("mean_ps", 2)
        norm_src = signal("norm_src", 4)
        norm_sq = signal("norm_sq", 4)
        norm_ps = signal("norm_ps", 4)
        norm_sd = signal("norm_sd", 4)
        norm_rc = signal("norm_rc", 4)
        norm_bc = signal("norm_bc", 4)
        norm_out = signal("norm_out", 4)
        qkv_ps = signal("qkv_ps", 6)
        z_done = signal("z_done", 6)
        conv_done = signal("conv_done", 6)
        silu_done = signal("silu_done", 6)
        beta_ps = signal("beta_ps", 1)
        beta_done = signal("beta_done", 1)
        l2_sq = signal("l2_sq", 1)
        l2_ps = signal("l2_ps", 1)
        l2_sd = signal("l2_sd", 1)
        l2_rc = signal("l2_rc", 1)
        l2_bc = signal("l2_bc", 1)
        qk_done = signal("qk_done", 1)
        stage[0] = 1
        kv_ps = signal("kv_ps", T)
        kv_tok = signal("kv_tok", T)
        kvb_done = signal("kvb_done", T)
        G_ps = signal("G_ps", T)
        M_done = signal("M_done", T)
        MT_ps = signal("MT_ps", T)
        MT_done = signal("MT_done", T)
        R_done = signal("R_done", 5 * T)
        sq_ps = signal("sq_ps", 4 * T)
        X_done = signal("X_done", 4 * T)
        XT_done = signal("XT_done", 3 * T)
        R_ps = signal("R_ps", 4 * T)
        uw_ps = signal("uw_ps", T)
        uw_done = signal("uw_done", T)
        at_ps = signal("at_ps", T)
        at_done = signal("at_done", T)
        w_ps = signal("w_ps", NCHUNK)
        ua_done = signal("ua_done", NCHUNK)
        S_ps = signal("S_ps", NCHUNK)
        S_done = signal("S_done", NCHUNK + 1)
        o_ps = signal("o_ps", T)
        o_done = signal("o_done", T)
        stage[0] = 2
        f_ps = signal("f_ps", T)
        f_tok = signal("f_tok", T)
        f_sq = signal("f_sq", T)
        f_used = signal("f_used", T)
        rms_in = signal("rms_in", 1)
        st_done = signal("st_done", 1)
        st_ps = signal("st_ps", 1)
        sT_done = signal("sT_done", 1)
        g1_ps = signal("g1_ps", 4)
        hd_done = signal("hd_done", 4)
        g2_ps = signal("g2_ps", 1)
        lg_in = signal("lg_in", 1)
        lg_exp = signal("lg_exp", 1)
        oss = signal("oss", 1)
        oss_sd = signal("oss_sd", 1)
        on_done = signal("on_done", 1)
        oT_ps = signal("oT_ps", 1)
        oT_done = signal("oT_done", 1)
        ow_ps = signal("ow_ps", 1)
        stage[0] = 3
        ck_ps = signal("ck_ps", 1)
        ck_done = signal("ck_done", 1)
        cks_ps = signal("cks_ps", 1)
        ckr_done = signal("ckr_done", 1)
        vt_ps = signal("vt_ps", 1)
        vt_done = signal("vt_done", 1)
        q_ps = signal("q_ps", QB)
        q_done = signal("q_done", QB)
        qs_ps = signal("qs_ps", QB)
        qT_done = signal("qT_done", QB + 1)
        s_ps = signal("s_ps", NSTEP)
        max_done = signal("max_done", NSTEP)
        exp_done = signal("exp_done", NSTEP)
        pT_ps = signal("pT_ps", NSTEP)
        pT_a = signal("pT_a", NSTEP // 2)
        pT_v = signal("pT_v", NSTEP // 2)
        y_ps = signal("y_ps", T)
        yn_done = signal("yn_done", T)
        yT_ps = signal("yT_ps", T)
        yT_done = signal("yT_done", T)
        wo_ps = signal("wo_ps", 1)
        stage[0] = 4
        gl_ps = signal("gl_ps", 1)
        gl_in = signal("gl_in", 1)
        gl_exp = signal("gl_exp", 1)
        comb_done = signal("comb_done", 1)
        cb_ps = signal("cb_ps", E)
        cb_done = signal("cb_done", E)
        gu_ps = signal("gu_ps", 2 * NE)
        gs_done = signal("gs_done", 2 * NE)
        gu_done = signal("gu_done", 2 * NE)
        dn_ps = signal("dn_ps", 2 * NE)
        res_done = signal("res_done", 2)
        rT_ps = signal("rT_ps", T)
        rT_done = signal("rT_done", T, start=1)

        block = ctx.enter_context(nc.Block())
        nloads = len(WEIGHTS) + 5

        @block.sync
        def _(sp):
            for name in WEIGHTS:
                sp.dma_start(Wt[name][:, :], weights[name]).then_inc(loaded.sem, 16)
            sp.dma_start(cst[:, :], consts).then_inc(loaded.sem, 16)
            sp.dma_start(tokws_sb, tokws.rearrange("(b p) o -> p b o", p=P)).then_inc(loaded.sem, 16)
            sp.dma_start(tokw_sb, tokw.rearrange("p (d o) -> p d o", d=D1)).then_inc(loaded.sem, 16)
            sp.dma_start(wqn_sb.rearrange("p b c -> p (b c)"), wqn).then_inc(loaded.sem, 16)
            sp.dma_start(wlat_sb.rearrange("p b l -> p (b l)"), wlat).then_inc(loaded.sem, 16)
            sp.wait_ge(setup.sem, 2)

            def load(i):
                sp.dma_start(xs.rearrange("p t i d -> p t (i d)"),
                             x[bass.ds(i, 1)].rearrange("a (t p) i d -> p (a t) (i d)", p=P)).then_inc(x_in.sem, 16)
                sp.dma_start(xt, txt[bass.ds(i, 1)].rearrange("a t c -> (a t) c")).then_inc(x_in.sem, 16)

            def store(i):
                sp.wait_ge(*rT_done(i, T))
                sp.dma_start(out[bass.ds(i, 1), 0:LI].rearrange("a (t p) c -> p (a t) c", p=P),
                             ot[:, 0:4, :]).then_inc(y_out.sem, 16)
                sp.dma_start(out[bass.ds(i, 1), LI:L].rearrange("a t c -> (a t) c"),
                             ot[0:LT, 4, :]).then_inc(y_out.sem, 16)

            sp.sem_inc(y_out.sem, y_out.start)
            load(0)
            with sp.Fori(0, nseq - 1) as i:
                sp.wait_ge(*on_done(i, 1))
                load(i + 1)
                store(i)
            store(nseq - 1)
            sp.wait_ge(*y_out(nseq, 0))

        @block.tensor
        def _(pe):
            mm, tr = pe.matmul, pe.transpose
            pe.wait_ge(loaded.sem, 16 * nloads)
            for b in range(4):
                for kb in range(KB):
                    mm(PS[:, kb, P * b:P * b + P], wqn_sb[:, b, P * kb:P * kb + P], wlat_sb[:, b, :],
                       start=True, stop=True)
                last = mm(PS[:, 2 + b // 2, C * (b % 2):C * (b % 2) + C], wlat_sb[:, b, :], wo[:, b, :],
                          start=True, stop=True)
            last.then_inc(setup_pe.sem, 1)
            pe.wait_ge(setup.sem, 3)

            def small(yes=True):
                if yes:
                    pe.nop(nofuse=True)

            def norm(i, n, bank):
                pe.wait_ge(*norm_sq(i, n + 1))
                for t in range(T):
                    for b in range(KB):
                        last = mm(PS[0:NT[t], bank, t:t + 1], sq[:, b, tok(t)], K["mean"][:, 0:1],
                                  start=b == 0, stop=b == KB - 1)
                last.then_inc(norm_ps.sem, 1)
                pe.wait_ge(*norm_rc(i, n + 1))
                small()
                for t in range(T):
                    n_t = NT[t]
                    last = mm(PS[:, bank + 1 + t // 4, P * (t % 4):P * (t % 4) + n_t],
                              rt[0:n_t, t:t + 1].to_broadcast([n_t, P]), ident[0:n_t, 0:n_t], start=True, stop=True)
                last.then_inc(norm_bc.sem, 1)

            def mean(i, n):
                pe.wait_ge(*mean_src(i, n + 1))
                for a in range(2):
                    for b in range(KB):
                        last = mm(PS[:, a, 0:HALF], K["mean"], h[:, b, cols(a)], start=b == 0, stop=b == KB - 1)
                last.then_inc(mean_ps.sem, 1)

            with pe.Fori(0, nseq) as i:
                pe.wait_ge(*x_in(i, 32))
                pe.wait_ge(*rT_done(i, 0))
                for k in range(8):
                    d, b = k // KB, k % KB
                    if k >= 2:
                        pe.wait_ge(*(xT_v if k % 2 else xT_a)(i, k // 2))
                    for t in range(4):
                        last = tr(PS[:, k % 2, P * t:P * t + P], xs[:, t, P * b:P * b + P, d], ident)
                    last.then_inc(xT_ps.sem, 1)
                for b in range(KB):
                    last = tr(PS[:, 4, LT * b:LT * b + LT], xt[:, P * b:P * b + P], ident[0:LT, 0:LT])
                last.then_inc(xT_ps.sem, 1)
                pe.wait_ge(*xT_a(i, 4))
                pe.wait_ge(*xT_v(i, 4))
                for m in range(KB):
                    for k in range(8):
                        last = mm(PS[:, 2 + m, :], tokwT[:, k, P * m:P * m + P], xT[:, k, :], start=k == 0, stop=k == 7)
                last.then_inc(tok_ps.sem, 1)
                mean(i, 0)
                norm(i, 0, 2)
                pe.wait_ge(*norm_out(i, 1))
                for n, m in enumerate(QKV):
                    if n >= 2:
                        pe.wait_ge(*z_done(i, n - 1))
                    for a in range(2):
                        for b in range(KB):
                            last = mm(PS[:, 2 + 2 * (n % 2) + a, 0:HALF], wqkv[:, b, P * m:P * m + P],
                                      hn[:, b, cols(a)], start=b == 0, stop=b == KB - 1)
                    last.then_inc(qkv_ps.sem, 1)
                for t in range(T):
                    for b in range(KB):
                        last = mm(PS[0:NT[t], 6, GH * t:GH * t + GH], hn[:, b, tok(t)], bw[:, b, :],
                                  start=b == 0, stop=b == KB - 1)
                last.then_inc(beta_ps.sem, 1)
                pe.wait_ge(*silu_done(i, KB))
                done = [0]

                def wide(upto):
                    for w in range(done[0], upto):
                        b, tap = w // WP, w % WP
                        pe.wait_ge(*diag_done(i, w + 1))
                        if tap == 0 and b:
                            pe.wait_ge(*wide_out(i, b))
                        for a in range(2):
                            src = PAD - tap + HALF * a
                            last = mm(PS[:, a, 0:HALF], diag[:, w % 8, :], vp[:, b, src:src + HALF],
                                      start=tap == 0, stop=tap == WP - 1)
                        last.then_inc(wide_ps.sem, 1)
                    done[0] = max(done[0], upto)

                wide(WIDE_AT[0])
                pe.wait_ge(*l2_sq(i, 1))
                for t in range(T):
                    for m in range(4):
                        last = mm(PS[0:NT[t], 7, 8 * t + 2 * m:8 * t + 2 * m + 2], sq4[:, m, tok(t)],
                                  K["heads"][:, 0:P:GD], start=True, stop=True)
                last.then_inc(l2_ps.sem, 1)
                wide(WIDE_AT[1])
                pe.wait_ge(*l2_rc(i, 1))
                pe.wait_ge(*beta_done(i, 1))
                small()
                for t in range(T):
                    n = NT[t]
                    for m in range(4):
                        dst = PS[:, 2 + m, P * t:P * t + P] if t < 4 else PS[:, 6, LT * m:LT * m + LT]
                        one = rlx[:, t, P * m:P * m + P] if t < 4 else rly[0:LT, P * m:P * m + P]
                        last = mm(dst, one, ident[0:n, 0:n], start=True, stop=True)
                last.then_inc(l2_bc.sem, 1)
                wide(WIDE_AT[2])
                pe.wait_ge(*qk_done(i, 1))
                for t in range(T):
                    if t >= 2:
                        pe.wait_ge(*kv_tok(i, t - 1))
                    for b in range(KB):
                        tr(PS[0:NT[t], 2 + t % 2, P * b:P * b + P], qk[:, 2 + b, tok(t)], ident)
                        last = tr(PS[0:NT[t], 2 + t % 2, C + P * b:C + P * b + P],
                                  vp[:, b, PAD + P * t:PAD + P * t + NT[t]], ident)
                    last.then_inc(kv_ps.sem, 1)
                pe.wait_ge(*kv_tok(i, T))
                for part, (what, t, k) in enumerate(DELTA):
                    n = NT[t]
                    if what == "inverse":
                        if k == 0:
                            if t:
                                pe.wait_ge(*uw_done(i, t))
                            small(t == 4)
                            for hh in range(GH):
                                kh = qk[GD * (hh % 2):GD * (hh % 2) + GD, 2 + hh // 2, tok(t)]
                                last = mm(PS[0:n, 2 + hh % 2, P * (hh // 2):P * (hh // 2) + n], kh, kh,
                                          start=True, stop=True)
                            last.then_inc(G_ps.sem, 1)
                            for hh in range(GH):
                                kh = qk[GD * (hh % 2):GD * (hh % 2) + GD, 2 + hh // 2, tok(t)]
                                qh = qk[GD * (hh % 2):GD * (hh % 2) + GD, hh // 2, tok(t)]
                                last = mm(PS[0:n, 4 + 2 * (hh % 2), P * (hh // 2):P * (hh // 2) + n], kh, qh,
                                          start=True, stop=True)
                            last.then_inc(at_ps.sem, 1)
                        elif k == 1:
                            pe.wait_ge(*M_done(i, t + 1))
                            small(t == 4)
                            for hh in range(GH):
                                last = tr(PS[0:n, 3, P * hh:P * hh + n], X[0:n, hh, 0:n], ident[0:n, 0:n])
                            last.then_inc(MT_ps.sem, 1)
                        elif k < 7:
                            lv = k - 2
                            if lv:
                                pe.wait_ge(*X_done(i, 4 * t + lv))
                                pe.wait_ge(*R_done(i, 5 * t + lv))
                                small(t == 4)
                                for hh in range(GH):
                                    last = mm(PS[0:n, 6, P * hh:P * hh + n], X[0:n, hh, 0:n], R[0:n, hh, 0:n],
                                              start=True, stop=True)
                                last.then_inc(R_ps.sem, 1)
                            if lv < 4:
                                if lv:
                                    pe.wait_ge(*XT_done(i, 3 * t + lv))
                                else:
                                    pe.wait_ge(*MT_done(i, t + 1))
                                    pe.wait_ge(*at_done(i, t + 1))
                                small(t == 4)
                                for hh in range(GH):
                                    last = mm(PS[0:n, 4, P * hh:P * hh + n], XT[0:n, hh, 0:n], X[0:n, hh, 0:n],
                                              start=True, stop=True)
                                    if lv < 3:
                                        last = mm(PS[0:n, 3, P * hh:P * hh + n], X[0:n, hh, 0:n], XT[0:n, hh, 0:n],
                                                  start=True, stop=True)
                                last.then_inc(sq_ps.sem, 1)
                        else:
                            pe.wait_ge(*R_done(i, 5 * t + 5))
                            pe.wait_ge(*kvb_done(i, t + 1))
                            small(t == 4)
                            for hh in range(GH):
                                mm(PS[0:n, 2, GD * hh:GD * hh + GD], R[0:n, hh, 0:n], vbt[0:n, GD * hh:GD * hh + GD],
                                   start=True, stop=True)
                                r0 = GD * (hh % 2)
                                last = mm(PS[r0:r0 + GD, 3, P * (hh // 2):P * (hh // 2) + n],
                                          kbt[0:n, GD * hh:GD * hh + GD], R[0:n, hh, 0:n], start=True, stop=True)
                            last.then_inc(uw_ps.sem, 1)
                    else:
                        j = k // 2
                        c = 4 * t + j
                        rows = slice(CH * j, CH * j + CH)
                        if k % 2 == 0:
                            if j == 0:
                                pe.wait_ge(*uw_done(i, t + 1))
                                if t:
                                    pe.wait_ge(*o_done(i, t))
                            pe.wait_ge(*S_done(i, c + 1))
                            for side, src in ((0, wT), (C, qk)):
                                for p in range(2):
                                    last = mm(PS[rows, 5, side + P * p:side + P * p + P], src[:, p, CH * c:CH * c + CH],
                                              Sb[:, p, :], start=side == 0 and p == 0, stop=side == 0,
                                              skip_group_check=True, tile_position=(0, CH * j))
                            last.then_inc(w_ps.sem, 1)
                        else:
                            pe.wait_ge(*ua_done(i, c + 1))
                            for p in range(2):
                                last = mm(PS[:, 7, P * p:P * p + P], ktok[rows, t, P * p:P * p + P],
                                          u[rows, t, P * p:P * p + P], start=c == 0 and p == 0, stop=True,
                                          skip_group_check=True, tile_position=(CH * j, 0))
                            last.then_inc(S_ps.sem, 1)
                            if j == n // CH - 1:
                                for hh in range(GH):
                                    last = mm(PS[0:n, 5, C + GD * hh:C + GD * hh + GD], atT[0:n, t % 2, hh, 0:n],
                                              u[0:n, t, GD * hh:GD * hh + GD], start=False, stop=True,
                                              skip_group_check=True)
                                last.then_inc(o_ps.sem, 1)
                    wide(wide_after(part))
                pe.wait_ge(*fir_step(i, NFIR))
                for t in range(T):
                    if t >= 2:
                        pe.wait_ge(*f_tok(i, t - 1))
                    for f in range(3):
                        for b in range(KB):
                            dst = C * f + P * b
                            last = tr(PS[0:NT[t], 2 * (t % 2) + dst // 512, dst % 512:dst % 512 + P],
                                      fir[:, f, b, tok(t)], ident)
                    last.then_inc(f_ps.sem, 1)
                pe.wait_ge(*st_done(i, 1))
                pe.wait_ge(*o_done(i, T))
                small()
                for t in range(T):
                    last = tr(PS[0:60, 4 + t // 4, P * (t % 4):P * (t % 4) + NT[t]], st[0:NT[t], 60 * t:60 * t + 60],
                              ident[0:NT[t], 0:NT[t]])
                last.then_inc(st_ps.sem, 1)
                pe.wait_ge(*sT_done(i, 1))
                for m in range(4):
                    if m >= 2:
                        pe.wait_ge(*hd_done(i, m - 1))
                    for a in range(2):
                        dst = PS[:, 2 * (m % 2) + a, 0:HALF]
                        mm(dst, g1[:, 0, P * m:P * m + P], hn[:, 0, cols(a)], start=True, stop=False)
                        mm(dst, g1[:, 1, P * m:P * m + P], hn[:, 1, cols(a)], start=False, stop=False)
                        last = mm(dst, g1[0:60, 2, P * m:P * m + P], sT[:, cols(a)], start=False, stop=True)
                    last.then_inc(g1_ps.sem, 1)
                pe.wait_ge(*hd_done(i, 4))
                for t in range(T):
                    for b in range(4):
                        last = mm(PS[0:NT[t], 6, 20 * t:20 * t + 20], hd[:, b, tok(t)], g2[:, b, :],
                                  start=b == 0, stop=b == 3)
                last.then_inc(g2_ps.sem, 1)
                pe.wait_ge(*on_done(i, 1))
                for t in range(T):
                    for b in range(KB):
                        dst = PS[:, 4 + b, P * t:P * t + P] if t < 4 else PS[:, 6, LT * b:LT * b + LT]
                        last = tr(dst, o[0:NT[t], t, P * b:P * b + P], ident[0:NT[t], 0:NT[t]])
                last.then_inc(oT_ps.sem, 1)
                pe.wait_ge(*oT_done(i, 1))
                for m in range(KB):
                    for a in range(2):
                        for b in range(KB):
                            last = mm(PS[:, 2 * m + a, 0:HALF], ow[:, b, P * m:P * m + P], oT[:, b, cols(a)],
                                      start=b == 0, stop=b == KB - 1)
                last.then_inc(ow_ps.sem, 1)
                mean(i, 1)
                norm(i, 1, 2)
                norm(i, 2, 5)
                pe.wait_ge(*norm_out(i, 3))
                for a in range(2):
                    for b in range(KB):
                        last = mm(PS[:, a, 0:HALF], wkva[:, b, :], x1[:, b, cols(a)], start=b == 0, stop=b == KB - 1)
                last.then_inc(ck_ps.sem, 1)
                for t in range(T):
                    for b in range(KB):
                        last = mm(PS[0:NT[t], 2, NOPE * t:NOPE * t + NOPE], x1[:, b, tok(t)], wkva[:, b, 0:NOPE],
                                  start=b == 0, stop=b == KB - 1)
                last.then_inc(vt_ps.sem, 1)
                pe.wait_ge(*ck_done(i, 1))
                pe.wait_ge(*norm_out(i, 3))
                for a in range(2):
                    last = mm(PS[:, 4 + a, 0:HALF], K["swap"], ck[:, cols(a)], start=True, stop=True)
                last.then_inc(cks_ps.sem, 1)
                pe.wait_ge(*vt_done(i, 1))
                pe.wait_ge(*ckr_done(i, 1))
                for m in range(QB + 1):
                    if m < QB:
                        if m >= 2:
                            pe.wait_ge(*q_done(i, m - 1))
                        for a in range(2):
                            for b in range(KB):
                                last = mm(PS[:, 2 * (m % 2) + a, 0:HALF], wq[:, b, P * m:P * m + P], x1[:, b, cols(a)],
                                          start=b == 0, stop=b == KB - 1)
                        last.then_inc(q_ps.sem, 1)
                    if m:
                        r = m - 1
                        pe.wait_ge(*q_done(i, r + 1))
                        if r >= 2:
                            pe.wait_ge(*qT_done(i, r - 1))
                        for a in range(2):
                            last = mm(PS[:, 4 + 2 * (r % 2) + a, 0:HALF], K["swap"], qraw[:, r % 2, cols(a)],
                                      start=True, stop=True)
                        last.then_inc(qs_ps.sem, 1)
                pe.wait_ge(*qT_done(i, QB + 1))
                def copied(n):
                    return (pT_v if n % 2 else pT_a)(i, n // 2 + 1)

                def scores(n):
                    t, hh = STEPS[n]
                    if t < 4:
                        if n >= 4:
                            pe.wait_ge(*exp_done(i, n - 3))
                        mm(PS[:, n % 4, 0:P * (t + 1)], qT[:, hh // 2, tok(t)], kz[:, hh % 2, 0:P * (t + 1)],
                           start=True, stop=True).then_inc(s_ps.sem, 1)
                    else:
                        pe.wait_ge(*exp_done(i, max(n - 1, NSTEP - 6 + 2 * (n % 2)) if hh >= 2 else NSTEP - 6 + 2 * hh))
                        q = qlast[:, P * (hh // 2):P * (hh // 2) + P]
                        for c0, c1 in ((0, 512), (512, L)):
                            last = mm(PS[:, 2 * (n % 2) + c0 // 512, 0:c1 - c0], q, kz[:, hh % 2, c0:c1],
                                      start=True, stop=True)
                        last.then_inc(s_ps.sem, 1)

                def turn(n):
                    t, hh = STEPS[n]
                    pe.wait_ge(*exp_done(i, n + 1))
                    if n >= 2:
                        pe.wait_ge(*copied(n - 2))
                    if t == 4:
                        pe.wait_ge(*copied(n - 1))
                    for k in range(t + 1):
                        bank = 4 + n % 2 if t < 4 else 4 + k // 4
                        last = tr(PS[0:NT[k], bank, P * (k % 4):P * (k % 4) + P], pr[:, n % 3, tok(k)], ident)
                    last.then_inc(pT_ps.sem, 1)

                def times_v(n):
                    t, hh = STEPS[n]
                    pe.wait_ge(*copied(n))
                    if hh == 0 and t >= 2:
                        pe.wait_ge(*yT_done(i, t - 1))
                    b, s = place(hh) if t < 4 else (0, hh)
                    for k in range(t + 1):
                        last = mm(PS[:, 6 + t % 2, P * b + NOPE * s:P * b + NOPE * s + NOPE],
                                  prT[0:NT[k], n % 2, P * k:P * k + P], vt[0:NT[k], k, :], start=k == 0, stop=k == t)
                    if n + 1 == NSTEP or STEPS[n + 1][0] != t:
                        last.then_inc(y_ps.sem, 1)

                def y_turn(t):
                    pe.wait_ge(*yn_done(i, t + 1))
                    for b in range(4 if t < 4 else 1):
                        last = tr(PS[:, 6 + t % 2, P * b:P * b + P],
                                  yn[:, 4 * b:4 * b + 4, :].rearrange("p h d -> p (h d)"), ident)
                    last.then_inc(yT_ps.sem, 1)

                for n in range(3):
                    scores(n)
                for n in range(NSTEP + 1):
                    if n < NSTEP:
                        turn(n)
                    if n + 3 < NSTEP:
                        scores(n + 3)
                    if n >= 1:
                        times_v(n - 1)
                    if n >= AH and n % AH == 3:
                        y_turn(n // AH - 1)
                y_turn(T - 1)
                pe.wait_ge(*yT_done(i, T))
                for m in range(KB):
                    for a in range(2):
                        for b in range(4):
                            last = mm(PS[:, 2 * m + a, 0:HALF], wo[:, b, P * m:P * m + P], yT[:, b, cols(a)],
                                      start=b == 0, stop=b == 3)
                last.then_inc(wo_ps.sem, 1)
                norm(i, 3, 4)
                pe.wait_ge(*norm_out(i, 4))
                for t in range(T):
                    for b in range(KB):
                        last = mm(PS[0:NT[t], 6, E * t:E * t + E], xn[:, b, tok(t)], wgate[:, b, :],
                                  start=b == 0, stop=b == KB - 1)
                last.then_inc(gl_ps.sem, 1)
                pe.wait_ge(*comb_done(i, 1))
                for e in range(E):
                    if e >= 4:
                        pe.wait_ge(*cb_done(i, e - 3))
                    for t in range(4):
                        last = mm(PS[:, e % 4, tok(t)], gl[:, t, e:e + 1].to_broadcast([P, P]), ident,
                                  start=True, stop=True)
                    if e == E - 1:
                        for r in range(E):
                            last = mm(PS[:, 4, LT * r:LT * r + LT], gl[0:LT, 4, r:r + 1].to_broadcast([LT, P]),
                                      ident[0:LT, 0:LT], start=True, stop=True)
                    last.then_inc(cb_ps.sem, 1)
                pe.wait_ge(*cb_done(i, E))
                units = [(a, e) for a in range(2) for e in range(NE)]
                for n in range(len(units) + 1):
                    if n < len(units):
                        a, e = units[n]
                        if n >= 2:
                            pe.wait_ge(*gu_done(i, n - 1))
                        for w, bank in ((wg, 2 * (n % 2)), (wu, 2 * (n % 2) + 1)):
                            for b in range(KB):
                                last = mm(PS[:, bank, 0:HALF], w[:, e, b, :], xn[:, b, cols(a)],
                                          start=b == 0, stop=b == KB - 1)
                        last.then_inc(gu_ps.sem, 1)
                    if n:
                        a, e = units[n - 1]
                        pe.wait_ge(*gu_done(i, n))
                        for m in range(KB):
                            last = mm(PS[:, 4 + 2 * a + m, 0:HALF], wd[:, e, P * m:P * m + P], gu[:, (n - 1) % 2, :],
                                      start=e == 0, stop=e == NE - 1)
                        last.then_inc(dn_ps.sem, 1)
                pe.wait_ge(*res_done(i, 2))
                for t in range(T):
                    if t >= 2:
                        pe.wait_ge(*rT_done(i, t - 1))
                    for b in range(KB):
                        last = tr(PS[0:NT[t], t % 2, P * b:P * b + P], h[:, b, tok(t)], ident)
                    last.then_inc(rT_ps.sem, 1)

        @block.scalar
        def _(act):
            A = act.activation
            act.wait_ge(loaded.sem, 16 * nloads)
            act.wait_ge(setup.sem, 2)
            for hh in range(GH):
                A(gk[:, 20 + 5 * hh:25 + 5 * hh], Wt["ltemp"][:, hh:hh + 1].to_broadcast([P, 5]), ACT.Exp, scale=-1.0)
                last = A(gk[:, 40 + 5 * hh:45 + 5 * hh], Wt["floor"][:, hh:hh + 1].to_broadcast([P, 5]), ACT.Sigmoid)
            last.then_inc(setup_act.sem, 1)

            act.sem_inc(rT_done.sem, rT_done.start)

            def norm(i, n, src):
                act.wait_ge(*norm_src(i, n + 1))
                A(sq, src, ACT.Square).then_inc(norm_sq.sem, 1)
                act.wait_ge(*norm_ps(i, n + 1))
                bank = (2, 2, 5, 4)[n]
                A(rt[:, 0:4], PS[:, bank, 0:4], ACT.Sqrt, bias=K["eps5"])
                A(rt[0:LT, 4:5], PS[0:LT, bank, 4:5], ACT.Sqrt, bias=K["eps5"][0:LT]).then_inc(norm_sd.sem, 1)

            prepared = [0]

            def prepare(function):
                A(scrap[:, prepared[0]:prepared[0] + 1], K["eps5"], function)
                prepared[0] += 1

            with act.Fori(0, nseq) as i:
                prepare(ACT.Sqrt)
                for k in range(0, 8, 2):
                    act.wait_ge(*xT_ps(i, k + 1))
                    A(xT[:, k, :], PS[:, 0, :], ACT.Copy).then_inc(xT_a.sem, 1)
                norm(i, 0, hc)
                prepare(ACT.Silu)
                made = [0]

                def diagonals(upto):
                    for w in range(made[0], min(upto, NWIDE)):
                        if w >= 8:
                            act.wait_ge(*wide_ps(i, w - 7))
                        col = sum(FIRS) - 1 - w % WP
                        A(diag[:, w % 8, :], ident, ACT.Copy,
                          scale=firw[:, w // WP, col:col + 1]).then_inc(diag_done.sem, 1)
                    made[0] = max(made[0], upto)

                for n in range(7):
                    if n < 6:
                        act.wait_ge(*qkv_ps(i, n + 1))
                        A(halves(z[:, QKV[n], 3:3 + L]), pair(2 + 2 * (n % 2)), ACT.Copy).then_inc(z_done.sem, 1)
                    if n:
                        m = QKV[n - 1]
                        act.wait_ge(*conv_done(i, n))
                        dst = qk[:, m, :] if m < 4 else vp[:, m - 4, PAD:PAD + L]
                        A(dst, cv[:, (n - 1) % 2, :], ACT.Silu).then_inc(silu_done.sem, 1)
                        if n >= 3:
                            diagonals(4 * (n - 2))
                act.wait_ge(*beta_ps(i, 1))
                A(beta[:, 0:4, :], PS[:, 6, 0:16].rearrange("p (t h) -> p t h", t=4), ACT.Sigmoid)
                A(beta[0:LT, 4, :], PS[0:LT, 6, 16:20], ACT.Sigmoid).then_inc(beta_done.sem, 1)
                act.wait_ge(*silu_done(i, 6))
                A(sq4, qk, ACT.Square).then_inc(l2_sq.sem, 1)
                prepare(ACT.Sqrt)
                diagonals(WIDE_AT[0] + 2)
                act.wait_ge(*l2_ps(i, 1))
                A(rl[:, 0:32], PS[:, 7, 0:32], ACT.Sqrt, bias=K["eps6"])
                A(rl[0:LT, 32:40], PS[0:LT, 7, 32:40], ACT.Sqrt, bias=K["eps6"][0:LT]).then_inc(l2_sd.sem, 1)
                diagonals(WIDE_AT[2] + 6)
                act.wait_ge(*y_out(i, 0))
                A(Sb, Sb, ACT.Copy, scale=0.0).then_inc(S_done.sem, 1)
                for t in range(T):
                    n = NT[t]
                    act.wait_ge(*kv_ps(i, t + 1))
                    A(ktok[0:n, t, :], PS[0:n, 2 + t % 2, 0:C], ACT.Copy)
                    A(F[0:n, t, 4, :], PS[0:n, 2 + t % 2, C:2 * C], ACT.Copy).then_inc(kv_tok.sem, 1)
                for part, (what, t, k) in enumerate(DELTA):
                    n = NT[t]
                    if what == "inverse":
                        if k == 1:
                            act.wait_ge(*MT_ps(i, t + 1))
                            A(XT[0:n, :, 0:n], PS[0:n, 3, :].rearrange("p (h n) -> p h n", h=GH)[:, :, 0:n],
                              ACT.Copy).then_inc(MT_done.sem, 1)
                        elif 2 <= k <= 4:
                            if k == 2:
                                act.wait_ge(*R_done(i, 5 * t + 1))
                            act.wait_ge(*sq_ps(i, 4 * t + k - 1))
                            A(XT[0:n, :, 0:n], PS[0:n, 3, :].rearrange("p (h n) -> p h n", h=GH)[:, :, 0:n],
                              ACT.Copy).then_inc(XT_done.sem, 1)
                        elif k == 7:
                            act.wait_ge(*uw_ps(i, t + 1))
                            A(u[0:n, t, :], PS[0:n, 2, 0:C], ACT.Copy)
                            A(wT[:, :, tok(t)], PS[:, 3, 0:C].rearrange("p (b n) -> p b n", b=2)[:, :, 0:n],
                              ACT.Copy).then_inc(uw_done.sem, 1)
                    elif k % 2:
                        c = 4 * t + k // 2
                        act.wait_ge(*S_ps(i, c + 1))
                        for q in range(2):
                            r = slice(GD * q, GD * q + GD)
                            last = A(Sb[r, :, r], PS[r, 7, 0:C].rearrange("p (b n) -> p b n", b=2)[:, :, r], ACT.Copy)
                        last.then_inc(S_done.sem, 1)
                        if k // 2 == n // CH - 1:
                            act.wait_ge(*o_ps(i, t + 1))
                            A(F[0:n, t, 3, :], PS[0:n, 5, C:2 * C], ACT.Copy).then_inc(o_done.sem, 1)
                    diagonals(wide_after(part) + 6)
                for t in range(T):
                    n = NT[t]
                    act.wait_ge(*f_ps(i, t + 1))
                    A(F[0:n, t, 0:2, :], PS[0:n, 2 * (t % 2), :].rearrange("p (k c) -> p k c", k=2), ACT.Copy)
                    A(F[0:n, t, 2, :], PS[0:n, 2 * (t % 2) + 1, 0:C], ACT.Copy).then_inc(f_tok.sem, 1)
                    act.wait_ge(*f_tok(i, t + 1))
                    if t:
                        act.wait_ge(*f_used(i, t))
                    A(fsq[0:n, :], F[0:n, t, :, :].rearrange("p k c -> p (k c)"), ACT.Square).then_inc(f_sq.sem, 1)
                act.wait_ge(*rms_in(i, 1))
                A(st.rearrange("p (g s h) -> p g s h", s=3, h=4)[:, :, 1, :], ms.rearrange("p (g h) -> p g h", h=4),
                  ACT.Sqrt).then_inc(st_done.sem, 1)
                prepare(ACT.Gelu)
                act.wait_ge(*st_ps(i, 1))
                A(sT[:, 0:512], PS[0:60, 4, :], ACT.Copy)
                A(sT[:, 512:L], PS[0:60, 5, 0:LT], ACT.Copy).then_inc(sT_done.sem, 1)
                for m in range(4):
                    act.wait_ge(*g1_ps(i, m + 1))
                    A(halves(hd[:, m, :]), pair(2 * (m % 2)), ACT.Gelu, bias=Wt["g1b"][:, m:m + 1]).then_inc(hd_done.sem, 1)
                prepare(ACT.Exp)
                act.wait_ge(*lg_in(i, 1))
                A(lg, lg, ACT.Exp).then_inc(lg_exp.sem, 1)
                prepare(ACT.Sqrt)
                act.wait_ge(*oss(i, 1))
                A(s20, m20, ACT.Sqrt, bias=K["eps5"]).then_inc(oss_sd.sem, 1)
                act.wait_ge(*oT_ps(i, 1))
                for b in range(KB):
                    A(oT[:, b, 0:512], PS[:, 4 + b, :], ACT.Copy)
                A(oT[:, :, 512:L], PS[:, 6, 0:2 * LT].rearrange("p (b l) -> p b l", b=2), ACT.Copy).then_inc(oT_done.sem, 1)
                norm(i, 1, hc)
                norm(i, 2, hn)
                prepare(ACT.Exp)
                act.wait_ge(*ck_ps(i, 1))
                A(halves(ck), pair(0), ACT.Copy).then_inc(ck_done.sem, 1)
                act.wait_ge(*vt_ps(i, 1))
                A(vt[:, 0:4, :], PS[:, 2, 0:4 * NOPE].rearrange("p (t c) -> p t c", t=4), ACT.Copy)
                A(vt[0:LT, 4, :], PS[0:LT, 2, 4 * NOPE:5 * NOPE], ACT.Copy).then_inc(vt_done.sem, 1)
                for m in range(QB):
                    act.wait_ge(*q_ps(i, m + 1))
                    if m >= 2:
                        act.wait_ge(*qT_done(i, m - 1))
                    A(halves(qraw[:, m % 2, :]), pair(2 * (m % 2)), ACT.Copy, scale=AD ** -0.5).then_inc(q_done.sem, 1)

                def soften(n):
                    t, hh = STEPS[n]
                    act.wait_ge(*max_done(i, n + 1))
                    if n >= 3:
                        act.wait_ge(*pT_ps(i, n - 2))
                    if hh == 0 and t >= 2:
                        act.wait_ge(*yn_done(i, t - 1))
                    if t < 4:
                        b, s = place(hh)
                        col, kk = 4 * b + s, P * (t + 1)
                        src = PS[:, n % 4, 0:kk]
                    else:
                        col, kk = hh, L
                        src = PS[:, 2 * (n % 2):2 * (n % 2) + 2, :].rearrange("p a c -> p (a c)")[:, 0:kk]
                    A(pr[:, n % 3, 0:kk], src, ACT.Exp, bias=nmax[:, t % 2, col:col + 1],
                      accum_out=rsum[:, t % 2, col:col + 1]).then_inc(exp_done.sem, 1)

                def y_copy(t):
                    act.wait_ge(*yT_ps(i, t + 1))
                    A(yT[:, :, tok(t)], PS[:, 6 + t % 2, 0:4 * NT[t]].rearrange("p (b n) -> p b n", b=4),
                      ACT.Copy).then_inc(yT_done.sem, 1)

                soften(0)
                for n in range(NSTEP):
                    if n + 1 < NSTEP:
                        soften(n + 1)
                    if n % 2 == 0:
                        t = STEPS[n][0]
                        act.wait_ge(*pT_ps(i, n + 1))
                        if t < 4:
                            A(prT[:, 0, 0:P * (t + 1)], PS[:, 4, 0:P * (t + 1)], ACT.Copy).then_inc(pT_a.sem, 1)
                        else:
                            A(prT[:, 0, 0:512], PS[:, 4, :], ACT.Copy)
                            A(prT[0:LT, 0, 512:640], PS[0:LT, 5, 0:P], ACT.Copy).then_inc(pT_a.sem, 1)
                    if n >= AH and n % AH == 5:
                        y_copy(n // AH - 1)
                y_copy(T - 2)
                prepare(ACT.Sqrt)
                y_copy(T - 1)
                norm(i, 3, x2)
                prepare(ACT.Exp)
                act.wait_ge(*gl_in(i, 1))
                A(gl, gl, ACT.Exp).then_inc(gl_exp.sem, 1)
                prepare(ACT.Silu)
                for e in range(E):
                    act.wait_ge(*cb_ps(i, e + 1))
                    last = A(cb[:, e, 0:512], PS[:, e % 4, :], ACT.Copy)
                    if e == E - 1:
                        last = A(cb[:, :, 512:L], PS[:, 4, 0:E * LT].rearrange("p (e l) -> p e l", e=E), ACT.Copy)
                    last.then_inc(cb_done.sem, 1)
                for n in range(2 * NE):
                    act.wait_ge(*gu_ps(i, n + 1))
                    if n >= 2:
                        act.wait_ge(*gu_done(i, n - 1))
                    A(gs[:, n % 2, :], PS[:, 2 * (n % 2), 0:HALF], ACT.Silu).then_inc(gs_done.sem, 1)
                for t in range(T):
                    n = NT[t]
                    act.wait_ge(*rT_ps(i, t + 1))
                    A(ot[0:n, t, :], PS[0:n, t % 2, 0:C], ACT.Copy).then_inc(rT_done.sem, 1)

        @block.vector
        def _(dve):
            steps = [0]

            def link(i, ins):
                ins.then_inc(v_step.sem, 1)
                steps[0] += 1
                dve.wait_ge(*v_step(i, steps[0]))

            TT, TS, STT, RED, CP = (dve.tensor_tensor, dve.tensor_scalar, dve.scalar_tensor_tensor,
                                    dve.tensor_reduce, dve.tensor_copy)

            dve.wait_ge(loaded.sem, 16 * nloads)
            dve.memset(hc, 0.0).then_inc(setup.sem, 1)
            for k in range(8):
                d, b = k // KB, k % KB
                TT(tokwT[:, k, :], tokws_sb[:, b, :], tokw_sb[:, d, :], ALU.mult)
            dve.wait_ge(setup_pe.sem, 1)
            wq6 = Wt["wq"][:, :].rearrange("p (k g b p2 d) -> p k g b p2 d", k=KB, g=2, b=4, p2=2)
            for b in range(4):
                for kb in range(KB):
                    CP(wq6[:, kb, :, b, :, 0:NOPE],
                       PS[:, kb, P * b:P * b + P].rearrange("p (g p2 d) -> p g p2 d", g=2, p2=2))
                CP(wo[:, b, :], PS[:, 2 + b // 2, C * (b % 2):C * (b % 2) + C])
            dve.memset(kz, 0.0)
            dve.memset(gfloor[:, :], 0.0)
            last = CP(gk[:, 0:20], Wt["g2b"][:, :])
            last.then_inc(setup_dve.sem, 1)
            dve.wait_ge(setup_dve.sem, 1)
            dve.memset(arena[:, :], 0.0).then_inc(setup.sem, 1)
            g3 = gk[:, 0:20].rearrange("p (h k) -> p h k", k=5)
            TT(g3[:, :, 4], g3[:, :, 4], Wt["vbias"][:, :], ALU.add)
            dve.wait_ge(setup_act.sem, 1)
            f3 = gfloor[:, :].rearrange("p (h k) -> p h k", k=5)
            s3 = gk[:, 40:60].rearrange("p (h k) -> p h k", k=5)
            CP(f3[:, :, 0:4], s3[:, :, 0:4]).then_inc(setup_dve.sem, 1)
            dve.wait_ge(setup_dve.sem, 2)
            TS(gk[:, 40:60], gk[:, 40:60], -4.0, 1.0, ALU.mult, ALU.add).then_inc(setup.sem, 1)

            def centre(i, n):
                dve.wait_ge(*mean_ps(i, n + 1))
                for b in range(KB):
                    last = TT(halves(hc[:, b, :]), halves(h[:, b, :]), pair(0), ALU.subtract)
                last.then_inc(norm_src.sem, 1)

            def norm(i, n, src, dst, weight=None):
                dve.wait_ge(*norm_sd(i, n + 1))
                dve.reciprocal(rt[:, 0:4], rt[:, 0:4])
                dve.reciprocal(rt[0:LT, 4:5], rt[0:LT, 4:5]).then_inc(norm_rc.sem, 1)
                dve.wait_ge(*norm_bc(i, n + 1))
                bank = (3, 3, 6, 5)[n]
                for b in range(KB):
                    for k, s in ((0, slice(0, 512)), (1, slice(512, L))):
                        one = PS[:, bank + k, 0:s.stop - s.start]
                        if weight is None:
                            last = TT(dst[:, b, s], src[:, b, s], one, ALU.mult)
                        else:
                            last = STT(dst[:, b, s], src[:, b, s], weight[:, b:b + 1], one, ALU.mult, ALU.mult)
                last.then_inc(norm_out.sem, 1)

            with dve.Fori(0, nseq) as i:
                for k in range(1, 8, 2):
                    dve.wait_ge(*xT_ps(i, k + 1))
                    CP(xT[:, k, :], PS[:, 1, :]).then_inc(xT_v.sem, 1)
                dve.wait_ge(*xT_ps(i, 9))
                CP(h[:, :, 512:L], PS[:, 4, 0:2 * LT].rearrange("p (b l) -> p b l", b=2))
                dve.wait_ge(*tok_ps(i, 1))
                CP(h[:, :, 0:512], PS[:, 2:4, :]).then_inc(mean_src.sem, 1)
                dve.wait_ge(*mean_src(i, 1))
                centre(i, 0)
                dve.wait_ge(*norm_src(i, 1))
                norm(i, 0, hc, hn)
                dve.memset(z[:, :, 0:3], 0.0)
                link(i, dve.memset(vp[:, :, 0:PAD], 0.0))
                for n, m in enumerate(QKV):
                    dve.wait_ge(*z_done(i, n + 1))
                    if n >= 2:
                        dve.wait_ge(*silu_done(i, n - 1))
                    link(i, TS(cv[:, n % 2, :], z[:, m, 0:L], convw[:, m, 0:1], None, ALU.mult))
                    for j in range(1, CONV):
                        last = STT(cv[:, n % 2, :], z[:, m, j:j + L], convw[:, m, j:j + 1], cv[:, n % 2, :],
                                   ALU.mult, ALU.add)
                        if j < CONV - 1:
                            link(i, last)
                    last.then_inc(conv_done.sem, 1)
                dve.wait_ge(*conv_done(i, 6))

                at_tap = {}
                done = [0, 0, 0]

                def step(f, b, ins):
                    ins.then_inc(fir_step.sem, 1)
                    done[0] += 1
                    at_tap[f, b] = done[0]

                def filters(n):
                    for f, j, b in VTAPS[done[1]:done[1] + n]:
                        src = vp[:, b, PAD - j:PAD - j + L]
                        w = firw[:, b, sum(FIRS[:f]) + FIRS[f] - 1 - j:sum(FIRS[:f]) + FIRS[f] - j]
                        if (f, b) not in at_tap:
                            ins = TS(fir[:, f, b, :], src, w, None, ALU.mult)
                        else:
                            dve.wait_ge(*fir_step(i, at_tap[f, b]))
                            ins = STT(fir[:, f, b, :], src, w, fir[:, f, b, :], ALU.mult, ALU.add)
                        step(f, b, ins)
                        done[1] += 1

                def add_wide():
                    b = done[2]
                    dve.wait_ge(*wide_ps(i, WP * (b + 1)))
                    dve.wait_ge(*fir_step(i, at_tap[2, b]))
                    TT(halves(fir[:, 2, b, :]), halves(fir[:, 2, b, :]), pair(0), ALU.add).then_inc(wide_out.sem, 1)
                    dve.wait_ge(*wide_out(i, b + 1))
                    step(2, b, dve.nop())
                    done[2] += 1

                filters(14)
                dve.wait_ge(*l2_sd(i, 1))
                dve.reciprocal(rl[:, 0:32], rl[:, 0:32])
                link(i, dve.reciprocal(rl[0:LT, 32:40], rl[0:LT, 32:40]))
                CP(rlx.rearrange("p t (h d) -> p (t h) d", d=GD),
                   rl[:, 0:32].rearrange("p (h a) -> p h a", a=1).to_broadcast([P, 32, GD]))
                CP(rly[0:LT, :].rearrange("p (h d) -> p h d", d=GD),
                   rl[0:LT, 32:40].rearrange("p (h a) -> p h a", a=1).to_broadcast([LT, 8, GD])).then_inc(l2_rc.sem, 1)
                filters(6)
                dve.wait_ge(*l2_bc(i, 1))
                TT(qk[:, :, 0:512], qk[:, :, 0:512], PS[:, 2:6, :], ALU.mult)
                TT(qk[:, :, 512:L], qk[:, :, 512:L], PS[:, 6, 0:4 * LT].rearrange("p (b l) -> p b l", b=4),
                   ALU.mult).then_inc(qk_done.sem, 1)
                dve.wait_ge(*beta_done(i, 1))
                filters(8)
                early = done[1]
                for part, (what, t, k) in enumerate(DELTA):
                    n = NT[t]
                    bt = beta[0:n, t, :]
                    if what == "inverse":
                        if k == 0:
                            dve.wait_ge(*G_ps(i, t + 1))
                            for hh in range(GH):
                                last = STT(X[0:n, hh, 0:n], PS[0:n, 2 + hh % 2, P * (hh // 2):P * (hh // 2) + n],
                                           bt[:, hh:hh + 1], K["strict"][0:n, 0:n], ALU.mult, ALU.mult)
                            last.then_inc(M_done.sem, 1)
                            dve.wait_ge(*at_ps(i, t + 1))
                            for q in range(2):
                                last = TT(atT[0:n, t % 2, q::2, 0:n],
                                          PS[0:n, 4 + 2 * q, 0:C].rearrange("p (h n) -> p h n", h=2)[:, :, 0:n],
                                          K["upper"][0:n, 0:n].rearrange("p (a n) -> p a n", a=1).to_broadcast([n, 2, n]),
                                          ALU.mult)
                            last.then_inc(at_done.sem, 1)
                        elif k == 1:
                            dve.wait_ge(*MT_done(i, t + 1))
                            TT(R[0:n, :, 0:n], XT[0:n, :, 0:n],
                               ident[0:n, 0:n].rearrange("p (a n) -> p a n", a=1).to_broadcast([n, GH, n]),
                               ALU.add).then_inc(R_done.sem, 1)
                            dve.wait_ge(*kv_tok(i, t + 1))
                            bb = bt.rearrange("p (h a) -> p h a", a=1).to_broadcast([n, GH, GD])
                            TT(kbt[0:n, :].rearrange("p (h d) -> p h d", h=GH),
                               ktok[0:n, t, :].rearrange("p (h d) -> p h d", h=GH), bb, ALU.mult)
                            TT(vbt[0:n, :].rearrange("p (h d) -> p h d", h=GH),
                               F[0:n, t, 4, :].rearrange("p (h d) -> p h d", h=GH), bb, ALU.mult
                               ).then_inc(kvb_done.sem, 1)
                        elif k < 7:
                            lv = k - 2
                            if lv:
                                dve.wait_ge(*R_ps(i, 4 * t + lv))
                                dve.wait_ge(*R_done(i, 5 * t + lv))
                                TT(R[0:n, :, 0:n], R[0:n, :, 0:n],
                                   PS[0:n, 6, :].rearrange("p (h n) -> p h n", h=GH)[:, :, 0:n],
                                   ALU.add).then_inc(R_done.sem, 1)
                            if lv < 4:
                                dve.wait_ge(*sq_ps(i, 4 * t + lv + 1))
                                CP(X[0:n, :, 0:n], PS[0:n, 4, :].rearrange("p (h n) -> p h n", h=GH)[:, :, 0:n]
                                   ).then_inc(X_done.sem, 1)
                    elif k % 2 == 0:
                        c = 4 * t + k // 2
                        rows = slice(CH * (k // 2), CH * (k // 2) + CH)
                        dve.wait_ge(*w_ps(i, c + 1))
                        TT(u[rows, t, :], u[rows, t, :], PS[rows, 5, 0:C], ALU.subtract).then_inc(ua_done.sem, 1)
                    if wide_after(part) >= WP > wide_after(part - 1):
                        add_wide()
                    filters(early + (part + 1) * (len(VTAPS) - early) // len(DELTA) - done[1])
                add_wide()
                assert done[0] == NFIR
                st4 = st.rearrange("p (g s h) -> p g s h", s=3, h=4)
                for t in range(T):
                    n = NT[t]
                    dve.wait_ge(*f_tok(i, t + 1))
                    f3 = F[0:n, t, :, :].rearrange("p k (h d) -> p (k h) d", h=GH)
                    s4 = st[0:n, 60 * t:60 * t + 60].rearrange("p (k s h) -> p k s h", s=3, h=4)
                    f4 = F[0:n, t, :, :].rearrange("p k (h d) -> p k h d", h=GH)
                    dve.wait_ge(*o_done(i, t + 1))
                    RED(s4[:, :, 0, :], f4, AX.X, ALU.add)
                    RED(s4[:, :, 2, :], f4, AX.X, ALU.max, apply_absolute_value=True)
                    dve.wait_ge(*f_sq(i, t + 1))
                    RED(ms[0:n, 20 * t:20 * t + 20], fsq[0:n, :].rearrange("p (g d) -> p g d", d=GD), AX.X,
                        ALU.add).then_inc(f_used.sem, 1)
                dve.wait_ge(*f_used(i, T))
                TS(st4[:, :, 0, :], st4[:, :, 0, :], 1.0 / GD, None, ALU.mult)
                TS(ms, ms, 1.0 / GD, 1e-8, ALU.mult, ALU.max).then_inc(rms_in.sem, 1)
                dve.wait_ge(*g2_ps(i, 1))
                for n, s in ((P, slice(0, 80)), (LT, slice(80, 100))):
                    g = (s.stop - s.start) // 20
                    last = TT(lg[0:n, s].rearrange("p (t k) -> p t k", t=g),
                              PS[0:n, 6, s].rearrange("p (t k) -> p t k", t=g),
                              gk[0:n, 0:20].rearrange("p (a k) -> p a k", a=1).to_broadcast([n, g, 20]), ALU.add)
                link(i, last)
                lg3 = lg.rearrange("p (t k) -> p t k", t=T)
                lg5 = lg.rearrange("p (g k) -> p g k", k=5)
                gw3 = gw.rearrange("p (t k) -> p t k", t=T)
                gw5 = gw.rearrange("p (g k) -> p g k", k=5)

                def over_tiles(v):
                    return v.rearrange("p (a k) -> p a k", a=1).to_broadcast([P, T, 20])

                def over_five(v):
                    return v.rearrange("p (g a) -> p g a", a=1).to_broadcast([P, 20, 5])

                link(i, TT(lg3, lg3, over_tiles(gk[:, 20:40]), ALU.mult))
                link(i, RED(m20, lg5, AX.X, ALU.max))
                TT(lg5, lg5, over_five(m20), ALU.subtract).then_inc(lg_in.sem, 1)
                dve.wait_ge(*lg_exp(i, 1))
                link(i, RED(s20, lg5, AX.X, ALU.add))
                link(i, dve.reciprocal(s20, s20))
                link(i, TT(gw5, lg5, over_five(s20), ALU.mult))
                link(i, TT(gw3, gw3, over_tiles(gk[:, 40:60]), ALU.mult))
                link(i, TT(gw3, gw3, over_tiles(gfloor[:, :]), ALU.add))
                gw4 = gw.rearrange("p (t h k) -> p t k h", t=T, h=GH)
                for t in range(T):
                    n = NT[t]
                    for k in range(5):
                        f3 = F[0:n, t, k, :].rearrange("p (h d) -> p h d", h=GH)
                        wb = gw[0:n, 20 * t:20 * t + 20].rearrange("p (h k a) -> p h k a", h=GH, a=1)[:, :, k, :]
                        last = TT(f3, f3, wb.to_broadcast([n, GH, GD]), ALU.mult)
                    link(i, last)
                    last = RED(o[0:n, t, :], F[0:n, t, :, :].rearrange("p k c -> p c k"), AX.X, ALU.add)
                link(i, last)
                o3 = o.rearrange("p t (h d) -> p (t h) d", h=GH)
                osq = view(asq4, T * C, "p (g d) -> p g d", d=GD)
                link(i, TT(osq, o3, o3, ALU.mult))
                link(i, RED(m20, osq, AX.X, ALU.add))
                TS(m20, m20, 1.0 / GD, None, ALU.mult).then_inc(oss.sem, 1)
                dve.wait_ge(*oss_sd(i, 1))
                link(i, dve.reciprocal(s20, s20))
                link(i, TT(o3, o3, s20.rearrange("p (g a) -> p g a", a=1).to_broadcast([P, 20, GD]), ALU.mult))
                TT(o3, o3, Wt["onorm"][:, :].rearrange("p (a d) -> p a d", a=1).to_broadcast([P, 20, GD]),
                   ALU.mult).then_inc(on_done.sem, 1)
                dve.wait_ge(*ow_ps(i, 1))
                for m in range(KB):
                    last = TT(halves(h[:, m, :]), halves(h[:, m, :]), pair(2 * m), ALU.add)
                last.then_inc(mean_src.sem, 1)
                dve.wait_ge(*mean_src(i, 2))
                centre(i, 1)
                dve.wait_ge(*norm_src(i, 2))
                norm(i, 1, hc, hn)
                dve.wait_ge(*norm_out(i, 2))
                dve.nop().then_inc(norm_src.sem, 1)
                norm(i, 2, hn, x1, Wt["ln1"])
                dve.wait_ge(*cks_ps(i, 1))
                TT(ckr, ck, K["cos"], ALU.mult)
                link(i, TT(halves(qrot), pair(4), halves(K["sin"]), ALU.mult))
                TT(kz[0:AD, 0, :], ckr[0:AD, :], qrot[0:AD, :], ALU.add)
                TT(kz[AD:P, 1, :], ckr[AD:P, :], qrot[AD:P, :], ALU.add).then_inc(ckr_done.sem, 1)
                for m in range(QB):
                    dve.wait_ge(*qs_ps(i, m + 1))
                    TT(qT[:, m, :], qraw[:, m % 2, :], K["cos"], ALU.mult)
                    if m:
                        dve.wait_ge(*qT_done(i, m))
                    link(i, TT(halves(qrot), pair(4 + 2 * (m % 2)), halves(K["sin"]), ALU.mult))
                    TT(qT[:, m, :], qT[:, m, :], qrot, ALU.add).then_inc(qT_done.sem, 1)
                dve.wait_ge(*qT_done(i, QB))
                CP(qlast.rearrange("p (m l) -> p m l", m=QB), qT[:, :, tok(T - 1)]).then_inc(qT_done.sem, 1)
                def top(n):
                    t, hh = STEPS[n]
                    dve.wait_ge(*s_ps(i, n + 1))
                    if hh == 0 and t >= 2:
                        dve.wait_ge(*exp_done(i, n - AH))
                    if t < 4:
                        b, s = place(hh)
                        col, row, mask = 4 * b + s, PS[:, n % 4, 0:P * (t + 1)], causal
                        link(i, TT(row[:, tok(t)], row[:, tok(t)], causal, ALU.min))
                    else:
                        col = hh
                        row = PS[:, 2 * (n % 2):2 * (n % 2) + 2, :].rearrange("p a c -> p (a c)")[:, 0:L]
                        link(i, TT(row[:, tok(t)], row[:, tok(t)], K["causal4"], ALU.min))
                    RED(nmax[:, t % 2, col:col + 1], row, AX.X, ALU.max, negate=True).then_inc(max_done.sem, 1)

                def over_sums(t):
                    heads = AH if t < 4 else 4
                    dve.wait_ge(*y_ps(i, t + 1))
                    if t:
                        dve.wait_ge(*yT_ps(i, t))
                    link(i, dve.reciprocal(rinv[:, 0:heads], rsum[:, t % 2, 0:heads]))
                    TT(yn[:, 0:heads, :], PS[:, 6 + t % 2, 0:NOPE * heads].rearrange("p (h d) -> p h d", h=heads),
                       rinv[:, 0:heads].rearrange("p (h a) -> p h a", a=1).to_broadcast([P, heads, NOPE]),
                       ALU.mult).then_inc(yn_done.sem, 1)

                top(0)
                top(1)
                for n in range(NSTEP):
                    if n + 2 < NSTEP:
                        top(n + 2)
                    if n % 2:
                        t = STEPS[n][0]
                        dve.wait_ge(*pT_ps(i, n + 1))
                        if t < 4:
                            CP(prT[:, 1, 0:P * (t + 1)], PS[:, 5, 0:P * (t + 1)]).then_inc(pT_v.sem, 1)
                        else:
                            CP(prT[:, 1, 0:512], PS[:, 4, :])
                            CP(prT[0:LT, 1, 512:640], PS[0:LT, 5, 0:P]).then_inc(pT_v.sem, 1)
                    if n >= AH and n % AH == 1:
                        over_sums(n // AH - 1)
                over_sums(T - 1)
                dve.wait_ge(*wo_ps(i, 1))
                for m in range(KB):
                    last = TT(halves(x2[:, m, :]), halves(hn[:, m, :]), pair(2 * m), ALU.add)
                last.then_inc(norm_src.sem, 1)
                dve.wait_ge(*norm_src(i, 4))
                TT(h, h, x2, ALU.add)
                norm(i, 3, x2, xn, Wt["ln2"])
                dve.wait_ge(*gl_ps(i, 1))
                TT(gl[:, 0:4, :], PS[:, 6, 0:4 * E].rearrange("p (t e) -> p t e", t=4),
                   Wt["ebias"][:, :].rearrange("p (a e) -> p a e", a=1).to_broadcast([P, 4, E]), ALU.add)
                link(i, TT(gl[0:LT, 4, :], PS[0:LT, 6, 4 * E:5 * E], Wt["ebias"][0:LT, :], ALU.add))
                link(i, RED(m5, gl, AX.X, ALU.max))
                TT(gl, gl, m5.rearrange("p (t a) -> p t a", a=1).to_broadcast([P, T, E]),
                   ALU.subtract).then_inc(gl_in.sem, 1)
                dve.wait_ge(*gl_exp(i, 1))
                mine = gl.rearrange("p t (e a) -> p t e a", a=1).to_broadcast([P, T, E, E])
                other = gl.rearrange("p t (a e) -> p t a e", a=1).to_broadcast([P, T, E, E])
                cmpA3, cmpB3 = (v.rearrange("p t e j -> p t (e j)") for v in (cmpA, cmpB))
                TT(cmpA, other, mine, ALU.is_gt)
                link(i, TT(cmpB, other, mine, ALU.is_equal))
                link(i, TT(cmpB3, cmpB3, K["before"].rearrange("p (a k) -> p a k", a=1).to_broadcast([P, T, E * E]),
                           ALU.mult))
                link(i, TT(cmpA3, cmpA3, cmpB3, ALU.add))
                link(i, RED(rank, cmpA, AX.X, ALU.add))
                link(i, TS(rank, rank, 1.5, None, ALU.is_lt))
                link(i, TT(gl, gl, rank, ALU.mult))
                link(i, RED(s5, gl, AX.X, ALU.add))
                link(i, dve.reciprocal(s5, s5))
                TT(gl, gl, s5.rearrange("p (t a) -> p t a", a=1).to_broadcast([P, T, E]),
                   ALU.mult).then_inc(comb_done.sem, 1)
                for n in range(2 * NE):
                    a, e = n // NE, n % NE
                    dve.wait_ge(*gs_done(i, n + 1))
                    if n >= 2:
                        dve.wait_ge(*dn_ps(i, n - 1))
                    if e < E:
                        dve.wait_ge(*cb_done(i, E))
                        link(i, TT(gu[:, n % 2, :], gs[:, n % 2, :], PS[:, 2 * (n % 2) + 1, 0:HALF], ALU.mult))
                        TT(gu[:, n % 2, :], gu[:, n % 2, :], cb[:, e, cols(a)], ALU.mult).then_inc(gu_done.sem, 1)
                    else:
                        TT(gu[:, n % 2, :], gs[:, n % 2, :], PS[:, 2 * (n % 2) + 1, 0:HALF],
                           ALU.mult).then_inc(gu_done.sem, 1)
                for a in range(2):
                    dve.wait_ge(*dn_ps(i, NE * (a + 1)))
                    TT(h[:, :, cols(a)], h[:, :, cols(a)], PS[:, 4 + 2 * a:6 + 2 * a, 0:HALF],
                       ALU.add).then_inc(res_done.sem, 1)
                assert steps[0] == VSTEPS, ("VSTEPS", steps[0])


def kernel(**inputs):
    import numpy as _np
    import concourse.bacc as _bacc
    from concourse import mybir as _mybir
    from concourse.bass_utils import run_bass_kernel_spmd as _run

    a = {k: _np.asarray(v) for k, v in inputs.items()}

    def blocks(w, p=P):
        return _np.ascontiguousarray(w.reshape(-1, p, w.shape[1]).transpose(1, 0, 2).reshape(p, -1))

    def everywhere(v):
        return _np.ascontiguousarray(_np.broadcast_to(v.reshape(1, -1), (P, v.size)))

    w = {}
    w["wqkv"] = blocks(_np.concatenate([a[f"L0_attn_{n}_w"].T for n in "qkv"], axis=1))
    w["bw"] = blocks(a["L0_attn_b_w"].T)
    w["convw"] = blocks(_np.concatenate([a[f"L0_attn_conv{n}_w"] for n in "qkv"], axis=0))
    w["firw"] = blocks(_np.concatenate([a["L0_attn_" + n].reshape(C, -1) for n in ("fir_s", "fir_l", "fir_wd")], axis=1))
    g1 = _np.zeros((3 * P, 512), _np.float32)
    g1[:316] = a["L0_attn_g1_w"].T
    w["g1"] = blocks(g1)
    w["g1b"] = _np.ascontiguousarray(a["L0_attn_g1_b"].reshape(4, P).T)
    w["g2"] = blocks(a["L0_attn_g2_w"].T)
    w["g2b"] = everywhere(a["L0_attn_g2_b"])
    w["vbias"] = everywhere(a["L0_attn_value_bias"])
    w["ltemp"] = everywhere(a["L0_attn_log_temp"])
    w["floor"] = everywhere(a["L0_attn_floor_logit"])
    w["onorm"] = everywhere(a["L0_attn_onorm_w"])
    w["ow"] = blocks(a["L0_attn_o_w"].T)
    w["ln1"] = _np.ascontiguousarray(a["L0_ffn_w_ln1"].reshape(KB, P).T)
    w["ln2"] = _np.ascontiguousarray(a["L0_ffn_w_ln2"].reshape(KB, P).T)
    w["wq"] = blocks(a["L0_ffn_Wq"])
    w["wkva"] = blocks(_np.concatenate([a["L0_ffn_Wkva"]] * 2, axis=1))
    order = [head_at(b, s) for b in range(4) for s in range(4)]
    w["wo"] = blocks(_np.ascontiguousarray(a["L0_ffn_Wo"].reshape(AH, AD, C)[order, :NOPE]).reshape(AH * NOPE, C))
    wqn = a["L0_ffn_Wq"].reshape(C, AH, AD)[:, order, :NOPE].reshape(C, AH * NOPE).T
    wlat = _np.zeros((4, P, P), _np.float32)
    for b in range(4):
        for s in range(4):
            n0, hh = NOPE * s, head_at(b, s)
            wlat[b, n0:n0 + NOPE, n0:n0 + NOPE] = a["L0_ffn_Wkvb"][:, NOPE * hh:NOPE * hh + NOPE].T
    w["wgate"] = blocks(a["L0_ffn_Wgate"])
    w["ebias"] = everywhere(a["L0_ffn_expert_bias"])
    for n, m in (("wg", "Wg"), ("wu", "Wu")):
        both = _np.concatenate([a["L0_ffn_" + m], a["L0_ffn_s" + m]], axis=0)
        w[n] = _np.ascontiguousarray(both.reshape(NE, KB, P, EI).transpose(2, 0, 1, 3).reshape(P, -1))
    both = _np.concatenate([a["L0_ffn_Wd"], a["L0_ffn_sWd"]], axis=0)
    w["wd"] = _np.ascontiguousarray(both.transpose(1, 0, 2).reshape(P, -1))

    nc = _bacc.Bacc("TRN2", target_bir_lowering=False, num_devices=1)
    arrays = {}

    def put(name, v):
        arrays[name] = v
        return nc.dram_tensor(name, v.shape, _mybir.dt.from_np(v.dtype), kind="ExternalInput").ap()

    x = put("x", _np.ascontiguousarray(a["x"]))
    txt = put("txt", _np.ascontiguousarray(a["txt"]))
    consts = put("consts", constants())
    tokw = put("tokw", everywhere(_np.ascontiguousarray(a["L0_tok_weight"].T)))
    tokws = put("tokws", _np.ascontiguousarray(a["L0_tok_weighted_sum"].T))
    wqn = put("wqn", blocks(wqn))
    wlat = put("wlat", blocks(wlat.reshape(4 * P, P)))
    weights = {n: put("w_" + n + "_dram", v) for n, v in w.items()}
    out = nc.dram_tensor("out", (B, L, C), F32, kind="ExternalOutput").ap()
    build(nc, x, txt, consts, tokw, tokws, wqn, wlat, weights, out)
    r = _run(nc, [arrays], core_ids=[0])
    return r.results[0]["out"]
```

```python
from contextlib import ExitStack

import numpy as np

import concourse.bass as bass
from concourse import mybir

F32 = mybir.dt.float32
ALU = mybir.AluOpType
ACT = mybir.ActivationFunctionType
AX = mybir.AxisListType

P = 128
B = 16
LI = 512
LT = 32
L = LI + LT
C = 256
KB = C // P
HALF = L // 2
D1 = 4
T = 5
NT = [128, 128, 128, 128, 32]
GH, GD = 4, 64
CH = 32
NCHUNK = L // CH
CONV = 4
FIRS = (3, 31, 64)
PAD = FIRS[2] - 1
WP = 36
NWIDE = KB * WP
VTAPS = [(f, j, b) for r in range(FIRS[2]) for f in range(3) for b in range(KB)
         for j in [r + (WP if f == 2 else 0)] if j < FIRS[f]]
NFIR = len(VTAPS) + KB
AH, AD, NOPE = 16, 64, 32
QB = AH // 2
E, EI = 8, 128
NE = E + 1
BIG = 3.0e38
TOGETHER = (4, 2, 1, 1)
STEPS = [(t, h0, TOGETHER[t]) for t in range(T - 1) for h0 in range(0, AH, TOGETHER[t])]
FIRST = [sum(AH // g for g in TOGETHER[:t]) for t in range(T)]
STEPS += [(T - 1, s, 1) for s in range(4)]
NSTEP = len(STEPS)


def head_at(b, s):
    return 8 * (s // 2) + 2 * b + s % 2


QKV = (4, 5, 0, 1, 2, 3)
WIDE_AT = (19, 22, 25)


def wide_after(part):
    return WIDE_AT[2] + (part + 1) * (NWIDE - WIDE_AT[2]) // len(DELTA)


def delta_parts():
    parts = [("inverse", 0, k) for k in range(8)]
    for t in range(T):
        for k in range(max(2 * (NT[t] // CH), 8 if t + 1 < T else 0)):
            if t + 1 < T and k < 8:
                parts.append(("inverse", t + 1, k))
            if k < 2 * (NT[t] // CH):
                parts.append(("chunk", t, k))
    return parts


DELTA = delta_parts()


ARENA = 26100
VSTEPS = 126


class Signal:

    def __init__(self, sem, per, start=0, stage=0):
        self.sem, self.per, self.start, self.stage = sem, per, start, stage

    def __call__(self, i, k):
        return self.sem, (i + self.stage) * self.per + (k + self.start - self.stage * self.per)


CONSTS = dict(ident=P, mean=P, heads=P, swap=P, causal=P, strict=P, upper=P, cos=L, sin=L, causal4=LT, before=64,
              eps5=1, eps6=1)


def constants():
    out = {}
    r = np.arange(P)
    out["ident"] = np.eye(P)
    out["mean"] = np.full((P, P), 1.0 / C)
    out["heads"] = (r[:, None] // GD == r[None, :] // GD) * 1.0
    swap = np.zeros((P, P))
    for m in range(P):
        if m % AD >= NOPE:
            if m % 2 == 0:
                swap[m + 1, m] = -1.0
            else:
                swap[m - 1, m] = 1.0
    out["swap"] = swap
    out["causal"] = np.where(r[None, :] <= r[:, None], BIG, -BIG)
    same = r[:, None] // CH == r[None, :] // CH
    out["strict"] = np.where(same & (r[None, :] < r[:, None]), -1.0, 0.0)
    out["upper"] = np.where(same & (r[None, :] >= r[:, None]), 1.0, 0.0)
    width = AD - NOPE
    freqs = (1.0 / np.float32(100000.0) ** (np.arange(0, width, 2, dtype=np.float32) / np.float32(width))).astype(np.float32)
    ang = np.outer(np.arange(L, dtype=np.float32), freqs).astype(np.float32)
    cos, sin = np.ones((P, L)), np.zeros((P, L))
    for m in range(P):
        if m % AD >= NOPE:
            pair = (m % AD - NOPE) // 2
            cos[m], sin[m] = np.cos(ang[:, pair]), np.sin(ang[:, pair])
    out["cos"], out["sin"] = cos, sin
    out["causal4"] = np.where(r[None, :LT] <= r[:, None] % LT, BIG, -BIG)
    e = np.arange(E)
    out["before"] = np.broadcast_to((e[None, :] < e[:, None]).reshape(1, 64), (P, 64)) * 1.0
    out["eps5"] = np.full((P, 1), 1e-5)
    out["eps6"] = np.full((P, 1), 1e-6)
    return np.ascontiguousarray(np.concatenate([out[k] for k in CONSTS], axis=1).astype(np.float32))


WEIGHTS = dict(wqkv=(P, KB * 3 * C), bw=(P, KB * GH), convw=(P, 6 * CONV), firw=(P, KB * sum(FIRS)),
               g1=(P, 3 * 512), g1b=(P, 4), g2=(P, 4 * 20), g2b=(P, 20), vbias=(P, GH), ltemp=(P, GH),
               floor=(P, GH), onorm=(P, 1), ow=(P, KB * C), ln1=(P, KB), ln2=(P, KB), wq=(P, KB * AH * AD),
               wkva=(P, KB * P), wo=(P, 4 * C), wgate=(P, KB * E),
               ebias=(P, E), wg=(P, NE * KB * EI), wu=(P, NE * KB * EI), wd=(P, NE * C))


def build(nc, x, txt, consts, tokw, tokws, wqn, wlat, weights, out, nseq=B):
    ctx = ExitStack()
    with ctx:
        def sb(name, words, parts=P):
            return ctx.enter_context(nc.sbuf_tensor(name, [parts, words], F32))

        stage = [0]

        def signal(name, per, start=0):
            return Signal(ctx.enter_context(nc.semaphore(name)), per, start, stage[0])

        PS = ctx.enter_context(nc.psum_tensor("PS", [P, 8, 512], F32))
        K = {}
        cst = sb("cst", sum(CONSTS.values()))
        at = 0
        for name, n in CONSTS.items():
            K[name] = cst[:, at:at + n]
            at += n
        Wt = {name: sb("w_" + name, n, parts) for name, (parts, n) in WEIGHTS.items()}
        tokwT = sb("tokwT", 8 * C)[:, :].rearrange("p (k o) -> p k o", k=8)
        h = sb("h", KB * L)[:, :].rearrange("p (b l) -> p b l", b=KB)
        hn = sb("hn", KB * L)[:, :].rearrange("p (b l) -> p b l", b=KB)
        hcsq = sb("hcsq", 2 * KB * L)
        hc = hcsq[:, 0:KB * L].rearrange("p (b l) -> p b l", b=KB)
        sq = hcsq[:, KB * L:2 * KB * L].rearrange("p (b l) -> p b l", b=KB)
        yT = hcsq[:, :].rearrange("p (b l) -> p b l", b=4)
        rt = sb("rt", T)[:, :]
        rr = sb("rr", T)[:, :]
        gk = sb("gk", 3 * 20)
        gfloor = sb("gfloor", 20)
        kz = sb("kz", 2 * L)[:, :].rearrange("p (b l) -> p b l", b=2)
        diag = sb("diag", 8 * P)[:, :].rearrange("p (b n) -> p b n", b=8)
        scrap = sb("scrap", 16)[:, :]

        arena = sb("arena", ARENA)
        used = [0]

        def take(words, again=None):
            start = used[0] if again is None else again
            if again is None:
                used[0] += words
            assert start + words <= ARENA, (start, words)
            return start

        def view(start, words, pattern=None, parts=P, **kw):
            v = arena[0:parts, start:start + words]
            return v.rearrange(pattern, **kw) if pattern else v

        aF = take(T * 5 * C)
        F = view(aF, T * 5 * C, "p (t k c) -> p t k c", t=T, k=5)
        hnext = view(aF, KB * L, "p (b l) -> p b l", b=KB)
        a0 = take(4096)
        z = view(a0, 6 * (L + 3), "p (b l) -> p b l", b=6)
        xT = view(a0, 8 * LI, "p (k l) -> p k l", k=8)
        fir = view(a0, 3 * KB * L, "p (f b l) -> p f b l", f=3, b=KB)
        acv = take(KB * L)
        cv = view(acv, KB * L, "p (b l) -> p b l", b=KB)
        oT = cv
        aqk = take(4 * L)
        qk = view(aqk, 4 * L, "p (b l) -> p b l", b=4)
        asq4 = take(4 * L)
        sq4 = view(asq4, 4 * L, "p (b l) -> p b l", b=4)
        rlx = view(asq4, 4 * 512, "p (t c) -> p t c", t=4)
        fsq = view(asq4, 3 * C)
        dvsq = view(asq4 + 3 * C, 2 * C)
        hd = sq4
        avp = take(KB * (L + PAD))
        vp = view(avp, KB * (L + PAD), "p (b l) -> p b l", b=KB)
        ktok = view(take(T * C), T * C, "p (t c) -> p t c", t=T)
        ot = ktok
        au = take(T * C)
        u = view(au, T * C, "p (t c) -> p t c", t=T)
        o = u
        akbt = take(2 * C)
        kbt = view(akbt, C)
        vbt = view(akbt + C, C)
        rly = view(akbt, 512)
        X = view(take(512), 512, "p (h n) -> p h n", h=GH)
        XT = view(take(512), 512, "p (h n) -> p h n", h=GH)
        R = view(take(512), 512, "p (h n) -> p h n", h=GH)
        atT = view(take(1024), 1024, "p (b h n) -> p b h n", b=2, h=GH)
        wT = view(take(2 * L), 2 * L, "p (b l) -> p b l", b=2)
        Sb = view(take(256), 256, "p (b n) -> p b n", b=2)
        assert used[0] - akbt >= 4 * 1024 + C
        xs = view(akbt, 4 * 1024, "p (t i d) -> p t i d", t=4, d=D1)
        xt = view(akbt + 4096, C, parts=LT)
        st = view(take(T * 60), T * 60)
        ast = take(L)
        sT = view(ast, L, parts=60)
        beta = view(take(20), 20, "p (t h) -> p t h", t=T)
        ms = view(take(100), 100)
        lg = view(take(100), 100)
        gw = view(take(100), 100)
        m20 = view(take(20), 20)
        s20 = view(take(20), 20)
        rl = view(take(T * 8), T * 8)
        ngdn = used[0]
        used[0] = a0
        qT = view(take(QB * L), QB * L, "p (b l) -> p b l", b=QB)
        qlast = view(take(QB * LT), QB * LT)
        cb = qT
        vt = view(take(T * NOPE), T * NOPE, "p (t c) -> p t c", t=T)
        x1 = view(take(KB * L), KB * L, "p (b l) -> p b l", b=KB)
        xn = x1
        x2 = view(take(KB * L), KB * L, "p (b l) -> p b l", b=KB)
        qraw = view(take(2 * L), 2 * L, "p (b l) -> p b l", b=2)
        qrot = view(take(L), L)
        ck = view(take(L), L)
        ckr = view(take(L), L)
        pr = view(take(3 * L), 3 * L, "p (b l) -> p b l", b=3)
        prT = view(take(2 * 640), 1280, "p (b l) -> p b l", b=2)
        yn = view(take(512), 512, "p (h d) -> p h d", h=AH)
        rsum = view(take(2 * AH), 2 * AH, "p (b h) -> p b h", b=2)
        rinv = view(take(AH), AH)
        nmax = view(take(2 * AH), 2 * AH, "p (b h) -> p b h", b=2)
        gl = view(take(T * E), T * E, "p (t e) -> p t e", t=T)
        rank = view(take(T * E), T * E, "p (t e) -> p t e", t=T)
        m5 = view(take(T), T)
        s5 = view(take(T), T)
        cmpA = view(take(T * 64), T * 64, "p (t e j) -> p t e j", t=T, e=E)
        cmpB = view(take(T * 64), T * 64, "p (t e j) -> p t e j", t=T, e=E)
        gs = view(take(L), L, "p (b l) -> p b l", b=2)
        gu = view(take(L), L, "p (b l) -> p b l", b=2)
        used[0] = max(used[0], ngdn)

        tokws_sb = view(a0, KB * C, "p (b o) -> p b o", b=KB)
        tokw_sb = view(a0 + KB * C, D1 * C, "p (d o) -> p d o", d=D1)
        wqn_sb = view(aF, 4 * C, "p (b c) -> p b c", b=4)
        wlat_sb = view(aF + 4 * C, 4 * P, "p (b l) -> p b l", b=4)

        ident, causal = K["ident"], K["causal"]
        wqkv = Wt["wqkv"][:, :].rearrange("p (b m) -> p b m", b=KB)
        bw = Wt["bw"][:, :].rearrange("p (b m) -> p b m", b=KB)
        convw = Wt["convw"][:, :].rearrange("p (b j) -> p b j", b=6)
        firw = Wt["firw"][:, :].rearrange("p (b j) -> p b j", b=KB)
        g1 = Wt["g1"][:, :].rearrange("p (b m) -> p b m", b=3)
        g2 = Wt["g2"][:, :].rearrange("p (b m) -> p b m", b=4)
        ow = Wt["ow"][:, :].rearrange("p (b m) -> p b m", b=KB)
        wq = Wt["wq"][:, :].rearrange("p (b m) -> p b m", b=KB)
        wkva = Wt["wkva"][:, :].rearrange("p (b m) -> p b m", b=KB)
        wo = Wt["wo"][:, :].rearrange("p (b m) -> p b m", b=4)
        wgate = Wt["wgate"][:, :].rearrange("p (b m) -> p b m", b=KB)
        wg = Wt["wg"][:, :].rearrange("p (e b m) -> p e b m", e=NE, b=KB)
        wu = Wt["wu"][:, :].rearrange("p (e b m) -> p e b m", e=NE, b=KB)
        wd = Wt["wd"][:, :].rearrange("p (e m) -> p e m", e=NE)

        def pair(bank, parts=P):
            return PS[0:parts, bank:bank + 2, 0:HALF]

        def halves(v):
            return v.rearrange("p (a c) -> p a c", a=2)

        def cols(a):
            return slice(a * HALF, (a + 1) * HALF)

        def tok(t):
            return slice(P * t, P * t + NT[t])

        loaded = signal("loaded", 0)
        setup = signal("setup", 0)
        setup_pe = signal("setup_pe", 0)
        setup_act = signal("setup_act", 0)
        setup_dve = signal("setup_dve", 0)
        stage[0] = 0
        x_in = signal("x_in", 32)
        y_out = signal("y_out", 32, start=16)
        stage[0] = 30
        v_step = signal("v_step", VSTEPS)
        stage[0] = 32
        fir_step = signal("fir_step", NFIR)
        diag_done = signal("diag_done", NWIDE)
        wide_ps = signal("wide_ps", NWIDE)
        wide_out = signal("wide_out", KB)
        xT_ps = signal("xT_ps", 9)
        xT_done = signal("xT_done", 9)
        tok_ps = signal("tok_ps", 1)
        tok_out = signal("tok_out", 1)
        stage[0] = 2
        mean_src = signal("mean_src", 1)
        mean_ps = signal("mean_ps", 2)
        norm_src = signal("norm_src", 3)
        norm_sq = signal("norm_sq", 3)
        norm_ps = signal("norm_ps", 3)
        norm_sd = signal("norm_sd", 4)
        norm_ms = signal("norm_ms", 1)
        norm_rc = signal("norm_rc", 4)
        norm_bc = signal("norm_bc", 4)
        norm_out = signal("norm_out", 4)
        stage[0] = 4
        qkv_ps = signal("qkv_ps", 6)
        z_done = signal("z_done", 6)
        conv_done = signal("conv_done", 6)
        silu_done = signal("silu_done", 6)
        beta_ps = signal("beta_ps", 1)
        beta_done = signal("beta_done", 1)
        l2_sq = signal("l2_sq", 1)
        l2_ps = signal("l2_ps", 1)
        l2_sd = signal("l2_sd", 1)
        l2_rc = signal("l2_rc", 1)
        l2_bc = signal("l2_bc", 1)
        qk_done = signal("qk_done", 1)
        stage[0] = 6
        kv_ps = signal("kv_ps", T)
        kv_tok = signal("kv_tok", T)
        kvb_done = signal("kvb_done", T)
        G_ps = signal("G_ps", T)
        M_done = signal("M_done", T)
        MT_ps = signal("MT_ps", T)
        MT_done = signal("MT_done", T)
        R_done = signal("R_done", 5 * T)
        sq_ps = signal("sq_ps", 4 * T)
        X_done = signal("X_done", 4 * T)
        XT_done = signal("XT_done", 3 * T)
        R_ps = signal("R_ps", 4 * T)
        uw_ps = signal("uw_ps", T)
        uw_done = signal("uw_done", T)
        at_ps = signal("at_ps", T)
        at_done = signal("at_done", T)
        w_ps = signal("w_ps", NCHUNK)
        ua_done = signal("ua_done", NCHUNK)
        S_ps = signal("S_ps", NCHUNK)
        S_done = signal("S_done", NCHUNK + 1)
        o_ps = signal("o_ps", T)
        o_done = signal("o_done", T)
        stage[0] = 8
        f_ps = signal("f_ps", T)
        f_tok = signal("f_tok", T)
        dv_sq = signal("dv_sq", T)
        dv_used = signal("dv_used", T)
        f_sq = signal("f_sq", T)
        f_used = signal("f_used", T)
        rms_in = signal("rms_in", 1)
        st_done = signal("st_done", 1)
        st_ps = signal("st_ps", 1)
        sT_done = signal("sT_done", 1)
        stage[0] = 10
        g1_ps = signal("g1_ps", 4)
        hd_done = signal("hd_done", 4)
        g2_ps = signal("g2_ps", 1)
        lg_in = signal("lg_in", 1)
        lg_exp = signal("lg_exp", 1)
        oss = signal("oss", 1)
        oss_sd = signal("oss_sd", 1)
        on_done = signal("on_done", 1)
        oT_ps = signal("oT_ps", 1)
        oT_done = signal("oT_done", 1)
        ow_ps = signal("ow_ps", 1)
        stage[0] = 12
        ck_ps = signal("ck_ps", 1)
        ck_done = signal("ck_done", 1)
        cks_ps = signal("cks_ps", 1)
        ckr_done = signal("ckr_done", 1)
        vt_ps = signal("vt_ps", 1)
        vt_done = signal("vt_done", 1)
        q_ps = signal("q_ps", QB)
        q_done = signal("q_done", QB)
        qs_ps = signal("qs_ps", QB)
        qT_done = signal("qT_done", QB + 1)
        stage[0] = 14
        s_ps = signal("s_ps", NSTEP)
        max_done = signal("max_done", NSTEP)
        exp_done = signal("exp_done", NSTEP)
        pT_ps = signal("pT_ps", NSTEP)
        pT_a = signal("pT_a", NSTEP // 2)
        pT_v = signal("pT_v", NSTEP // 2)
        y_ps = signal("y_ps", T)
        yn_done = signal("yn_done", T)
        yT_ps = signal("yT_ps", T)
        yT_done = signal("yT_done", T)
        wo_ps = signal("wo_ps", 1)
        stage[0] = 16
        gl_ps = signal("gl_ps", 1)
        gl_in = signal("gl_in", 1)
        gl_exp = signal("gl_exp", 1)
        comb_done = signal("comb_done", 1)
        cb_ps = signal("cb_ps", E)
        cb_done = signal("cb_done", E)
        stage[0] = 18
        gu_ps = signal("gu_ps", 2 * NE)
        gs_done = signal("gs_done", 2 * NE)
        gu_done = signal("gu_done", 2 * NE)
        dn_ps = signal("dn_ps", 2 * NE)
        res_done = signal("res_done", 2)
        stage[0] = 20
        rT_ps = signal("rT_ps", T)
        rT_done = signal("rT_done", T, start=1)

        block = ctx.enter_context(nc.Block())
        nloads = len(WEIGHTS) + 5

        @block.sync
        def _(sp):
            for name in WEIGHTS:
                sp.dma_start(Wt[name][:, :], weights[name]).then_inc(loaded.sem, 16)
            sp.dma_start(cst[:, :], consts).then_inc(loaded.sem, 16)
            sp.dma_start(tokws_sb, tokws.rearrange("(b p) o -> p b o", p=P)).then_inc(loaded.sem, 16)
            sp.dma_start(tokw_sb, tokw.rearrange("p (d o) -> p d o", d=D1)).then_inc(loaded.sem, 16)
            sp.dma_start(wqn_sb.rearrange("p b c -> p (b c)"), wqn).then_inc(loaded.sem, 16)
            sp.dma_start(wlat_sb.rearrange("p b l -> p (b l)"), wlat).then_inc(loaded.sem, 16)
            sp.wait_ge(setup.sem, 2)

            def load(i):
                sp.dma_start(xs.rearrange("p t i d -> p t (i d)"),
                             x[bass.ds(i, 1)].rearrange("a (t p) i d -> p (a t) (i d)", p=P)).then_inc(x_in.sem, 16)
                sp.dma_start(xt, txt[bass.ds(i, 1)].rearrange("a t c -> (a t) c")).then_inc(x_in.sem, 16)

            def store(i):
                sp.wait_ge(*rT_done(i, T))
                sp.dma_start(out[bass.ds(i, 1), 0:LI].rearrange("a (t p) c -> p (a t) c", p=P),
                             ot[:, 0:4, :]).then_inc(y_out.sem, 16)
                sp.dma_start(out[bass.ds(i, 1), LI:L].rearrange("a t c -> (a t) c"),
                             ot[0:LT, 4, :]).then_inc(y_out.sem, 16)

            sp.sem_inc(y_out.sem, y_out.start)
            load(0)
            with sp.Fori(0, nseq - 1) as i:
                sp.wait_ge(*o_done(i, T))
                load(i + 1)
                store(i)
            sp.wait_ge(*o_done(nseq - 1, T))
            load(nseq - 1)
            store(nseq - 1)
            sp.wait_ge(*x_in(nseq, 32))
            sp.wait_ge(*y_out(nseq, 0))

        @block.tensor
        def _(pe):
            mm, tr = pe.matmul, pe.transpose
            pe.wait_ge(loaded.sem, 16 * nloads)
            for b in range(4):
                for kb in range(KB):
                    mm(PS[:, kb, P * b:P * b + P], wqn_sb[:, b, P * kb:P * kb + P], wlat_sb[:, b, :],
                       start=True, stop=True)
                last = mm(PS[:, 2 + b // 2, C * (b % 2):C * (b % 2) + C], wlat_sb[:, b, :], wo[:, b, :],
                          start=True, stop=True)
            last.then_inc(setup_pe.sem, 1)
            pe.wait_ge(setup.sem, 3)

            def small(yes=True):
                if yes:
                    pe.nop(nofuse=True)

            def squares(i, n):
                pe.wait_ge(*norm_sq(i, n + 1))
                bank = (7, 2, 6)[n]
                for t in range(T):
                    for b in range(KB):
                        last = mm(PS[0:NT[t], bank, t:t + 1], sq[:, b, tok(t)], K["mean"][:, 0:1],
                                  start=b == 0, stop=b == KB - 1)
                last.then_inc(norm_ps.sem, 1)

            def spread(i, n):
                pe.wait_ge(*norm_rc(i, n + 1))
                small()
                bank = (4, 3, 5, 0)[n]
                for t in range(T):
                    n_t = NT[t]
                    last = mm(PS[:, bank + t // 4, P * (t % 4):P * (t % 4) + n_t],
                              (rt if n % 2 else rr)[0:n_t, t:t + 1].to_broadcast([n_t, P]), ident[0:n_t, 0:n_t],
                              start=True, stop=True)
                last.then_inc(norm_bc.sem, 1)

            def x_turn(i, k):
                if k >= 2:
                    pe.wait_ge(*xT_done(i, k - 1))
                bank = 3 if k % 2 else 7
                if k < 8:
                    for t in range(4):
                        last = tr(PS[:, bank, P * t:P * t + P], xs[:, t, P * (k % KB):P * (k % KB) + P, k // KB], ident)
                else:
                    small()
                    for b in range(KB):
                        last = tr(PS[:, bank, LT * b:LT * b + LT], xt[:, P * b:P * b + P], ident[0:LT, 0:LT])
                last.then_inc(xT_ps.sem, 1)

            def project_tokens(i):
                pe.wait_ge(*xT_done(i, 8))
                for m in range(KB):
                    for k in range(8):
                        last = mm(PS[:, m, :], tokwT[:, k, P * m:P * m + P], xT[:, k, :], start=k == 0, stop=k == 7)
                last.then_inc(tok_ps.sem, 1)

            def mean(i, n, src, bank):
                for a in range(2):
                    for b in range(KB):
                        last = mm(PS[:, bank + a, 0:HALF], K["mean"], src[:, b, cols(a)], start=b == 0, stop=b == KB - 1)
                last.then_inc(mean_ps.sem, 1)

            pe.wait_ge(*x_in(0, 32))
            for k in range(9):
                x_turn(0, k)
            project_tokens(0)
            pe.wait_ge(*tok_out(0, 1))
            mean(0, 0, hnext, 4)
            squares(0, 0)
            spread(0, 0)

            with pe.Fori(0, nseq) as i:
                pe.wait_ge(*norm_out(i, 1))
                for n, m in enumerate(QKV):
                    if n >= 2:
                        pe.wait_ge(*z_done(i, n - 1))
                    for a in range(2):
                        for b in range(KB):
                            last = mm(PS[:, 2 + 2 * (n % 2) + a, 0:HALF], wqkv[:, b, P * m:P * m + P],
                                      hn[:, b, cols(a)], start=b == 0, stop=b == KB - 1)
                    last.then_inc(qkv_ps.sem, 1)
                pe.wait_ge(*rT_done(i, 0))
                for t in range(T):
                    for b in range(KB):
                        last = mm(PS[0:NT[t], 6, GH * t:GH * t + GH], hn[:, b, tok(t)], bw[:, b, :],
                                  start=b == 0, stop=b == KB - 1)
                last.then_inc(beta_ps.sem, 1)
                pe.wait_ge(*silu_done(i, KB))
                done = [0]

                def wide(upto):
                    for w in range(done[0], upto):
                        b, tap = w // WP, w % WP
                        pe.wait_ge(*diag_done(i, w + 1))
                        if tap == 0 and b:
                            pe.wait_ge(*wide_out(i, b))
                        for a in range(2):
                            src = PAD - tap + HALF * a
                            last = mm(PS[:, a, 0:HALF], diag[:, w % 8, :], vp[:, b, src:src + HALF],
                                      start=tap == 0, stop=tap == WP - 1)
                        last.then_inc(wide_ps.sem, 1)
                    done[0] = max(done[0], upto)

                wide(WIDE_AT[0])
                pe.wait_ge(*l2_sq(i, 1))
                for t in range(T):
                    for m in range(4):
                        last = mm(PS[0:NT[t], 7, 8 * t + 2 * m:8 * t + 2 * m + 2], sq4[:, m, tok(t)],
                                  K["heads"][:, 0:P:GD], start=True, stop=True)
                last.then_inc(l2_ps.sem, 1)
                wide(WIDE_AT[1])
                pe.wait_ge(*l2_rc(i, 1))
                pe.wait_ge(*beta_done(i, 1))
                small()
                for t in range(T):
                    n = NT[t]
                    for m in range(4):
                        dst = PS[:, 2 + m, P * t:P * t + P] if t < 4 else PS[:, 6, LT * m:LT * m + LT]
                        one = rlx[:, t, P * m:P * m + P] if t < 4 else rly[0:LT, P * m:P * m + P]
                        last = mm(dst, one, ident[0:n, 0:n], start=True, stop=True)
                last.then_inc(l2_bc.sem, 1)
                wide(WIDE_AT[2])
                pe.wait_ge(*qk_done(i, 1))
                for t in range(T):
                    if t >= 2:
                        pe.wait_ge(*kv_tok(i, t - 1))
                    for b in range(KB):
                        tr(PS[0:NT[t], 2 + t % 2, P * b:P * b + P], qk[:, 2 + b, tok(t)], ident)
                        last = tr(PS[0:NT[t], 2 + t % 2, C + P * b:C + P * b + P],
                                  vp[:, b, PAD + P * t:PAD + P * t + NT[t]], ident)
                    last.then_inc(kv_ps.sem, 1)
                pe.wait_ge(*kv_tok(i, T))
                for part, (what, t, k) in enumerate(DELTA):
                    n = NT[t]
                    if what == "inverse":
                        if k == 0:
                            if t:
                                pe.wait_ge(*uw_done(i, t))
                            small(t == 4)
                            for hh in range(GH):
                                kh = qk[GD * (hh % 2):GD * (hh % 2) + GD, 2 + hh // 2, tok(t)]
                                last = mm(PS[0:n, 2 + hh % 2, P * (hh // 2):P * (hh // 2) + n], kh, kh,
                                          start=True, stop=True)
                            last.then_inc(G_ps.sem, 1)
                            for hh in range(GH):
                                kh = qk[GD * (hh % 2):GD * (hh % 2) + GD, 2 + hh // 2, tok(t)]
                                qh = qk[GD * (hh % 2):GD * (hh % 2) + GD, hh // 2, tok(t)]
                                last = mm(PS[0:n, 4 + 2 * (hh % 2), P * (hh // 2):P * (hh // 2) + n], kh, qh,
                                          start=True, stop=True)
                            last.then_inc(at_ps.sem, 1)
                        elif k == 1:
                            pe.wait_ge(*M_done(i, t + 1))
                            small(t == 4)
                            for hh in range(GH):
                                last = tr(PS[0:n, 3, P * hh:P * hh + n], X[0:n, hh, 0:n], ident[0:n, 0:n])
                            last.then_inc(MT_ps.sem, 1)
                        elif k < 7:
                            lv = k - 2
                            if lv:
                                pe.wait_ge(*X_done(i, 4 * t + lv))
                                pe.wait_ge(*R_done(i, 5 * t + lv))
                                small(t == 4)
                                for hh in range(GH):
                                    last = mm(PS[0:n, 6, P * hh:P * hh + n], X[0:n, hh, 0:n], R[0:n, hh, 0:n],
                                              start=True, stop=True)
                                last.then_inc(R_ps.sem, 1)
                            if lv < 4:
                                if lv:
                                    pe.wait_ge(*XT_done(i, 3 * t + lv))
                                else:
                                    pe.wait_ge(*MT_done(i, t + 1))
                                    pe.wait_ge(*at_done(i, t + 1))
                                small(t == 4)
                                for hh in range(GH):
                                    last = mm(PS[0:n, 4, P * hh:P * hh + n], XT[0:n, hh, 0:n], X[0:n, hh, 0:n],
                                              start=True, stop=True)
                                    if lv < 3:
                                        last = mm(PS[0:n, 3, P * hh:P * hh + n], X[0:n, hh, 0:n], XT[0:n, hh, 0:n],
                                                  start=True, stop=True)
                                last.then_inc(sq_ps.sem, 1)
                        else:
                            pe.wait_ge(*R_done(i, 5 * t + 5))
                            pe.wait_ge(*kvb_done(i, t + 1))
                            small(t == 4)
                            for hh in range(GH):
                                mm(PS[0:n, 2, GD * hh:GD * hh + GD], R[0:n, hh, 0:n], vbt[0:n, GD * hh:GD * hh + GD],
                                   start=True, stop=True)
                                r0 = GD * (hh % 2)
                                last = mm(PS[r0:r0 + GD, 3, P * (hh // 2):P * (hh // 2) + n],
                                          kbt[0:n, GD * hh:GD * hh + GD], R[0:n, hh, 0:n], start=True, stop=True)
                            last.then_inc(uw_ps.sem, 1)
                    else:
                        j = k // 2
                        c = 4 * t + j
                        rows = slice(CH * j, CH * j + CH)
                        if k % 2 == 0:
                            if j == 0:
                                pe.wait_ge(*uw_done(i, t + 1))
                                if t:
                                    pe.wait_ge(*o_done(i, t))
                            pe.wait_ge(*S_done(i, c + 1))
                            for side, src in ((0, wT), (C, qk)):
                                for p in range(2):
                                    last = mm(PS[rows, 5, side + P * p:side + P * p + P], src[:, p, CH * c:CH * c + CH],
                                              Sb[:, p, :], start=side == 0 and p == 0, stop=side == 0,
                                              skip_group_check=True, tile_position=(0, CH * j))
                            last.then_inc(w_ps.sem, 1)
                        else:
                            pe.wait_ge(*ua_done(i, c + 1))
                            for p in range(2):
                                last = mm(PS[:, 7, P * p:P * p + P], ktok[rows, t, P * p:P * p + P],
                                          u[rows, t, P * p:P * p + P], start=c == 0 and p == 0, stop=True,
                                          skip_group_check=True, tile_position=(CH * j, 0))
                            last.then_inc(S_ps.sem, 1)
                            if j == n // CH - 1:
                                for hh in range(GH):
                                    last = mm(PS[0:n, 5, C + GD * hh:C + GD * hh + GD], atT[0:n, t % 2, hh, 0:n],
                                              u[0:n, t, GD * hh:GD * hh + GD], start=False, stop=True,
                                              skip_group_check=True)
                                last.then_inc(o_ps.sem, 1)
                    wide(wide_after(part))
                pe.wait_ge(*fir_step(i, NFIR))
                for t in range(T):
                    if t >= 2:
                        pe.wait_ge(*f_tok(i, t - 1))
                    for f in range(3):
                        for b in range(KB):
                            dst = C * f + P * b
                            last = tr(PS[0:NT[t], 2 * (t % 2) + dst // 512, dst % 512:dst % 512 + P],
                                      fir[:, f, b, tok(t)], ident)
                    last.then_inc(f_ps.sem, 1)
                def g1_bank(m):
                    return (6, 0, 2, 6)[m]

                def gate_hn(m):
                    for a in range(2):
                        for b in range(KB):
                            mm(PS[:, g1_bank(m) + a, 0:HALF], g1[:, b, P * m:P * m + P], hn[:, b, cols(a)],
                               start=b == 0, stop=False)

                gate_hn(0)
                pe.wait_ge(*f_tok(i, T))
                gate_hn(1)
                gate_hn(2)
                pe.wait_ge(*st_done(i, 1))
                pe.wait_ge(*o_done(i, T))
                small()
                for t in range(T):
                    last = tr(PS[0:60, 4 + t // 4, P * (t % 4):P * (t % 4) + NT[t]], st[0:NT[t], 60 * t:60 * t + 60],
                              ident[0:NT[t], 0:NT[t]])
                last.then_inc(st_ps.sem, 1)
                pe.wait_ge(*sT_done(i, 1))
                for m in range(4):
                    if m == 3:
                        pe.wait_ge(*hd_done(i, 1))
                        gate_hn(3)
                    for a in range(2):
                        last = mm(PS[:, g1_bank(m) + a, 0:HALF], g1[0:60, 2, P * m:P * m + P], sT[:, cols(a)],
                                  start=False, stop=True)
                    last.then_inc(g1_ps.sem, 1)
                pe.wait_ge(*hd_done(i, 4))
                for t in range(T):
                    for b in range(4):
                        last = mm(PS[0:NT[t], 4, 20 * t:20 * t + 20], hd[:, b, tok(t)], g2[:, b, :],
                                  start=b == 0, stop=b == 3)
                last.then_inc(g2_ps.sem, 1)
                pe.wait_ge(*x_in(i + 1, 32))
                for k in range(9):
                    x_turn(i + 1, k)
                project_tokens(i + 1)
                pe.wait_ge(*on_done(i, 1))
                for t in range(T):
                    for b in range(KB):
                        dst = PS[:, 4 + b, P * t:P * t + P] if t < 4 else PS[:, 6, LT * b:LT * b + LT]
                        last = tr(dst, o[0:NT[t], t, P * b:P * b + P], ident[0:NT[t], 0:NT[t]])
                last.then_inc(oT_ps.sem, 1)
                pe.wait_ge(*oT_done(i, 1))
                pe.wait_ge(*xT_done(i + 1, 9))
                for m in range(KB):
                    for a in range(2):
                        for b in range(KB):
                            last = mm(PS[:, 2 + 4 * m + a, 0:HALF], ow[:, b, P * m:P * m + P], oT[:, b, cols(a)],
                                      start=b == 0, stop=b == KB - 1)
                last.then_inc(ow_ps.sem, 1)
                pe.wait_ge(*mean_src(i, 1))
                mean(i, 1, h, 4)
                squares(i, 1)
                spread(i, 1)
                spread(i, 2)
                pe.wait_ge(*norm_out(i, 3))
                pe.wait_ge(*tok_out(i + 1, 1))
                for a in range(2):
                    for b in range(KB):
                        last = mm(PS[:, a, 0:HALF], wkva[:, b, :], x1[:, b, cols(a)], start=b == 0, stop=b == KB - 1)
                last.then_inc(ck_ps.sem, 1)
                for t in range(T):
                    for b in range(KB):
                        last = mm(PS[0:NT[t], 2, NOPE * t:NOPE * t + NOPE], x1[:, b, tok(t)], wkva[:, b, 0:NOPE],
                                  start=b == 0, stop=b == KB - 1)
                last.then_inc(vt_ps.sem, 1)
                pe.wait_ge(*ck_done(i, 1))
                pe.wait_ge(*norm_out(i, 3))
                for a in range(2):
                    last = mm(PS[:, 4 + a, 0:HALF], K["swap"], ck[:, cols(a)], start=True, stop=True)
                last.then_inc(cks_ps.sem, 1)
                for m in range(QB + 1):
                    if m < QB:
                        if m >= 2:
                            pe.wait_ge(*q_done(i, m - 1))
                        elif m == 1:
                            pe.wait_ge(*vt_done(i, 1))
                        for a in range(2):
                            for b in range(KB):
                                last = mm(PS[:, 2 * (m % 2) + a, 0:HALF], wq[:, b, P * m:P * m + P], x1[:, b, cols(a)],
                                          start=b == 0, stop=b == KB - 1)
                        last.then_inc(q_ps.sem, 1)
                    if m:
                        r = m - 1
                        pe.wait_ge(*q_done(i, r + 1))
                        if r == 0:
                            pe.wait_ge(*ckr_done(i, 1))
                        if r >= 2:
                            pe.wait_ge(*qT_done(i, r - 1))
                        for a in range(2):
                            last = mm(PS[:, 4 + 2 * (r % 2) + a, 0:HALF], K["swap"], qraw[:, r % 2, cols(a)],
                                      start=True, stop=True)
                        last.then_inc(qs_ps.sem, 1)
                pe.wait_ge(*qT_done(i, QB))
                def copied(n):
                    return (pT_v if n % 2 else pT_a)(i, n // 2 + 1)

                def scores(n):
                    t, h0, g = STEPS[n]
                    if t < 4:
                        if n >= 4:
                            pe.wait_ge(*exp_done(i, n - 3))
                        w = P * (t + 1)
                        for r in range(g):
                            hh = head_at((h0 + r) // 4, (h0 + r) % 4)
                            last = mm(PS[:, n % 4, w * r:w * r + w], qT[:, hh // 2, tok(t)], kz[:, hh % 2, 0:w],
                                      start=True, stop=True)
                    else:
                        if h0 == 0:
                            pe.wait_ge(*qT_done(i, QB + 1))
                        pe.wait_ge(*exp_done(i, n - 1 if h0 else n - 2))
                        for c0, c1 in ((0, 512), (512, L)):
                            last = mm(PS[:, 2 * (n % 2) + c0 // 512, 0:c1 - c0], qlast[:, P * (h0 // 2):P * (h0 // 2) + P],
                                      kz[:, h0 % 2, c0:c1], start=True, stop=True)
                    last.then_inc(s_ps.sem, 1)

                def turn(n):
                    t, h0, g = STEPS[n]
                    pe.wait_ge(*exp_done(i, n + 1))
                    if n >= 2:
                        pe.wait_ge(*copied(n - 2))
                    if t == 4:
                        pe.wait_ge(*copied(n - 1))
                    for k in range(g * (t + 1)):
                        bank = 4 + n % 2 if t < 4 else 4 + k // 4
                        src = pr[:, n % 3, P * k:P * k + (P if t < 4 else NT[k])]
                        last = tr(PS[0:P if t < 4 else NT[k], bank, P * (k % 4):P * (k % 4) + P], src, ident)
                    last.then_inc(pT_ps.sem, 1)

                def times_v(n):
                    t, h0, g = STEPS[n]
                    pe.wait_ge(*copied(n))
                    if n == FIRST[t] and t >= 2:
                        pe.wait_ge(*yT_done(i, t - 1))
                    for r in range(g):
                        for k in range(t + 1):
                            at = P * (r * (t + 1) + k)
                            last = mm(PS[:, 6 + t % 2, NOPE * (h0 + r):NOPE * (h0 + r) + NOPE],
                                      prT[0:NT[k], n % 2, at:at + P], vt[0:NT[k], k, :], start=k == 0, stop=k == t)
                    if n + 1 == NSTEP or STEPS[n + 1][0] != t:
                        last.then_inc(y_ps.sem, 1)

                def y_turn(t):
                    pe.wait_ge(*yn_done(i, t + 1))
                    for b in range(4 if t < 4 else 1):
                        last = tr(PS[:, 6 + t % 2, P * b:P * b + P],
                                  yn[:, 4 * b:4 * b + 4, :].rearrange("p h d -> p (h d)"), ident)
                    last.then_inc(yT_ps.sem, 1)

                for n in range(3):
                    scores(n)
                for n in range(NSTEP + 1):
                    if n + 3 < NSTEP:
                        scores(n + 3)
                    if n < NSTEP:
                        turn(n)
                    if n >= 1:
                        times_v(n - 1)
                    if n - 3 in FIRST[1:]:
                        y_turn(FIRST.index(n - 3) - 1)
                y_turn(T - 1)
                pe.wait_ge(*yT_done(i, T))
                for m in range(KB):
                    for a in range(2):
                        for b in range(4):
                            last = mm(PS[:, 2 * m + a, 0:HALF], wo[:, b, P * m:P * m + P], yT[:, b, cols(a)],
                                      start=b == 0, stop=b == 3)
                last.then_inc(wo_ps.sem, 1)
                mean(i + 1, 0, hnext, 4)
                squares(i, 2)
                spread(i, 3)
                squares(i + 1, 0)
                pe.wait_ge(*norm_out(i, 4))
                for t in range(T):
                    for b in range(KB):
                        last = mm(PS[0:NT[t], 6, E * t:E * t + E], xn[:, b, tok(t)], wgate[:, b, :],
                                  start=b == 0, stop=b == KB - 1)
                last.then_inc(gl_ps.sem, 1)
                spread(i + 1, 0)
                pe.wait_ge(*comb_done(i, 1))
                for e in range(E):
                    if e >= 4:
                        pe.wait_ge(*cb_done(i, e - 3))
                    for t in range(4):
                        last = mm(PS[:, e % 4, tok(t)], gl[:, t, e:e + 1].to_broadcast([P, P]), ident,
                                  start=True, stop=True)
                    if e == E - 1:
                        for r in range(E):
                            last = mm(PS[:, 6, LT * r:LT * r + LT], gl[0:LT, 4, r:r + 1].to_broadcast([LT, P]),
                                      ident[0:LT, 0:LT], start=True, stop=True)
                    last.then_inc(cb_ps.sem, 1)
                pe.wait_ge(*cb_done(i, E))
                def result_turn(t):
                    if t == 4:
                        pe.wait_ge(*rT_done(i, 1))
                    for b in range(KB):
                        last = tr(PS[0:NT[t], (6, 7, 0, 1, 6)[t], P * b:P * b + P], h[:, b, tok(t)], ident)
                    last.then_inc(rT_ps.sem, 1)

                units = [(a, e) for a in range(2) for e in range(NE)]
                for n in range(len(units) + 1):
                    if n < len(units):
                        a, e = units[n]
                        if n >= 2:
                            pe.wait_ge(*gu_done(i, n - 1))
                        for w, bank in ((wg, 2 * (n % 2)), (wu, 2 * (n % 2) + 1)):
                            for b in range(KB):
                                last = mm(PS[:, bank, 0:HALF], w[:, e, b, :], xn[:, b, cols(a)],
                                          start=b == 0, stop=b == KB - 1)
                        last.then_inc(gu_ps.sem, 1)
                    if n == NE + 1:
                        pe.wait_ge(*norm_out(i + 1, 1))
                    if n == NE + 4:
                        pe.wait_ge(*res_done(i, 1))
                        result_turn(0)
                        result_turn(1)
                    if n:
                        a, e = units[n - 1]
                        pe.wait_ge(*gu_done(i, n))
                        for m in range(KB):
                            last = mm(PS[:, 6 - 2 * a + m, 0:HALF], wd[:, e, P * m:P * m + P], gu[:, (n - 1) % 2, :],
                                      start=e == 0, stop=e == NE - 1)
                        last.then_inc(dn_ps.sem, 1)
                pe.wait_ge(*res_done(i, 2))
                for t in range(2, T):
                    result_turn(t)

        @block.scalar
        def _(act):
            A = act.activation
            act.wait_ge(loaded.sem, 16 * nloads)
            act.wait_ge(setup.sem, 2)
            for hh in range(GH):
                A(gk[:, 20 + 5 * hh:25 + 5 * hh], Wt["ltemp"][:, hh:hh + 1].to_broadcast([P, 5]), ACT.Exp, scale=-1.0)
                last = A(gk[:, 40 + 5 * hh:45 + 5 * hh], Wt["floor"][:, hh:hh + 1].to_broadcast([P, 5]), ACT.Sigmoid)
            last.then_inc(setup_act.sem, 1)

            act.sem_inc(rT_done.sem, rT_done.start)

            def norm(i, n, src):
                act.wait_ge(*norm_src(i, n + 1))
                A(sq, src, ACT.Square).then_inc(norm_sq.sem, 1)

            def root(i, n):
                act.wait_ge(*norm_ps(i, n + 1))
                bank, r = (7, 2, 6)[n], rt if n else rr
                A(r[:, 0:4], PS[:, bank, 0:4], ACT.Sqrt, bias=K["eps5"])
                A(r[0:LT, 4:5], PS[0:LT, bank, 4:5], ACT.Sqrt, bias=K["eps5"][0:LT]).then_inc(norm_sd.sem, 1)

            def x_copy(i, k):
                act.wait_ge(*xT_ps(i, k + 1))
                bank = 3 if k % 2 else 7
                if k < 8:
                    last = A(xT[:, k, :], PS[:, bank, :], ACT.Copy)
                else:
                    last = A(hnext[:, :, 512:L], PS[:, bank, 0:2 * LT].rearrange("p (b l) -> p b l", b=2), ACT.Copy)
                last.then_inc(xT_done.sem, 1)

            def tokens_copy(i):
                act.wait_ge(*tok_ps(i, 1))
                A(hnext[:, :, 0:512], PS[:, 0:2, :], ACT.Copy).then_inc(tok_out.sem, 1)

            prepared = [0]

            def prepare(function):
                A(scrap[:, prepared[0]:prepared[0] + 1], K["eps5"], function)
                prepared[0] += 1

            for k in range(9):
                x_copy(0, k)
            tokens_copy(0)
            norm(0, 0, hc)
            root(0, 0)
            with act.Fori(0, nseq) as i:
                prepare(ACT.Silu)
                made = [0]

                def diagonals(upto):
                    for w in range(made[0], min(upto, NWIDE)):
                        if w >= 8:
                            act.wait_ge(*wide_ps(i, w - 7))
                        col = sum(FIRS) - 1 - w % WP
                        A(diag[:, w % 8, :], ident, ACT.Copy,
                          scale=firw[:, w // WP, col:col + 1]).then_inc(diag_done.sem, 1)
                    made[0] = max(made[0], upto)

                for n in range(7):
                    if n < 6:
                        act.wait_ge(*qkv_ps(i, n + 1))
                        A(halves(z[:, QKV[n], 3:3 + L]), pair(2 + 2 * (n % 2)), ACT.Copy).then_inc(z_done.sem, 1)
                    if n:
                        m = QKV[n - 1]
                        act.wait_ge(*conv_done(i, n))
                        dst = qk[:, m, :] if m < 4 else vp[:, m - 4, PAD:PAD + L]
                        A(dst, cv[:, (n - 1) % 2, :], ACT.Silu).then_inc(silu_done.sem, 1)
                        if n >= 3:
                            diagonals(4 * (n - 2))
                act.wait_ge(*beta_ps(i, 1))
                A(beta[:, 0:4, :], PS[:, 6, 0:16].rearrange("p (t h) -> p t h", t=4), ACT.Sigmoid)
                A(beta[0:LT, 4, :], PS[0:LT, 6, 16:20], ACT.Sigmoid).then_inc(beta_done.sem, 1)
                act.wait_ge(*silu_done(i, 6))
                A(sq4, qk, ACT.Square).then_inc(l2_sq.sem, 1)
                prepare(ACT.Sqrt)
                diagonals(WIDE_AT[0] + 2)
                act.wait_ge(*l2_ps(i, 1))
                A(rl[:, 0:32], PS[:, 7, 0:32], ACT.Sqrt, bias=K["eps6"])
                A(rl[0:LT, 32:40], PS[0:LT, 7, 32:40], ACT.Sqrt, bias=K["eps6"][0:LT]).then_inc(l2_sd.sem, 1)
                diagonals(WIDE_AT[2] + 6)
                act.wait_ge(*y_out(i, 0))
                A(Sb, Sb, ACT.Copy, scale=0.0).then_inc(S_done.sem, 1)
                for t in range(T):
                    n = NT[t]
                    act.wait_ge(*kv_ps(i, t + 1))
                    A(ktok[0:n, t, :], PS[0:n, 2 + t % 2, 0:C], ACT.Copy)
                    A(F[0:n, t, 4, :], PS[0:n, 2 + t % 2, C:2 * C], ACT.Copy).then_inc(kv_tok.sem, 1)
                for part, (what, t, k) in enumerate(DELTA):
                    n = NT[t]
                    if what == "inverse":
                        if k == 1:
                            act.wait_ge(*MT_ps(i, t + 1))
                            A(XT[0:n, :, 0:n], PS[0:n, 3, :].rearrange("p (h n) -> p h n", h=GH)[:, :, 0:n],
                              ACT.Copy).then_inc(MT_done.sem, 1)
                        elif 2 <= k <= 4:
                            if k == 2:
                                act.wait_ge(*R_done(i, 5 * t + 1))
                            act.wait_ge(*sq_ps(i, 4 * t + k - 1))
                            A(XT[0:n, :, 0:n], PS[0:n, 3, :].rearrange("p (h n) -> p h n", h=GH)[:, :, 0:n],
                              ACT.Copy).then_inc(XT_done.sem, 1)
                        elif k == 7:
                            act.wait_ge(*uw_ps(i, t + 1))
                            A(u[0:n, t, :], PS[0:n, 2, 0:C], ACT.Copy)
                            A(wT[:, :, tok(t)], PS[:, 3, 0:C].rearrange("p (b n) -> p b n", b=2)[:, :, 0:n],
                              ACT.Copy).then_inc(uw_done.sem, 1)
                    elif k % 2:
                        c = 4 * t + k // 2
                        act.wait_ge(*S_ps(i, c + 1))
                        for q in range(2):
                            r = slice(GD * q, GD * q + GD)
                            last = A(Sb[r, :, r], PS[r, 7, 0:C].rearrange("p (b n) -> p b n", b=2)[:, :, r], ACT.Copy)
                        last.then_inc(S_done.sem, 1)
                        if k // 2 == n // CH - 1:
                            act.wait_ge(*o_ps(i, t + 1))
                            A(F[0:n, t, 3, :], PS[0:n, 5, C:2 * C], ACT.Copy).then_inc(o_done.sem, 1)
                            act.wait_ge(*o_done(i, t + 1))
                            if t:
                                act.wait_ge(*dv_used(i, t))
                            A(dvsq[0:n, :], F[0:n, t, 3:5, :].rearrange("p k c -> p (k c)"), ACT.Square
                              ).then_inc(dv_sq.sem, 1)
                    diagonals(wide_after(part) + 6)
                for t in range(T):
                    n = NT[t]
                    act.wait_ge(*f_ps(i, t + 1))
                    A(F[0:n, t, 0:2, :], PS[0:n, 2 * (t % 2), :].rearrange("p (k c) -> p k c", k=2), ACT.Copy)
                    A(F[0:n, t, 2, :], PS[0:n, 2 * (t % 2) + 1, 0:C], ACT.Copy).then_inc(f_tok.sem, 1)
                    act.wait_ge(*f_tok(i, t + 1))
                    if t:
                        act.wait_ge(*f_used(i, t))
                    A(fsq[0:n, :], F[0:n, t, 0:3, :].rearrange("p k c -> p (k c)"), ACT.Square).then_inc(f_sq.sem, 1)
                act.wait_ge(*rms_in(i, 1))
                A(st.rearrange("p (g s h) -> p g s h", s=3, h=4)[:, :, 1, :], ms.rearrange("p (g h) -> p g h", h=4),
                  ACT.Sqrt).then_inc(st_done.sem, 1)
                prepare(ACT.Gelu)
                act.wait_ge(*st_ps(i, 1))
                A(sT[:, 0:512], PS[0:60, 4, :], ACT.Copy)
                A(sT[:, 512:L], PS[0:60, 5, 0:LT], ACT.Copy).then_inc(sT_done.sem, 1)
                for m in range(4):
                    act.wait_ge(*g1_ps(i, m + 1))
                    A(halves(hd[:, m, :]), pair((6, 0, 2, 6)[m]), ACT.Gelu, bias=Wt["g1b"][:, m:m + 1]).then_inc(hd_done.sem, 1)
                prepare(ACT.Exp)
                act.wait_ge(*lg_in(i, 1))
                A(lg, lg, ACT.Exp).then_inc(lg_exp.sem, 1)
                prepare(ACT.Sqrt)
                for k in range(8):
                    x_copy(i + 1, k)
                act.wait_ge(*oss(i, 1))
                A(s20, m20, ACT.Sqrt, bias=K["eps5"]).then_inc(oss_sd.sem, 1)
                act.wait_ge(*oT_ps(i, 1))
                for b in range(KB):
                    A(oT[:, b, 0:512], PS[:, 4 + b, :], ACT.Copy)
                A(oT[:, :, 512:L], PS[:, 6, 0:2 * LT].rearrange("p (b l) -> p b l", b=2), ACT.Copy).then_inc(oT_done.sem, 1)
                x_copy(i + 1, 8)
                tokens_copy(i + 1)
                norm(i, 1, hc)
                root(i, 1)
                act.wait_ge(*norm_ms(i, 1))
                A(rr, rr, ACT.Sqrt, bias=K["eps5"]).then_inc(norm_sd.sem, 1)
                prepare(ACT.Exp)
                act.wait_ge(*ck_ps(i, 1))
                A(halves(ck), pair(0), ACT.Copy).then_inc(ck_done.sem, 1)
                act.wait_ge(*vt_ps(i, 1))
                A(vt[:, 0:4, :], PS[:, 2, 0:4 * NOPE].rearrange("p (t c) -> p t c", t=4), ACT.Copy)
                A(vt[0:LT, 4, :], PS[0:LT, 2, 4 * NOPE:5 * NOPE], ACT.Copy).then_inc(vt_done.sem, 1)
                for m in range(QB):
                    act.wait_ge(*q_ps(i, m + 1))
                    if m >= 2:
                        act.wait_ge(*qT_done(i, m - 1))
                    A(halves(qraw[:, m % 2, :]), pair(2 * (m % 2)), ACT.Copy, scale=AD ** -0.5).then_inc(q_done.sem, 1)

                def soften(n):
                    t, h0, g = STEPS[n]
                    act.wait_ge(*max_done(i, n + 1))
                    if n >= 3:
                        act.wait_ge(*pT_ps(i, n - 2))
                    if n == FIRST[t] and t >= 2:
                        act.wait_ge(*yn_done(i, t - 1))
                    for r in range(g):
                        if t < 4:
                            w = P * (t + 1)
                            src = PS[:, n % 4, w * r:w * r + w]
                        else:
                            w = L
                            src = PS[:, 2 * (n % 2):2 * (n % 2) + 2, :].rearrange("p a c -> p (a c)")[:, 0:w]
                        last = A(pr[:, n % 3, w * r:w * r + w], src, ACT.Exp, bias=nmax[:, t % 2, h0 + r:h0 + r + 1],
                                 accum_out=rsum[:, t % 2, h0 + r:h0 + r + 1])
                    last.then_inc(exp_done.sem, 1)

                def y_copy(t):
                    act.wait_ge(*yT_ps(i, t + 1))
                    A(yT[:, :, tok(t)], PS[:, 6 + t % 2, 0:4 * NT[t]].rearrange("p (b n) -> p b n", b=4),
                      ACT.Copy).then_inc(yT_done.sem, 1)

                soften(0)
                for n in range(NSTEP):
                    if n + 1 < NSTEP:
                        soften(n + 1)
                    if n % 2 == 0:
                        t, h0, g = STEPS[n]
                        act.wait_ge(*pT_ps(i, n + 1))
                        if t < 4:
                            A(prT[:, 0, 0:P * (t + 1) * g], PS[:, 4, 0:P * (t + 1) * g], ACT.Copy).then_inc(pT_a.sem, 1)
                        else:
                            A(prT[:, 0, 0:512], PS[:, 4, :], ACT.Copy)
                            A(prT[0:LT, 0, 512:640], PS[0:LT, 5, 0:P], ACT.Copy).then_inc(pT_a.sem, 1)
                    if n - 5 in FIRST[1:]:
                        y_copy(FIRST.index(n - 5) - 1)
                y_copy(T - 2)
                prepare(ACT.Sqrt)
                y_copy(T - 1)
                norm(i, 2, x2)
                root(i, 2)
                norm(i + 1, 0, hc)
                root(i + 1, 0)
                prepare(ACT.Exp)
                act.wait_ge(*gl_in(i, 1))
                A(gl, gl, ACT.Exp).then_inc(gl_exp.sem, 1)
                prepare(ACT.Silu)
                for e in range(E):
                    act.wait_ge(*cb_ps(i, e + 1))
                    last = A(cb[:, e, 0:512], PS[:, e % 4, :], ACT.Copy)
                    if e == E - 1:
                        last = A(cb[:, :, 512:L], PS[:, 6, 0:E * LT].rearrange("p (e l) -> p e l", e=E), ACT.Copy)
                    last.then_inc(cb_done.sem, 1)
                def result_copy(t):
                    n = NT[t]
                    act.wait_ge(*rT_ps(i, t + 1))
                    A(ot[0:n, t, :], PS[0:n, (6, 7, 0, 1, 6)[t], 0:C], ACT.Copy).then_inc(rT_done.sem, 1)

                for n in range(2 * NE):
                    act.wait_ge(*gu_ps(i, n + 1))
                    if n >= 2:
                        act.wait_ge(*gu_done(i, n - 1))
                    A(gs[:, n % 2, :], PS[:, 2 * (n % 2), 0:HALF], ACT.Silu).then_inc(gs_done.sem, 1)
                    if n in (NE + 5, NE + 6):
                        result_copy(n - NE - 5)
                for t in range(2, T):
                    result_copy(t)

        @block.vector
        def _(dve):
            steps = [0]

            def link(i, ins):
                ins.then_inc(v_step.sem, 1)
                steps[0] += 1
                dve.wait_ge(*v_step(i, steps[0]))

            TT, TS, STT, RED, CP = (dve.tensor_tensor, dve.tensor_scalar, dve.scalar_tensor_tensor,
                                    dve.tensor_reduce, dve.tensor_copy)

            dve.wait_ge(loaded.sem, 16 * nloads)
            dve.memset(hc, 0.0).then_inc(setup.sem, 1)
            for k in range(8):
                d, b = k // KB, k % KB
                TT(tokwT[:, k, :], tokws_sb[:, b, :], tokw_sb[:, d, :], ALU.mult)
            dve.wait_ge(setup_pe.sem, 1)
            wq6 = Wt["wq"][:, :].rearrange("p (k g b p2 d) -> p k g b p2 d", k=KB, g=2, b=4, p2=2)
            for b in range(4):
                for kb in range(KB):
                    CP(wq6[:, kb, :, b, :, 0:NOPE],
                       PS[:, kb, P * b:P * b + P].rearrange("p (g p2 d) -> p g p2 d", g=2, p2=2))
                CP(wo[:, b, :], PS[:, 2 + b // 2, C * (b % 2):C * (b % 2) + C])
            dve.memset(kz, 0.0)
            TS(ow, ow, Wt["onorm"][:, :], None, ALU.mult)
            dve.memset(rt, 1.0)
            dve.memset(rr, 1.0)
            dve.memset(gfloor[:, :], 0.0)
            last = CP(gk[:, 0:20], Wt["g2b"][:, :])
            last.then_inc(setup_dve.sem, 1)
            dve.wait_ge(setup_dve.sem, 1)
            dve.memset(arena[:, :], 0.0).then_inc(setup.sem, 1)
            g3 = gk[:, 0:20].rearrange("p (h k) -> p h k", k=5)
            TT(g3[:, :, 4], g3[:, :, 4], Wt["vbias"][:, :], ALU.add)
            dve.wait_ge(setup_act.sem, 1)
            f3 = gfloor[:, :].rearrange("p (h k) -> p h k", k=5)
            s3 = gk[:, 40:60].rearrange("p (h k) -> p h k", k=5)
            CP(f3[:, :, 0:4], s3[:, :, 0:4]).then_inc(setup_dve.sem, 1)
            dve.wait_ge(setup_dve.sem, 2)
            TS(gk[:, 40:60], gk[:, 40:60], -4.0, 1.0, ALU.mult, ALU.add).then_inc(setup.sem, 1)

            def centre(i, n, src, bank):
                dve.wait_ge(*mean_ps(i, n + 1))
                for b in range(KB):
                    last = TT(halves(hc[:, b, :]), halves(src[:, b, :]), pair(bank), ALU.subtract)
                last.then_inc(norm_src.sem, 1)

            def one_over(i, n):
                r = rt if n else rr
                dve.wait_ge(*norm_sd(i, n + 1))
                return dve.reciprocal(r, r)

            def scaled(i, n, src, dst, weight=None):
                dve.wait_ge(*norm_bc(i, n + 1))
                bank = (4, 3, 5, 0)[n]
                for b in range(KB):
                    for k, s in ((0, slice(0, 512)), (1, slice(512, L))):
                        one = PS[:, bank + k, 0:s.stop - s.start]
                        if weight is None:
                            last = TT(dst[:, b, s], src[:, b, s], one, ALU.mult)
                        else:
                            last = STT(dst[:, b, s], src[:, b, s], weight[:, b:b + 1], one, ALU.mult, ALU.mult)
                last.then_inc(norm_out.sem, 1)

            centre(0, 0, hnext, 4)
            one_over(0, 0).then_inc(norm_rc.sem, 1)
            scaled(0, 0, hc, hn)
            with dve.Fori(0, nseq) as i:
                dve.memset(z[:, :, 0:3], 0.0)
                link(i, dve.memset(vp[:, :, 0:PAD], 0.0))
                for n, m in enumerate(QKV):
                    dve.wait_ge(*z_done(i, n + 1))
                    if n >= 2:
                        dve.wait_ge(*silu_done(i, n - 1))
                    link(i, TS(cv[:, n % 2, :], z[:, m, 0:L], convw[:, m, 0:1], None, ALU.mult))
                    for j in range(1, CONV):
                        last = STT(cv[:, n % 2, :], z[:, m, j:j + L], convw[:, m, j:j + 1], cv[:, n % 2, :],
                                   ALU.mult, ALU.add)
                        if j < CONV - 1:
                            link(i, last)
                    last.then_inc(conv_done.sem, 1)
                dve.wait_ge(*conv_done(i, 6))

                at_tap = {}
                done = [0, 0, 0]

                def step(f, b, ins):
                    ins.then_inc(fir_step.sem, 1)
                    done[0] += 1
                    at_tap[f, b] = done[0]

                def filters(n):
                    for f, j, b in VTAPS[done[1]:done[1] + n]:
                        src = vp[:, b, PAD - j:PAD - j + L]
                        w = firw[:, b, sum(FIRS[:f]) + FIRS[f] - 1 - j:sum(FIRS[:f]) + FIRS[f] - j]
                        if (f, b) not in at_tap:
                            ins = TS(fir[:, f, b, :], src, w, None, ALU.mult)
                        else:
                            dve.wait_ge(*fir_step(i, at_tap[f, b]))
                            ins = STT(fir[:, f, b, :], src, w, fir[:, f, b, :], ALU.mult, ALU.add)
                        step(f, b, ins)
                        done[1] += 1

                def add_wide():
                    b = done[2]
                    dve.wait_ge(*wide_ps(i, WP * (b + 1)))
                    dve.wait_ge(*fir_step(i, at_tap[2, b]))
                    TT(halves(fir[:, 2, b, :]), halves(fir[:, 2, b, :]), pair(0), ALU.add).then_inc(wide_out.sem, 1)
                    dve.wait_ge(*wide_out(i, b + 1))
                    step(2, b, dve.nop())
                    done[2] += 1

                filters(24)
                dve.wait_ge(*rT_done(i, 0))
                CP(h, hnext)
                dve.wait_ge(*l2_sd(i, 1))
                dve.reciprocal(rl[:, 0:32], rl[:, 0:32])
                link(i, dve.reciprocal(rl[0:LT, 32:40], rl[0:LT, 32:40]))
                CP(rlx.rearrange("p t (h d) -> p (t h) d", d=GD),
                   rl[:, 0:32].rearrange("p (h a) -> p h a", a=1).to_broadcast([P, 32, GD]))
                CP(rly[0:LT, :].rearrange("p (h d) -> p h d", d=GD),
                   rl[0:LT, 32:40].rearrange("p (h a) -> p h a", a=1).to_broadcast([LT, 8, GD])).then_inc(l2_rc.sem, 1)
                filters(6)
                dve.wait_ge(*l2_bc(i, 1))
                TT(qk[:, :, 0:512], qk[:, :, 0:512], PS[:, 2:6, :], ALU.mult)
                TT(qk[:, :, 512:L], qk[:, :, 512:L], PS[:, 6, 0:4 * LT].rearrange("p (b l) -> p b l", b=4),
                   ALU.mult).then_inc(qk_done.sem, 1)
                dve.wait_ge(*beta_done(i, 1))
                filters(8)
                early = done[1]

                def statistics(t, k0, k1, squares, used):
                    n = NT[t]
                    s4 = st[0:n, 60 * t:60 * t + 60].rearrange("p (k s h) -> p k s h", s=3, h=4)[:, k0:k1]
                    f4 = F[0:n, t, k0:k1, :].rearrange("p k (h d) -> p k h d", h=GH)
                    RED(s4[:, :, 0, :], f4, AX.X, ALU.add)
                    RED(s4[:, :, 2, :], f4, AX.X, ALU.max, apply_absolute_value=True)
                    dve.wait_ge(*used[0](i, t + 1))
                    RED(ms[0:n, 20 * t + 4 * k0:20 * t + 4 * k1], squares[0:n, :].rearrange("p (g d) -> p g d", d=GD),
                        AX.X, ALU.add).then_inc(used[1].sem, 1)

                for part, (what, t, k) in enumerate(DELTA):
                    n = NT[t]
                    bt = beta[0:n, t, :]
                    if what == "inverse":
                        if k == 0:
                            dve.wait_ge(*G_ps(i, t + 1))
                            for hh in range(GH):
                                last = STT(X[0:n, hh, 0:n], PS[0:n, 2 + hh % 2, P * (hh // 2):P * (hh // 2) + n],
                                           bt[:, hh:hh + 1], K["strict"][0:n, 0:n], ALU.mult, ALU.mult)
                            last.then_inc(M_done.sem, 1)
                            dve.wait_ge(*at_ps(i, t + 1))
                            for q in range(2):
                                last = TT(atT[0:n, t % 2, q::2, 0:n],
                                          PS[0:n, 4 + 2 * q, 0:C].rearrange("p (h n) -> p h n", h=2)[:, :, 0:n],
                                          K["upper"][0:n, 0:n].rearrange("p (a n) -> p a n", a=1).to_broadcast([n, 2, n]),
                                          ALU.mult)
                            last.then_inc(at_done.sem, 1)
                        elif k == 1:
                            dve.wait_ge(*MT_done(i, t + 1))
                            TT(R[0:n, :, 0:n], XT[0:n, :, 0:n],
                               ident[0:n, 0:n].rearrange("p (a n) -> p a n", a=1).to_broadcast([n, GH, n]),
                               ALU.add).then_inc(R_done.sem, 1)
                            dve.wait_ge(*kv_tok(i, t + 1))
                            bb = bt.rearrange("p (h a) -> p h a", a=1).to_broadcast([n, GH, GD])
                            TT(kbt[0:n, :].rearrange("p (h d) -> p h d", h=GH),
                               ktok[0:n, t, :].rearrange("p (h d) -> p h d", h=GH), bb, ALU.mult)
                            TT(vbt[0:n, :].rearrange("p (h d) -> p h d", h=GH),
                               F[0:n, t, 4, :].rearrange("p (h d) -> p h d", h=GH), bb, ALU.mult
                               ).then_inc(kvb_done.sem, 1)
                        elif k < 7:
                            lv = k - 2
                            if lv:
                                dve.wait_ge(*R_ps(i, 4 * t + lv))
                                dve.wait_ge(*R_done(i, 5 * t + lv))
                                TT(R[0:n, :, 0:n], R[0:n, :, 0:n],
                                   PS[0:n, 6, :].rearrange("p (h n) -> p h n", h=GH)[:, :, 0:n],
                                   ALU.add).then_inc(R_done.sem, 1)
                            if lv < 4:
                                dve.wait_ge(*sq_ps(i, 4 * t + lv + 1))
                                CP(X[0:n, :, 0:n], PS[0:n, 4, :].rearrange("p (h n) -> p h n", h=GH)[:, :, 0:n]
                                   ).then_inc(X_done.sem, 1)
                    elif k % 2 == 0:
                        c = 4 * t + k // 2
                        rows = slice(CH * (k // 2), CH * (k // 2) + CH)
                        dve.wait_ge(*w_ps(i, c + 1))
                        TT(u[rows, t, :], u[rows, t, :], PS[rows, 5, 0:C], ALU.subtract).then_inc(ua_done.sem, 1)
                    if what == "chunk" and t and (k == 3 or (t == T - 1 and k == 1)):
                        dve.wait_ge(*o_done(i, t))
                        statistics(t - 1, 3, 5, dvsq, (dv_sq, dv_used))
                    if wide_after(part) >= WP > wide_after(part - 1):
                        add_wide()
                    filters(early + (part + 1) * (len(VTAPS) - early) // len(DELTA) - done[1])
                add_wide()
                assert done[0] == NFIR
                st4 = st.rearrange("p (g s h) -> p g s h", s=3, h=4)
                dve.wait_ge(*o_done(i, T))
                statistics(T - 1, 3, 5, dvsq, (dv_sq, dv_used))
                for t in range(T):
                    dve.wait_ge(*f_tok(i, t + 1))
                    statistics(t, 0, 3, fsq, (f_sq, f_used))
                dve.wait_ge(*f_used(i, T))
                dve.wait_ge(*dv_used(i, T))
                TS(st4[:, :, 0, :], st4[:, :, 0, :], 1.0 / GD, None, ALU.mult)
                TS(ms, ms, 1.0 / GD, 1e-8, ALU.mult, ALU.max).then_inc(rms_in.sem, 1)
                dve.wait_ge(*g2_ps(i, 1))
                for n, s in ((P, slice(0, 80)), (LT, slice(80, 100))):
                    g = (s.stop - s.start) // 20
                    last = TT(lg[0:n, s].rearrange("p (t k) -> p t k", t=g),
                              PS[0:n, 4, s].rearrange("p (t k) -> p t k", t=g),
                              gk[0:n, 0:20].rearrange("p (a k) -> p a k", a=1).to_broadcast([n, g, 20]), ALU.add)
                link(i, last)
                lg3 = lg.rearrange("p (t k) -> p t k", t=T)
                lg5 = lg.rearrange("p (g k) -> p g k", k=5)
                gw3 = gw.rearrange("p (t k) -> p t k", t=T)
                gw5 = gw.rearrange("p (g k) -> p g k", k=5)

                def over_tiles(v):
                    return v.rearrange("p (a k) -> p a k", a=1).to_broadcast([P, T, 20])

                def over_five(v):
                    return v.rearrange("p (g a) -> p g a", a=1).to_broadcast([P, 20, 5])

                link(i, TT(lg3, lg3, over_tiles(gk[:, 20:40]), ALU.mult))
                link(i, RED(m20, lg5, AX.X, ALU.max))
                TT(lg5, lg5, over_five(m20), ALU.subtract).then_inc(lg_in.sem, 1)
                dve.wait_ge(*lg_exp(i, 1))
                link(i, RED(s20, lg5, AX.X, ALU.add))
                link(i, dve.reciprocal(s20, s20))
                link(i, TT(gw5, lg5, over_five(s20), ALU.mult))
                link(i, TT(gw3, gw3, over_tiles(gk[:, 40:60]), ALU.mult))
                link(i, TT(gw3, gw3, over_tiles(gfloor[:, :]), ALU.add))
                gw4 = gw.rearrange("p (t h k) -> p t k h", t=T, h=GH)
                for ts, n in ((slice(0, 4), P), (slice(4, 5), LT)):
                    g = ts.stop - ts.start
                    for k in range(5):
                        f4 = F[0:n, ts, k, :].rearrange("p t (h d) -> p t h d", h=GH)
                        wb = gw4[0:n, ts, k, :].rearrange("p t (h a) -> p t h a", a=1)
                        last = TT(f4, f4, wb.to_broadcast([n, g, GH, GD]), ALU.mult)
                link(i, last)
                for ts, n in ((slice(0, 4), P), (slice(4, 5), LT)):
                    TT(F[0:n, ts, 0, :], F[0:n, ts, 0, :], F[0:n, ts, 1, :], ALU.add)
                    last = TT(F[0:n, ts, 2, :], F[0:n, ts, 2, :], F[0:n, ts, 3, :], ALU.add)
                link(i, last)
                for ts, n in ((slice(0, 4), P), (slice(4, 5), LT)):
                    last = TT(F[0:n, ts, 0, :], F[0:n, ts, 0, :], F[0:n, ts, 2, :], ALU.add)
                link(i, last)
                for ts, n in ((slice(0, 4), P), (slice(4, 5), LT)):
                    last = TT(o[0:n, ts, :], F[0:n, ts, 0, :], F[0:n, ts, 4, :], ALU.add)
                link(i, last)
                o3 = o.rearrange("p t (h d) -> p (t h) d", h=GH)
                osq = view(asq4, T * C, "p (g d) -> p g d", d=GD)
                link(i, TT(osq, o3, o3, ALU.mult))
                link(i, RED(m20, osq, AX.X, ALU.add))
                TS(m20, m20, 1.0 / GD, None, ALU.mult).then_inc(oss.sem, 1)
                dve.wait_ge(*oss_sd(i, 1))
                link(i, dve.reciprocal(s20, s20))
                TT(o3, o3, s20.rearrange("p (g a) -> p g a", a=1).to_broadcast([P, 20, GD]),
                   ALU.mult).then_inc(on_done.sem, 1)
                dve.wait_ge(*ow_ps(i, 1))
                for m in range(KB):
                    last = TT(halves(h[:, m, :]), halves(h[:, m, :]), pair(2 + 4 * m), ALU.add)
                last.then_inc(mean_src.sem, 1)
                centre(i, 1, h, 4)
                dve.wait_ge(*norm_src(i, 2))
                link(i, one_over(i, 1))
                TT(rr[:, 0:4], PS[:, 2, 0:4], rt[:, 0:4], ALU.mult)
                link(i, TT(rr[0:LT, 4:5], PS[0:LT, 2, 4:5], rt[0:LT, 4:5], ALU.mult))
                TT(rr, rr, rt, ALU.mult).then_inc(norm_ms.sem, 1)
                dve.nop().then_inc(norm_rc.sem, 1)
                dve.wait_ge(*norm_sd(i, 3))
                link(i, dve.reciprocal(rr, rr))
                TT(rr, rr, rt, ALU.mult).then_inc(norm_rc.sem, 1)
                scaled(i, 1, hc, hn)
                scaled(i, 2, hc, x1, Wt["ln1"])
                dve.wait_ge(*cks_ps(i, 1))
                TT(ckr, ck, K["cos"], ALU.mult)
                link(i, TT(halves(qrot), pair(4), halves(K["sin"]), ALU.mult))
                TT(kz[0:AD, 0, :], ckr[0:AD, :], qrot[0:AD, :], ALU.add)
                TT(kz[AD:P, 1, :], ckr[AD:P, :], qrot[AD:P, :], ALU.add).then_inc(ckr_done.sem, 1)
                for m in range(QB):
                    dve.wait_ge(*qs_ps(i, m + 1))
                    TT(qT[:, m, :], qraw[:, m % 2, :], K["cos"], ALU.mult)
                    if m:
                        dve.wait_ge(*qT_done(i, m))
                    link(i, TT(halves(qrot), pair(4 + 2 * (m % 2)), halves(K["sin"]), ALU.mult))
                    TT(qT[:, m, :], qT[:, m, :], qrot, ALU.add).then_inc(qT_done.sem, 1)
                dve.wait_ge(*qT_done(i, QB))
                CP(qlast.rearrange("p (m l) -> p m l", m=QB), qT[:, :, tok(T - 1)]).then_inc(qT_done.sem, 1)
                def top(n):
                    t, h0, g = STEPS[n]
                    dve.wait_ge(*s_ps(i, n + 1))
                    if n == FIRST[t] and t >= 2:
                        dve.wait_ge(*exp_done(i, FIRST[t - 1]))
                    if t < 4:
                        row = PS[:, n % 4, 0:P * (t + 1) * g].rearrange("p (g c) -> p g c", g=g)
                        link(i, TT(row[:, :, tok(t)], row[:, :, tok(t)],
                                   causal.rearrange("p (a c) -> p a c", a=1).to_broadcast([P, g, P]), ALU.min))
                    else:
                        row = PS[:, 2 * (n % 2):2 * (n % 2) + 2, :].rearrange("p a c -> p (a c)")[:, 0:L]
                        link(i, TT(row[:, tok(t)], row[:, tok(t)], K["causal4"], ALU.min))
                    RED(nmax[:, t % 2, h0:h0 + g], row, AX.X, ALU.max, negate=True).then_inc(max_done.sem, 1)

                def over_sums(t):
                    heads = AH if t < 4 else 4
                    dve.wait_ge(*y_ps(i, t + 1))
                    if t:
                        dve.wait_ge(*yT_ps(i, t))
                    link(i, dve.reciprocal(rinv[:, 0:heads], rsum[:, t % 2, 0:heads]))
                    TT(yn[:, 0:heads, :], PS[:, 6 + t % 2, 0:NOPE * heads].rearrange("p (h d) -> p h d", h=heads),
                       rinv[:, 0:heads].rearrange("p (h a) -> p h a", a=1).to_broadcast([P, heads, NOPE]),
                       ALU.mult).then_inc(yn_done.sem, 1)

                top(0)
                top(1)
                for n in range(NSTEP):
                    if n + 2 < NSTEP:
                        top(n + 2)
                    if n % 2:
                        t, h0, g = STEPS[n]
                        dve.wait_ge(*pT_ps(i, n + 1))
                        if t < 4:
                            CP(prT[:, 1, 0:P * (t + 1) * g], PS[:, 5, 0:P * (t + 1) * g]).then_inc(pT_v.sem, 1)
                        else:
                            CP(prT[:, 1, 0:512], PS[:, 4, :])
                            CP(prT[0:LT, 1, 512:640], PS[0:LT, 5, 0:P]).then_inc(pT_v.sem, 1)
                    if n - 1 in FIRST[1:]:
                        over_sums(FIRST.index(n - 1) - 1)
                over_sums(T - 1)
                dve.wait_ge(*wo_ps(i, 1))
                for m in range(KB):
                    last = TT(halves(x2[:, m, :]), halves(hn[:, m, :]), pair(2 * m), ALU.add)
                last.then_inc(norm_src.sem, 1)
                dve.wait_ge(*norm_src(i, 3))
                TT(h, h, x2, ALU.add)
                one_over(i, 3).then_inc(norm_rc.sem, 1)
                centre(i + 1, 0, hnext, 4)
                scaled(i, 3, x2, xn, Wt["ln2"])
                one_over(i + 1, 0).then_inc(norm_rc.sem, 1)
                dve.wait_ge(*gl_ps(i, 1))
                TT(gl[:, 0:4, :], PS[:, 6, 0:4 * E].rearrange("p (t e) -> p t e", t=4),
                   Wt["ebias"][:, :].rearrange("p (a e) -> p a e", a=1).to_broadcast([P, 4, E]), ALU.add)
                link(i, TT(gl[0:LT, 4, :], PS[0:LT, 6, 4 * E:5 * E], Wt["ebias"][0:LT, :], ALU.add))
                link(i, RED(m5, gl, AX.X, ALU.max))
                TT(gl, gl, m5.rearrange("p (t a) -> p t a", a=1).to_broadcast([P, T, E]),
                   ALU.subtract).then_inc(gl_in.sem, 1)
                dve.wait_ge(*gl_exp(i, 1))
                mine = gl.rearrange("p t (e a) -> p t e a", a=1).to_broadcast([P, T, E, E])
                other = gl.rearrange("p t (a e) -> p t a e", a=1).to_broadcast([P, T, E, E])
                cmpA3, cmpB3 = (v.rearrange("p t e j -> p t (e j)") for v in (cmpA, cmpB))
                TT(cmpA, other, mine, ALU.is_gt)
                link(i, TT(cmpB, other, mine, ALU.is_equal))
                link(i, TT(cmpB3, cmpB3, K["before"].rearrange("p (a k) -> p a k", a=1).to_broadcast([P, T, E * E]),
                           ALU.mult))
                link(i, TT(cmpA3, cmpA3, cmpB3, ALU.add))
                link(i, RED(rank, cmpA, AX.X, ALU.add))
                link(i, TS(rank, rank, 1.5, None, ALU.is_lt))
                link(i, TT(gl, gl, rank, ALU.mult))
                link(i, RED(s5, gl, AX.X, ALU.add))
                link(i, dve.reciprocal(s5, s5))
                TT(gl, gl, s5.rearrange("p (t a) -> p t a", a=1).to_broadcast([P, T, E]),
                   ALU.mult).then_inc(comb_done.sem, 1)
                scaled(i + 1, 0, hc, hn)
                def result_half(a):
                    dve.wait_ge(*dn_ps(i, NE * (a + 1)))
                    TT(h[:, :, cols(a)], h[:, :, cols(a)], PS[:, 6 - 2 * a:8 - 2 * a, 0:HALF],
                       ALU.add).then_inc(res_done.sem, 1)

                for n in range(2 * NE):
                    a, e = n // NE, n % NE
                    dve.wait_ge(*gs_done(i, n + 1))
                    if n >= 2:
                        dve.wait_ge(*dn_ps(i, n - 1))
                    if e < E:
                        dve.wait_ge(*cb_done(i, E))
                        link(i, TT(gu[:, n % 2, :], gs[:, n % 2, :], PS[:, 2 * (n % 2) + 1, 0:HALF], ALU.mult))
                        TT(gu[:, n % 2, :], gu[:, n % 2, :], cb[:, e, cols(a)], ALU.mult).then_inc(gu_done.sem, 1)
                    else:
                        TT(gu[:, n % 2, :], gs[:, n % 2, :], PS[:, 2 * (n % 2) + 1, 0:HALF],
                           ALU.mult).then_inc(gu_done.sem, 1)
                    if n == NE:
                        result_half(0)
                result_half(1)
                assert steps[0] == VSTEPS, ("VSTEPS", steps[0])


def kernel(**inputs):
    import numpy as _np
    import concourse.bacc as _bacc
    from concourse import mybir as _mybir
    from concourse.bass_utils import run_bass_kernel_spmd as _run

    a = {k: _np.asarray(v) for k, v in inputs.items()}

    def blocks(w, p=P):
        return _np.ascontiguousarray(w.reshape(-1, p, w.shape[1]).transpose(1, 0, 2).reshape(p, -1))

    def everywhere(v):
        return _np.ascontiguousarray(_np.broadcast_to(v.reshape(1, -1), (P, v.size)))

    w = {}
    w["wqkv"] = blocks(_np.concatenate([a[f"L0_attn_{n}_w"].T for n in "qkv"], axis=1))
    w["bw"] = blocks(a["L0_attn_b_w"].T)
    w["convw"] = blocks(_np.concatenate([a[f"L0_attn_conv{n}_w"] for n in "qkv"], axis=0))
    w["firw"] = blocks(_np.concatenate([a["L0_attn_" + n].reshape(C, -1) for n in ("fir_s", "fir_l", "fir_wd")], axis=1))
    g1 = _np.zeros((3 * P, 512), _np.float32)
    g1[:316] = a["L0_attn_g1_w"].T
    w["g1"] = blocks(g1)
    w["g1b"] = _np.ascontiguousarray(a["L0_attn_g1_b"].reshape(4, P).T)
    w["g2"] = blocks(a["L0_attn_g2_w"].T)
    w["g2b"] = everywhere(a["L0_attn_g2_b"])
    w["vbias"] = everywhere(a["L0_attn_value_bias"])
    w["ltemp"] = everywhere(a["L0_attn_log_temp"])
    w["floor"] = everywhere(a["L0_attn_floor_logit"])
    w["onorm"] = _np.ascontiguousarray(_np.tile(a["L0_attn_onorm_w"], P // GD).reshape(P, 1))
    w["ow"] = blocks(a["L0_attn_o_w"].T)
    w["ln1"] = _np.ascontiguousarray(a["L0_ffn_w_ln1"].reshape(KB, P).T)
    w["ln2"] = _np.ascontiguousarray(a["L0_ffn_w_ln2"].reshape(KB, P).T)
    w["wq"] = blocks(a["L0_ffn_Wq"])
    w["wkva"] = blocks(_np.concatenate([a["L0_ffn_Wkva"]] * 2, axis=1))
    order = [head_at(b, s) for b in range(4) for s in range(4)]
    w["wo"] = blocks(_np.ascontiguousarray(a["L0_ffn_Wo"].reshape(AH, AD, C)[order, :NOPE]).reshape(AH * NOPE, C))
    wqn = a["L0_ffn_Wq"].reshape(C, AH, AD)[:, order, :NOPE].reshape(C, AH * NOPE).T
    wlat = _np.zeros((4, P, P), _np.float32)
    for b in range(4):
        for s in range(4):
            n0, hh = NOPE * s, head_at(b, s)
            wlat[b, n0:n0 + NOPE, n0:n0 + NOPE] = a["L0_ffn_Wkvb"][:, NOPE * hh:NOPE * hh + NOPE].T
    w["wgate"] = blocks(a["L0_ffn_Wgate"])
    w["ebias"] = everywhere(a["L0_ffn_expert_bias"])
    for n, m in (("wg", "Wg"), ("wu", "Wu")):
        both = _np.concatenate([a["L0_ffn_" + m], a["L0_ffn_s" + m]], axis=0)
        w[n] = _np.ascontiguousarray(both.reshape(NE, KB, P, EI).transpose(2, 0, 1, 3).reshape(P, -1))
    both = _np.concatenate([a["L0_ffn_Wd"], a["L0_ffn_sWd"]], axis=0)
    w["wd"] = _np.ascontiguousarray(both.transpose(1, 0, 2).reshape(P, -1))

    nc = _bacc.Bacc("TRN2", target_bir_lowering=False, num_devices=1)
    arrays = {}

    def put(name, v):
        arrays[name] = v
        return nc.dram_tensor(name, v.shape, _mybir.dt.from_np(v.dtype), kind="ExternalInput").ap()

    x = put("x", _np.ascontiguousarray(a["x"]))
    txt = put("txt", _np.ascontiguousarray(a["txt"]))
    consts = put("consts", constants())
    tokw = put("tokw", everywhere(_np.ascontiguousarray(a["L0_tok_weight"].T)))
    tokws = put("tokws", _np.ascontiguousarray(a["L0_tok_weighted_sum"].T))
    wqn = put("wqn", blocks(wqn))
    wlat = put("wlat", blocks(wlat.reshape(4 * P, P)))
    weights = {n: put("w_" + n + "_dram", v) for n, v in w.items()}
    out = nc.dram_tensor("out", (B, L, C), F32, kind="ExternalOutput").ap()
    build(nc, x, txt, consts, tokw, tokws, wqn, wlat, weights, out)
    r = _run(nc, [arrays], core_ids=[0])
    return r.results[0]["out"]
```
